# Optimizing a Trainium2 kernel written in Bass

```python
import numpy as np
import jax
import jax.numpy as jnp

def _softmax(x, axis=-1):
    return jax.nn.softmax(x, axis=axis)

def _gelu(x):
    return jax.nn.gelu(x, approximate=True)

def _silu(x):
    return jax.nn.silu(x)

def _sigmoid(x):
    return jax.nn.sigmoid(x)

def _layernorm(x, axis=-1, eps=1e-05):
    m = jnp.mean(x, axis=axis, keepdims=True)
    v = jnp.var(x, axis=axis, keepdims=True)
    return (x - m) / jnp.sqrt(v + eps)

def _scatter_add(tgt, idx, src, axis=0):
    return tgt.at[idx].add(src)

def _segment_sum(src, seg, n):
    return jax.ops.segment_sum(src, seg, n)
kernel_name = 'mk_seq_postln_d2_jaxref_r8_aa3fa8'

def setup_inputs(seed: int=0):
    np.random.seed(seed)
    _w = jnp.asarray

    def _L0_attn_setup():
        import jax, jax.numpy as jnp
        import numpy as np
        B, L = (2, 128)
        D_MODEL, D_CKV, D_CQ = (128, 32, 64)
        N_HEAD, D_HEAD, D_ROPE = (8, 64, 32)
        N_IDX_HEAD = 4
        K_TS, LW = (96, 64)
        ROPE_BASE = 10000.0

        def _pope(x, angles):
            cos, sin = (jnp.cos(angles), jnp.sin(angles))
            mu1, mu2 = jnp.split(jax.nn.softplus(x), 2, axis=-1)
            return jnp.concatenate([mu1 * cos - mu2 * sin, mu1 * sin + mu2 * cos], axis=-1)

        def _forward(x, W_dkv, W_uk, W_uv, W_dq, W_uq, W_qr, W_kr, W_out, idx_wq, idx_wk, idx_w, raw_delta):
            B_, L_, _ = x.shape
            c_kv = x @ W_dkv
            q_i = (x @ idx_wq).reshape(B_, L_, N_IDX_HEAD, D_HEAD)
            k_i = x @ idx_wk
            s_i = jax.nn.relu(jnp.einsum('bthd,bsd->bths', q_i, k_i))
            I = jnp.einsum('bths,h->bts', s_i, idx_w)
            qpos = jnp.arange(L_)[:, None]
            kpos = jnp.arange(L_)[None, :]
            local = (kpos >= qpos - LW + 1) & (kpos <= qpos)
            causal = kpos > qpos
            I = jnp.where(local[None], jnp.inf, I)
            I = jnp.where(causal[None], -jnp.inf, I)
            kk = min(K_TS, L_)
            _, idx = jax.lax.top_k(I, kk)
            bi = jnp.arange(B_)[:, None, None]
            key_c = (c_kv @ W_uk)[bi, idx].reshape(B_, L_, kk, N_HEAD, D_HEAD)
            value = (c_kv @ W_uv)[bi, idx].reshape(B_, L_, kk, N_HEAD, D_HEAD)
            c_q = x @ W_dq
            query_c = (c_q @ W_uq).reshape(B_, L_, N_HEAD, D_HEAD)
            half = D_ROPE // 2
            theta = 1.0 / ROPE_BASE ** (2.0 * jnp.arange(half, dtype=jnp.float32) / D_ROPE)
            delta = -2.0 * jnp.pi * jax.nn.sigmoid(raw_delta)
            angles_q = jnp.arange(L_, dtype=jnp.float32)[:, None] * theta[None, :] + delta
            query_r = _pope((c_q @ W_qr).reshape(B_, L_, N_HEAD, D_ROPE), angles_q[None, :, None, :])
            kr_sel = (x @ W_kr)[bi, idx]
            angles_k = jnp.arange(kk, dtype=jnp.float32)[:, None] * theta[None, :] + delta
            key_r = _pope(kr_sel, angles_k[None, None, :, :])
            scale = (D_HEAD + D_ROPE) ** (-0.5)
            q_c = query_c.transpose(0, 2, 1, 3)
            q_r = query_r.transpose(0, 2, 1, 3)
            k_c = key_c.transpose(0, 3, 1, 2, 4)
            v = value.transpose(0, 3, 1, 2, 4)
            scores = (jnp.einsum('bhld,bhlkd->bhlk', q_c, k_c) + jnp.einsum('bhld,blkd->bhlk', q_r, key_r)) * scale
            attn = jax.nn.softmax(scores.astype(jnp.float32), axis=-1).astype(v.dtype)
            out = jnp.einsum('bhlk,bhlkd->bhld', attn, v)
            out = out.transpose(0, 2, 1, 3).reshape(B_, L_, N_HEAD * D_HEAD)
            return out @ W_out
        key = jax.random.key(seed)
        ks = jax.random.split(key, 14)

        def w(k, shape, fan_in):
            return jax.random.normal(k, shape, dtype=jnp.float32) * fan_in ** (-0.5)
        return {'x': jax.random.normal(ks[0], (B, L, D_MODEL), dtype=jnp.float32), 'W_dkv': w(ks[1], (D_MODEL, D_CKV), D_MODEL), 'W_uk': w(ks[2], (D_CKV, N_HEAD * D_HEAD), D_CKV), 'W_uv': w(ks[3], (D_CKV, N_HEAD * D_HEAD), D_CKV), 'W_dq': w(ks[4], (D_MODEL, D_CQ), D_MODEL), 'W_uq': w(ks[5], (D_CQ, N_HEAD * D_HEAD), D_CQ), 'W_qr': w(ks[6], (D_CQ, N_HEAD * D_ROPE), D_CQ), 'W_kr': w(ks[7], (D_MODEL, D_ROPE), D_MODEL), 'W_out': w(ks[8], (N_HEAD * D_HEAD, D_MODEL), N_HEAD * D_HEAD), 'idx_wq': w(ks[9], (D_MODEL, N_IDX_HEAD * D_HEAD), D_MODEL), 'idx_wk': w(ks[10], (D_MODEL, D_HEAD), D_MODEL), 'idx_w': jnp.ones((N_IDX_HEAD,), dtype=jnp.float32), 'raw_delta': jax.random.normal(ks[11], (D_ROPE // 2,), dtype=jnp.float32) * 0.1}
    _L0_attn_in = _L0_attn_setup()

    def _L0_ffn_setup():
        import jax, jax.numpy as jnp
        import numpy as np
        from jax import lax
        DIM = 128
        INTER = 64
        N_EXPERTS = 16
        TOPK = 4
        ROUTE_SCALE = 2.5
        VOCAB = 4000

        def _silu_and_mul(gu):
            gate, up = jnp.split(gu, 2, axis=-1)
            return jax.nn.silu(gate) * up
        key = jax.random.key(seed)
        ks = jax.random.split(key, 8)
        x = jax.random.normal(ks[0], (2, 64, DIM), dtype=jnp.float32)
        input_ids = jax.random.randint(ks[1], (2, 64), 0, VOCAB)
        s = 0.02
        gate_w = jax.random.normal(ks[2], (N_EXPERTS, DIM), dtype=jnp.float32) * s
        gate_b = jax.random.normal(ks[3], (N_EXPERTS,), dtype=jnp.float32) * s
        w13 = jax.random.normal(ks[4], (N_EXPERTS, 2 * INTER, DIM), dtype=jnp.float32) * s
        w2 = jax.random.normal(ks[5], (N_EXPERTS, DIM, INTER), dtype=jnp.float32) * s
        w13_s = jax.random.normal(ks[6], (2 * INTER, DIM), dtype=jnp.float32) * s
        w2_s = jax.random.normal(ks[7], (DIM, INTER), dtype=jnp.float32) * s
        return {'x': x, 'input_ids': input_ids, 'gate_w': gate_w, 'gate_b': gate_b, 'w13': w13, 'w2': w2, 'w13_s': w13_s, 'w2_s': w2_s}
    _L0_ffn_in = _L0_ffn_setup()

    def _L1_attn_setup():
        import jax, jax.numpy as jnp
        import numpy as np
        D_MODEL = 128
        D_STATE = 16
        D_CONV = 4
        D_INNER = 2 * D_MODEL
        DT_RANK = (D_MODEL + 15) // 16
        BATCH, SEQLEN = (2, 128)

        def _forward(hidden_states, in_proj_w, conv_w, conv_b, x_proj_w, dt_proj_w, dt_proj_b, A_log, D, out_proj_w):
            B, L, _ = hidden_states.shape
            xz = hidden_states @ in_proj_w.T
            x, z = jnp.split(xz, 2, axis=-1)
            xc = jnp.transpose(x, (0, 2, 1))
            xc = jax.lax.conv_general_dilated(xc, conv_w, window_strides=(1,), padding=[(D_CONV - 1, 0)], feature_group_count=D_INNER, dimension_numbers=('NCH', 'OIH', 'NCH')) + conv_b[None, :, None]
            xc = jax.nn.silu(xc)
            u = jnp.transpose(xc, (0, 2, 1)).astype(jnp.float32)
            x_dbl = u @ x_proj_w.T
            dt_low, Bp, Cp = jnp.split(x_dbl, [DT_RANK, DT_RANK + D_STATE], axis=-1)
            dt = dt_low @ dt_proj_w.T + dt_proj_b
            delta = jax.nn.softplus(dt + dt_proj_b)
            A = -jnp.exp(A_log.astype(jnp.float32))
            dA = jnp.exp(jnp.einsum('bld,dn->lbdn', delta, A))
            dBu = jnp.einsum('bld,bln,bld->lbdn', delta, Bp.astype(jnp.float32), u)
            C_t = jnp.transpose(Cp.astype(jnp.float32), (1, 0, 2))

            def step(state, inp):
                a, b, c = inp
                state = a * state + b
                y = jnp.einsum('bdn,bn->bd', state, c)
                return (state, y)
            x0 = jnp.zeros((B, D_INNER, D_STATE), jnp.float32)
            _, ys = jax.lax.scan(step, x0, (dA, dBu, C_t))
            y = jnp.transpose(ys, (1, 0, 2))
            y = y + u * D.astype(jnp.float32)
            y = y * jax.nn.silu(z.astype(jnp.float32))
            y = y.astype(hidden_states.dtype)
            return y @ out_proj_w.T
        key = jax.random.key(seed)
        ks = jax.random.split(key, 8)
        s = lambda k, shape, scale=0.02: jax.random.normal(k, shape, jnp.float32) * scale
        return {'hidden_states': jax.random.normal(ks[0], (BATCH, SEQLEN, D_MODEL), jnp.float32), 'in_proj_w': s(ks[1], (2 * D_INNER, D_MODEL)), 'conv_w': s(ks[2], (D_INNER, 1, D_CONV), 0.3), 'conv_b': jnp.zeros((D_INNER,), jnp.float32), 'x_proj_w': s(ks[3], (DT_RANK + 2 * D_STATE, D_INNER)), 'dt_proj_w': s(ks[4], (D_INNER, DT_RANK), 0.1), 'dt_proj_b': jax.random.uniform(ks[5], (D_INNER,), jnp.float32, minval=-5.0, maxval=-2.0), 'A_log': jnp.log(jnp.broadcast_to(jnp.arange(1, D_STATE + 1, dtype=jnp.float32), (D_INNER, D_STATE))), 'D': jnp.ones((D_INNER,), jnp.float32), 'out_proj_w': s(ks[6], (D_MODEL, D_INNER))}
    _L1_attn_in = _L1_attn_setup()

    def _L1_ffn_setup():
        import jax, jax.numpy as jnp
        import numpy as np
        H = 128
        E = 8
        B, S = (4, 256)
        key = jax.random.key(seed)
        k1, k2, k3, k4 = jax.random.split(key, 4)
        x = jax.random.normal(k1, (B, S, H), dtype=jnp.float32)
        wg = jax.random.normal(k2, (H, E), dtype=jnp.float32) * 0.02
        W = jax.random.normal(k3, (E, H, H), dtype=jnp.float32) * 0.02
        b = jax.random.normal(k4, (E, H), dtype=jnp.float32) * 0.02
        return {'x': x, 'wg': wg, 'W': W, 'b': b}
    _L1_ffn_in = _L1_ffn_setup()
    _d = {'L0_attn_x': _L0_attn_in['x'], 'L0_attn_W_dkv': _L0_attn_in['W_dkv'], 'L0_attn_W_uk': _L0_attn_in['W_uk'], 'L0_attn_W_uv': _L0_attn_in['W_uv'], 'L0_attn_W_dq': _L0_attn_in['W_dq'], 'L0_attn_W_uq': _L0_attn_in['W_uq'], 'L0_attn_W_qr': _L0_attn_in['W_qr'], 'L0_attn_W_kr': _L0_attn_in['W_kr'], 'L0_attn_W_out': _L0_attn_in['W_out'], 'L0_attn_idx_wq': _L0_attn_in['idx_wq'], 'L0_attn_idx_wk': _L0_attn_in['idx_wk'], 'L0_attn_idx_w': _L0_attn_in['idx_w'], 'L0_attn_raw_delta': _L0_attn_in['raw_delta'], 'L0_ffn_input_ids': _L0_ffn_in['input_ids'], 'L0_ffn_gate_w': _L0_ffn_in['gate_w'], 'L0_ffn_gate_b': _L0_ffn_in['gate_b'], 'L0_ffn_w13': _L0_ffn_in['w13'], 'L0_ffn_w2': _L0_ffn_in['w2'], 'L0_ffn_w13_s': _L0_ffn_in['w13_s'], 'L0_ffn_w2_s': _L0_ffn_in['w2_s'], 'L1_attn_in_proj_w': _L1_attn_in['in_proj_w'], 'L1_attn_conv_w': _L1_attn_in['conv_w'], 'L1_attn_conv_b': _L1_attn_in['conv_b'], 'L1_attn_x_proj_w': _L1_attn_in['x_proj_w'], 'L1_attn_dt_proj_w': _L1_attn_in['dt_proj_w'], 'L1_attn_dt_proj_b': _L1_attn_in['dt_proj_b'], 'L1_attn_A_log': _L1_attn_in['A_log'], 'L1_attn_D': _L1_attn_in['D'], 'L1_attn_out_proj_w': _L1_attn_in['out_proj_w'], 'L1_ffn_wg': _L1_ffn_in['wg'], 'L1_ffn_W': _L1_ffn_in['W'], 'L1_ffn_b': _L1_ffn_in['b']}
    _x0 = _d['L0_attn_x']
    _d['L0_attn_x'] = jax.random.normal(jax.random.fold_in(jax.random.key(seed), 1), (4, 512, 128), dtype=_x0.dtype)
    del _x0
    return _d

def reference(L0_attn_x, L0_attn_W_dkv, L0_attn_W_uk, L0_attn_W_uv, L0_attn_W_dq, L0_attn_W_uq, L0_attn_W_qr, L0_attn_W_kr, L0_attn_W_out, L0_attn_idx_wq, L0_attn_idx_wk, L0_attn_idx_w, L0_attn_raw_delta, L0_ffn_input_ids, L0_ffn_gate_w, L0_ffn_gate_b, L0_ffn_w13, L0_ffn_w2, L0_ffn_w13_s, L0_ffn_w2_s, L1_attn_in_proj_w, L1_attn_conv_w, L1_attn_conv_b, L1_attn_x_proj_w, L1_attn_dt_proj_w, L1_attn_dt_proj_b, L1_attn_A_log, L1_attn_D, L1_attn_out_proj_w, L1_ffn_wg, L1_ffn_W, L1_ffn_b):

    def _L0_attn_ref(x, W_dkv, W_uk, W_uv, W_dq, W_uq, W_qr, W_kr, W_out, idx_wq, idx_wk, idx_w, raw_delta):
        import jax, jax.numpy as jnp
        import numpy as np
        B, L = (2, 128)
        D_MODEL, D_CKV, D_CQ = (128, 32, 64)
        N_HEAD, D_HEAD, D_ROPE = (8, 64, 32)
        N_IDX_HEAD = 4
        K_TS, LW = (96, 64)
        ROPE_BASE = 10000.0

        def _pope(x, angles):
            cos, sin = (jnp.cos(angles), jnp.sin(angles))
            mu1, mu2 = jnp.split(jax.nn.softplus(x), 2, axis=-1)
            return jnp.concatenate([mu1 * cos - mu2 * sin, mu1 * sin + mu2 * cos], axis=-1)

        def _forward(x, W_dkv, W_uk, W_uv, W_dq, W_uq, W_qr, W_kr, W_out, idx_wq, idx_wk, idx_w, raw_delta):
            B_, L_, _ = x.shape
            c_kv = x @ W_dkv
            q_i = (x @ idx_wq).reshape(B_, L_, N_IDX_HEAD, D_HEAD)
            k_i = x @ idx_wk
            s_i = jax.nn.relu(jnp.einsum('bthd,bsd->bths', q_i, k_i))
            I = jnp.einsum('bths,h->bts', s_i, idx_w)
            qpos = jnp.arange(L_)[:, None]
            kpos = jnp.arange(L_)[None, :]
            local = (kpos >= qpos - LW + 1) & (kpos <= qpos)
            causal = kpos > qpos
            I = jnp.where(local[None], jnp.inf, I)
            I = jnp.where(causal[None], -jnp.inf, I)
            kk = min(K_TS, L_)
            _, idx = jax.lax.top_k(I, kk)
            bi = jnp.arange(B_)[:, None, None]
            key_c = (c_kv @ W_uk)[bi, idx].reshape(B_, L_, kk, N_HEAD, D_HEAD)
            value = (c_kv @ W_uv)[bi, idx].reshape(B_, L_, kk, N_HEAD, D_HEAD)
            c_q = x @ W_dq
            query_c = (c_q @ W_uq).reshape(B_, L_, N_HEAD, D_HEAD)
            half = D_ROPE // 2
            theta = 1.0 / ROPE_BASE ** (2.0 * jnp.arange(half, dtype=jnp.float32) / D_ROPE)
            delta = -2.0 * jnp.pi * jax.nn.sigmoid(raw_delta)
            angles_q = jnp.arange(L_, dtype=jnp.float32)[:, None] * theta[None, :] + delta
            query_r = _pope((c_q @ W_qr).reshape(B_, L_, N_HEAD, D_ROPE), angles_q[None, :, None, :])
            kr_sel = (x @ W_kr)[bi, idx]
            angles_k = jnp.arange(kk, dtype=jnp.float32)[:, None] * theta[None, :] + delta
            key_r = _pope(kr_sel, angles_k[None, None, :, :])
            scale = (D_HEAD + D_ROPE) ** (-0.5)
            q_c = query_c.transpose(0, 2, 1, 3)
            q_r = query_r.transpose(0, 2, 1, 3)
            k_c = key_c.transpose(0, 3, 1, 2, 4)
            v = value.transpose(0, 3, 1, 2, 4)
            scores = (jnp.einsum('bhld,bhlkd->bhlk', q_c, k_c) + jnp.einsum('bhld,blkd->bhlk', q_r, key_r)) * scale
            attn = jax.nn.softmax(scores.astype(jnp.float32), axis=-1).astype(v.dtype)
            out = jnp.einsum('bhlk,bhlkd->bhld', attn, v)
            out = out.transpose(0, 2, 1, 3).reshape(B_, L_, N_HEAD * D_HEAD)
            return out @ W_out
        return _forward(x, W_dkv, W_uk, W_uv, W_dq, W_uq, W_qr, W_kr, W_out, idx_wq, idx_wk, idx_w, raw_delta)

    def _L0_ffn_ref(x, input_ids, gate_w, gate_b, w13, w2, w13_s, w2_s):
        import jax, jax.numpy as jnp
        import numpy as np
        from jax import lax
        DIM = 128
        INTER = 64
        N_EXPERTS = 16
        TOPK = 4
        ROUTE_SCALE = 2.5
        VOCAB = 4000

        def _silu_and_mul(gu):
            gate, up = jnp.split(gu, 2, axis=-1)
            return jax.nn.silu(gate) * up
        B, S, D = x.shape
        xt = x.reshape(-1, D)
        T = xt.shape[0]
        scores = jax.nn.sigmoid(xt.astype(jnp.float32) @ gate_w.T)
        biased = scores + gate_b
        _, idx = lax.top_k(biased, TOPK)
        w = jnp.take_along_axis(scores, idx, axis=-1)
        w = w / jnp.sum(w, axis=-1, keepdims=True)
        w = w * ROUTE_SCALE
        comb = jnp.zeros((T, N_EXPERTS), jnp.float32)
        comb = comb.at[jnp.arange(T)[:, None], idx].add(w)
        comb = comb.astype(x.dtype)

        def expert_body(y, args):
            w13_e, w2_e, c_e = args
            h = _silu_and_mul(xt @ w13_e.T)
            return (y + c_e[:, None] * (h @ w2_e.T), None)
        y, _ = lax.scan(expert_body, jnp.zeros_like(xt), (w13, w2, comb.T))
        y = y + _silu_and_mul(xt @ w13_s.T) @ w2_s.T
        return y.astype(x.dtype).reshape(B, S, D)

    def _L1_attn_ref(hidden_states, in_proj_w, conv_w, conv_b, x_proj_w, dt_proj_w, dt_proj_b, A_log, D, out_proj_w):
        import jax, jax.numpy as jnp
        import numpy as np
        D_MODEL = 128
        D_STATE = 16
        D_CONV = 4
        D_INNER = 2 * D_MODEL
        DT_RANK = (D_MODEL + 15) // 16
        BATCH, SEQLEN = (2, 128)

        def _forward(hidden_states, in_proj_w, conv_w, conv_b, x_proj_w, dt_proj_w, dt_proj_b, A_log, D, out_proj_w):
            B, L, _ = hidden_states.shape
            xz = hidden_states @ in_proj_w.T
            x, z = jnp.split(xz, 2, axis=-1)
            xc = jnp.transpose(x, (0, 2, 1))
            xc = jax.lax.conv_general_dilated(xc, conv_w, window_strides=(1,), padding=[(D_CONV - 1, 0)], feature_group_count=D_INNER, dimension_numbers=('NCH', 'OIH', 'NCH')) + conv_b[None, :, None]
            xc = jax.nn.silu(xc)
            u = jnp.transpose(xc, (0, 2, 1)).astype(jnp.float32)
            x_dbl = u @ x_proj_w.T
            dt_low, Bp, Cp = jnp.split(x_dbl, [DT_RANK, DT_RANK + D_STATE], axis=-1)
            dt = dt_low @ dt_proj_w.T + dt_proj_b
            delta = jax.nn.softplus(dt + dt_proj_b)
            A = -jnp.exp(A_log.astype(jnp.float32))
            dA = jnp.exp(jnp.einsum('bld,dn->lbdn', delta, A))
            dBu = jnp.einsum('bld,bln,bld->lbdn', delta, Bp.astype(jnp.float32), u)
            C_t = jnp.transpose(Cp.astype(jnp.float32), (1, 0, 2))

            def step(state, inp):
                a, b, c = inp
                state = a * state + b
                y = jnp.einsum('bdn,bn->bd', state, c)
                return (state, y)
            x0 = jnp.zeros((B, D_INNER, D_STATE), jnp.float32)
            _, ys = jax.lax.scan(step, x0, (dA, dBu, C_t))
            y = jnp.transpose(ys, (1, 0, 2))
            y = y + u * D.astype(jnp.float32)
            y = y * jax.nn.silu(z.astype(jnp.float32))
            y = y.astype(hidden_states.dtype)
            return y @ out_proj_w.T
        return _forward(hidden_states, in_proj_w, conv_w, conv_b, x_proj_w, dt_proj_w, dt_proj_b, A_log, D, out_proj_w)

    def _L1_ffn_ref(x, wg, W, b):
        import jax, jax.numpy as jnp
        import numpy as np
        H = 128
        E = 8
        B, S = (4, 256)
        Bb, Ss, Hh = x.shape
        Ee = wg.shape[1]
        T = Bb * Ss
        C = T // Ee
        xt = x.reshape(T, Hh)
        logits = xt @ wg
        probs = jax.nn.softmax(logits, axis=-1)
        idx = jnp.argmax(probs, axis=-1)
        mask = jax.nn.one_hot(idx, Ee, dtype=xt.dtype)
        locations = jnp.cumsum(mask, axis=0) - mask
        mask = mask * (locations < C).astype(xt.dtype)
        gate = jnp.sum(probs * mask, axis=-1)
        loc_s = jnp.sum(locations * mask, axis=-1).astype(jnp.int32)
        loc_oh = jax.nn.one_hot(loc_s, C, dtype=xt.dtype)
        dispatch = mask[:, :, None] * loc_oh[:, None, :]
        combine = gate[:, None, None] * dispatch
        exp_in = jnp.einsum('tec,th->ech', dispatch, xt)
        exp_out = jnp.einsum('ech,efh->ecf', exp_in, W) + b[:, None, :]
        out = jnp.einsum('tec,ecf->tf', combine, exp_out)
        return out.reshape(Bb, Ss, Hh)
    x = L0_attn_x
    x = _layernorm(x + _L0_attn_ref(x, L0_attn_W_dkv, L0_attn_W_uk, L0_attn_W_uv, L0_attn_W_dq, L0_attn_W_uq, L0_attn_W_qr, L0_attn_W_kr, L0_attn_W_out, L0_attn_idx_wq, L0_attn_idx_wk, L0_attn_idx_w, L0_attn_raw_delta), axis=-1)
    x = _layernorm(x + _L0_ffn_ref(x, L0_ffn_input_ids, L0_ffn_gate_w, L0_ffn_gate_b, L0_ffn_w13, L0_ffn_w2, L0_ffn_w13_s, L0_ffn_w2_s), axis=-1)
    x = _layernorm(x + _L1_attn_ref(x, L1_attn_in_proj_w, L1_attn_conv_w, L1_attn_conv_b, L1_attn_x_proj_w, L1_attn_dt_proj_w, L1_attn_dt_proj_b, L1_attn_A_log, L1_attn_D, L1_attn_out_proj_w), axis=-1)
    x = _layernorm(x + _L1_ffn_ref(x, L1_ffn_wg, L1_ffn_W, L1_ffn_b), axis=-1)
    return x

_drawn_inputs = setup_inputs


def setup_inputs(seed=0):
    import zlib

    import numpy as np

    out = dict(_drawn_inputs(seed))
    spreads = {'L0_attn_idx_w': (1.0, 0.2), 'L1_attn_conv_b': (0.0, 0.8), 'L1_attn_D': (1.0, 0.6)}
    factors = {'L0_attn_raw_delta': 8.0,
     'L0_ffn_gate_w': 8.0,
     'L0_ffn_gate_b': 8.0,
     'L0_ffn_w13': 8.0,
     'L0_ffn_w2': 8.0,
     'L0_ffn_w13_s': 8.0,
     'L0_ffn_w2_s': 8.0,
     'L1_attn_in_proj_w': 8.0,
     'L1_attn_conv_w': 8.0,
     'L1_attn_x_proj_w': 8.0,
     'L1_attn_dt_proj_w': 8.0,
     'L1_attn_dt_proj_b': 8.0,
     'L1_attn_A_log': 8.0,
     'L1_attn_out_proj_w': 8.0,
     'L1_ffn_b': 8.0}
    for name, (base, spread) in spreads.items():
        noise = np.random.default_rng([zlib.crc32(name.encode()), seed]).standard_normal(out[name].shape)
        drawn = base * np.exp(spread * noise) if base else spread * noise
        out[name] = jnp.asarray(drawn.astype(out[name].dtype))
    for name, factor in factors.items():
        out[name] = (out[name] * factor).astype(out[name].dtype)
    return out
```

```python
from contextlib import ExitStack

import numpy as np

import concourse.bass as bass
from concourse import mybir

F32 = mybir.dt.float32
F16 = mybir.dt.float16
BF16 = mybir.dt.bfloat16
U32 = mybir.dt.uint32
ALU = mybir.AluOpType
ACT = mybir.ActivationFunctionType
AX = mybir.AxisListType

B, L, D = 4, 512, 128
P = 128
NT = L // P
NH, DH, DR, DC, DQ = 8, 64, 32, 32, 64
HALF = DR // 2
NIH = 4
TOPK, LW = 96, 64
NREM = TOPK - LW
NCOL = P // 4
SCALE = float(DH + DR) ** -0.5
NEG_TOP = -3.0e38
NEG = -1.0e30
NE, INTER, TOP_E = 16, 64, 4
ROUTE = 2.5
DI, DS, DCONV, DTR = 256, 16, 4, 8
NE2 = 8
CAP = B * L // NE2
EPS = 1e-5
LOG1P = (2.000000007877749, 0.6666631593507906, 0.4002485372356232, 0.2796141883332212, 0.28174657270344106)


class Signal:

    def __init__(self, sem, per, unit=1, first=0):
        self.sem, self.per, self.unit, self.first, self.k = sem, per, unit, first, 0

    def up(self):
        self.k += 1
        return self.unit

    def now(self, b):
        return self.at(b, self.k)

    def at(self, b, k):
        return b * (self.per * self.unit) + (self.first + k) * self.unit


def index_width(i):
    return P * i + P - LW


def first_width(i):
    return TOPK if i == 0 else LW


def build(nc, x, w128, w64, consts, out, at128, at64, atc):
    with ExitStack() as ctx:
        def sb(name, shape, dt=F32):
            return ctx.enter_context(nc.sbuf_tensor(name, shape, dt))

        def semaphore(name):
            return ctx.enter_context(nc.semaphore(name))

        def signal(name, per, unit=1, first=0):
            s = Signal(semaphore(name), per, unit, first)
            signals[name] = s
            return s

        signals = {}
        bank = [ctx.enter_context(nc.psum_tensor(f"bank{n}", [P, 512], F32)) for n in range(8)]

        W = sb("W", [P, w128.shape[1]])
        assert w64.shape[1] >= 4 * L
        WHP = sb("WHP", [P, w64.shape[1]])
        WH = WHP[0:64, :]
        CO = sb("CO", [P, consts.shape[1]])

        def piece(t, table, name):
            off, rows, shape = table[name]
            ap = t[0:rows, off:off + int(np.prod(shape))]
            if len(shape) == 2:
                ap = ap.rearrange("p (a c) -> p a c", a=shape[0])
            if len(shape) == 3:
                ap = ap.rearrange("p (a b c) -> p a b c", a=shape[0], b=shape[1])
            return ap

        def w(name):
            return piece(W, at128, name)

        def wh(name):
            return piece(WH, at64, name)

        def co(name):
            return piece(CO, atc, name)

        ident = co("ident")
        ident_bf = sb("ident_bf", [P, P], BF16)
        ident_h = sb("ident_h", [P, P], F16)
        tri_bf = sb("tri_bf", [P, P], BF16)
        ones_bf = sb("ones_bf", [P, P], BF16)
        lmask_bf = sb("lmask_bf", [P, 2, 224], BF16)
        WQ = sb("WQ", [64, 2, 256])
        WVO = sb("WVO", [P, 2, D])
        trig = sb("trig", [P, 2, 9, HALF])
        dl = sb("dl", [P, 8, HALF])
        Aneg = sb("Aneg", [P, 2, DS])
        dtb2 = sb("dtb2", [P, 2])
        one = sb("one", [P, 1])
        eps = sb("eps", [P, 1])
        cum = sb("cum", [P, NE2])
        cum_bf = sb("cum_bf", [P, NE2], BF16)
        trig_t = sb("trig_t", [P, 2, 9, HALF])
        X = sb("X", [P, NT, D])
        XT = sb("XT", [P, L])
        KIT = sb("KIT", [P, 2, L])
        KI, KT = KIT[:, 0, :], KIT[:, 1, :]
        QI = sb("QI", [P, 2, L])
        CQ = sb("CQ", [64, L])
        table = sb("table", [P, NT, 64])
        tparts = sb("tparts", [P, NT, 3, 64], BF16)
        tres = sb("tres", [P, 2, NT, 64])
        prev_c = sb("prev_c", [64, 3, DC])
        kr_e = sb("kr_e", [P, 3, NT, DR])
        krot = sb("krot", [P, 2, NT, DR])
        KD = sb("KD", [P, NT, 2, 64])
        relu_s = sb("relu_s", [P, NIH, L])
        score = sb("score", [P, 2, 448])
        top = sb("top", [P, NREM])
        idx = sb("idx", [P, NREM], U32)
        idxT = sb("idxT", [P, NCOL], U32)
        idxh = sb("idxh", [P, NCOL], F16)
        q_e = sb("q_e", [P, 3, 256])
        muq = sb("muq", [P, NH, DR])
        qr_c = sb("qr_c", [P, NH, DR])
        qr_s = sb("qr_s", [P, NH, DR])
        QA = sb("QA", [P, NH, 2, 32])
        QB = sb("QB", [P, NH, 2, 32])
        QABT = sb("QABT", [P, 2, 4, P])
        QAT, QBT = QABT[:, 0, :, :], QABT[:, 1, :, :]
        QT = sb("QT", [P, NH, 2, NCOL])
        QBD = sb("QBD", [P, NCOL, 2, 4, NH])
        ib = sb("ib", [P, NCOL, P], F16)
        onehot = sb("onehot", [P, 2, NT, 8 * P], BF16)
        G = sb("G", [P, NCOL, 64])
        g_cs = sb("g_cs", [P, 2, NCOL, DR])
        g_c, g_s = g_cs[:, 0, :, :], g_cs[:, 1, :, :]
        GR = sb("GR", [P, NCOL, DR])
        GT = sb("GT", [P, 2, NCOL, 32])
        SR = sb("SR", [P, 8, 32])
        SRd = sb("SRd", [P, 8, 32])
        PR = sb("PR", [P, 8, 32])
        PT = sb("PT", [P, 8, 32])
        PBD = sb("PBD", [P, 8, 4, 4, NH])
        RO = sb("RO", [P, 8, 34])
        RB = sb("RB", [P, NH, 34])
        PL = sb("PL", [P, 2, 4, 224])
        PLT1 = sb("PLT1", [TOPK, 4, P])
        PLT2 = sb("PLT2", [P, 4, P])
        ml = sb("ml", [P, NH])
        nml = sb("nml", [P, NH])
        ll = sb("ll", [P, NH])
        mj = sb("mj", [P, NH])
        dm = sb("dm", [P, 2, NH])
        em = sb("em", [P, 2, NH])
        den = sb("den", [P, 4, NH])
        fac = sb("fac", [P, 2, NH])
        On = sb("On", [P, 2, NH, DC])
        OT = sb("OT", [P, 2, P])
        Y = sb("Y", [P, NT, D])
        stats = sb("stats", [P, NT, 6])
        mv = sb("mv", [P, NT, 2])
        lnv = sb("lnv", [P, NT])
        rstd = sb("rstd", [P, NT])
        X1 = sb("X1", [P, NT, D])
        X1T = XT
        rt = sb("rt", [P, 6, NT, NE])
        r8 = sb("r8", [P, NT, 8])
        ri = sb("ri", [P, NT, 8], U32)
        rif = sb("rif", [P, NT, 8])
        req = sb("req", [P, NT, NE, TOP_E])
        rs = sb("rs", [P, 2, NT])
        CT = sb("CT", [NE, L])
        CB = onehot[:, :, :, :].rearrange("p a n c -> p (a n c)").bitcast(F32).rearrange("p (e t) -> p e t", e=NE // 2)
        SG = sb("SG", [P, 2, 256])
        HU = sb("HU", [P, 2, 256])
        HT = sb("HT", [P, 2, 256])
        XP = sb("XP", [P, 2, L + DCONV - 1])
        SZ = GR[:, :, :].rearrange("p (j n) c -> p j (n c)", j=2)
        CV = relu_s[:, :, :].rearrange("p (j k) t -> p j k t", j=2)
        U = KIT
        XD = sb("XD", [DTR + 2 * DS, L])
        DEL = QI
        DU = QABT[:, :, :, :].rearrange("p j k t -> p j (k t)")
        dA = ib[:, :, :].rearrange("p t c -> p (t c)").bitcast(F32).rearrange("p (k j t) -> p k j t", k=2, j=2)
        Bn = WHP[:, 0:2 * L].rearrange("p (k t) -> p k t", k=2)
        Cn = WHP[:, 2 * L:4 * L].rearrange("p (k t) -> p k t", k=2)
        dBu = G[:, :, :].rearrange("p (k j n) c -> p k j (n c)", k=2, j=2)
        hs = GT[:, :, :, :].rearrange("p k (j n) c -> p k j (n c)", j=2)
        hC = g_cs[:, :, :, :].rearrange("p k (j n) c -> p k j (n c)", j=2)
        YG = CV[:, :, 1, :]
        dt_x, dt_a, dt_b, dt_c = hs[:, 0, :, :], hs[:, 1, :, :], hC[:, 0, :, :], hC[:, 1, :, :]
        pr = sb("pr", [P, 4, NT, NE2])
        ps1 = sb("ps1", [P, 3, NT])
        mk = sb("mk", [P, NT, NE2])
        mk_bf = sb("mk_bf", [P, NT, NE2], BF16)
        keep = sb("keep", [P, NT, NE2])
        gate = sb("gate", [P, NT, NE2])
        csum = sb("csum", [P, NE2])
        GTs = CT[0:NE2, :]
        OUT = sb("OUT", [P, NT, D])
        scr = nc.dram_tensor("rows_bounce", [2, P, NH * 34], F32, kind="Internal").ap()

        s_load = semaphore("weights_loaded")
        set_v = Signal(semaphore("setup_vector"), SET_VEC)
        s_seta = semaphore("setup_scalar")
        s_setp = semaphore("setup_tensor")
        hold_dve, hold_pe = semaphore("hold_vector"), semaphore("hold_tensor")
        x_in = signal("x_in", 1, 16)
        batch_done = signal("batch_done", 1, first=1)
        out_stored = signal("out_stored", 1, 16, first=1)
        vec = signal("vector_step", PER["vec"])
        act_s = signal("scalar_step", PER["act"])
        xt_ps = signal("xt_in_psum", 4)
        xt_sb = signal("xt_in_sbuf", 4)
        proj_ps = signal("proj_in_psum", 4)
        proj_sb = signal("proj_in_sbuf", 4)
        kv_ps = signal("kv_in_psum", 1)
        kr_sp = signal("kr_logs_ready", 1)
        kv_in = signal("kv_dup_ready", 1)
        kt_ps = signal("kt_in_psum", 1)
        kt_sb = signal("kt_in_sbuf", 1)
        parts_ok = signal("table_parts_ready", 1)
        ix_ps = signal("index_scores_in_psum", 4 * NT)
        ix_relu = signal("index_relu_ready", 4 * NT)
        ix_used = signal("index_relu_used", NT)
        q_ps = signal("q_in_psum", NT)
        q_sp = signal("q_logs_ready", NT)
        q_rows = signal("q_rows_ready", NT)
        qT_ps = signal("qt_in_psum", NT + 1)
        qT_sb = signal("qt_in_sbuf", NT + 1)
        idx_ok = signal("idx_columns_ready", NT)
        ib_ps = signal("idx_spread_in_psum", 8 * NT)
        ib_sb = signal("idx_spread_in_sbuf", 8 * NT)
        oh_ok = signal("onehot_chunk_ready", 4 * NT)
        g_ps = signal("rows_in_psum", 4 * NT)
        g_sb = signal("rows_in_sbuf", 4 * NT)
        g_sin = signal("rows_sin_ready", NT)
        gt_ok = signal("picked_keys_ready", NT)
        sr_ps = signal("picked_scores_in_psum", NT)
        sr_d = signal("picked_scores_shifted", NT)
        pr_ok = signal("picked_probs_ready", NT)
        pbd_ok = signal("picked_probs_spread", NT)
        ro_ps = signal("picked_out_in_psum", NT)
        ro_sb = signal("picked_out_in_sbuf", NT)
        ro_st = signal("picked_out_stored", 16 * NT, 16)
        rb_in = signal("picked_out_back", NT, 16)
        sl_ps = signal("local_scores_in_psum", 2 * NT)
        ml_ok = signal("local_max_ready", 2 * NT)
        pl_ok = signal("local_probs_ready", 2 * NT)
        pt_ps = signal("local_probs_t_in_psum", 2 * NT)
        pt_sb = signal("local_probs_t_in_sbuf", 2 * NT)
        ol_ps = signal("local_out_in_psum", 2 * NT)
        dm_ok = signal("max_gaps_ready", NT)
        em_ok = signal("merge_weights_ready", NT)
        on_ok = signal("attn_rows_ready", NT)
        oT_ps = signal("attn_t_in_psum", NT)
        oT_sb = signal("attn_t_in_sbuf", NT)
        at_ps = signal("attn_out_in_psum", NT)
        at_used = signal("attn_out_added", NT)
        var_ok = signal("variances_ready", 4)
        rstd_ok = signal("rstd_ready", 4)
        ln_ok = signal("normed_rows_ready", 3)
        rl_ps = signal("router_logits_in_psum", 2)
        rl_e = signal("router_exp_ready", 1)
        comb_ok = signal("comb_ready", 1)
        ct_ps = signal("comb_t_in_psum", 1)
        ct_sb = signal("comb_t_in_sbuf", 1)
        cb_ps = signal("comb_spread_in_psum", 8)
        cb_sb = signal("comb_spread_in_sbuf", 8)
        gu_ps = signal("gate_up_in_psum", 18)
        sg_ok = signal("silu_ready", 18)
        hu_ok = signal("hidden_ready", 18)
        ht_ok = signal("hidden_scaled", 16)
        y_part = signal("expert_out_part", 18)
        xz_ps = signal("xz_in_psum", 4)
        xz_sb = signal("xz_in_sbuf", 4)
        cv_ok = signal("conv_ready", 2)
        u_ok = signal("u_ready", 2)
        xd_ps = signal("xdbl_in_psum", 1)
        xd_sb = signal("xdbl_in_sbuf", 1)
        dt_ps = signal("dt_in_psum", 2)
        dtx_ok = signal("dt_biased", 1)
        dt_sp = signal("dt_logs_ready", 1)
        del_ok = signal("delta_ready", 1)
        bc_ps = signal("bc_in_psum", 2 * DS)
        bc_sb = signal("bc_in_sbuf", 2 * DS)
        dA_ok = signal("decay_ready", 2 * DS)
        dBu_ok = signal("drive_ready", 2 * DS)
        scan_ok = signal("states_ready", 2 * DS)
        hC_ok = signal("readout_ready", 2 * DS)
        ysum = signal("readout_summed", 2 * DS)
        yg_ok = signal("gated_ready", 1)
        op_ps = signal("scan_out_in_psum", 1)
        pm_ok = signal("gate_shifted", 1)
        pe_ok = signal("gate_exp_ready", 1)
        mk_ok = signal("choice_ready", 1)
        loc_ps = signal("slots_in_psum", 1)
        gate_ok = signal("gates_ready", 1)
        gT_ps = signal("gates_t_in_psum", 1)
        gT_sb = signal("gates_t_in_sbuf", 1)
        bias_ps = signal("bias_in_psum", 1)
        e_ps = signal("top1_out_in_psum", NT)
        e_used = signal("top1_out_used", NT)

        NSETP = 3
        block = ctx.enter_context(nc.Block())

        @block.sync
        def _(sp):
            sp.dma_start(CO[:, :], consts).then_inc(s_load, 16)
            sp.dma_start(W[:, :], w128).then_inc(s_load, 16)
            sp.dma_start(WH, w64).then_inc(s_load, 16)
            sp.sem_inc(out_stored.sem, 16)
            with sp.Fori(0, B) as b:
                sp.wait_ge(batch_done.sem, batch_done.at(b, 0))
                sp.dma_start(X[:, :, :], x[b].rearrange("(n p) d -> p n d", p=P)).then_inc(x_in.sem, x_in.up())
                for i in range(NT):
                    sp.wait_ge(ro_sb.sem, ro_sb.at(b, i + 1))
                    rows = scr[i % 2].rearrange("(b x a) (h e) -> a b h x e", b=4, a=4, h=NH)
                    for a in range(4):
                        for bb in range(4):
                            p0 = 32 * a + 8 * bb
                            sp.dma_start(rows[a, bb], RO[p0:p0 + 8, :, :]).then_inc(ro_st.sem, ro_st.up())
                    sp.wait_ge(ro_st.sem, ro_st.at(b, 16 * (i + 1)))
                    if i >= 1:
                        sp.wait_ge(on_ok.sem, on_ok.at(b, i))
                    sp.dma_start(RB[:, :, :].rearrange("p h e -> p (h e)"), scr[i % 2]).then_inc(rb_in.sem, rb_in.up())
                sp.wait_ge(batch_done.sem, batch_done.at(b, 1))
                sp.dma_start(out[b].rearrange("(n p) d -> p n d", p=P), OUT[:, :, :]).then_inc(out_stored.sem, out_stored.up())
            sp.wait_ge(out_stored.sem, 16 * (B + 1))

        @block.tensor
        def _(pe):
            mm = pe.matmul

            def turn(o, i_, k=P):
                return pe.transpose(o, i_, ident[0:k, 0:k])

            def t2(src):
                for i in range(NT):
                    m = turn(bank[6][:, i * P:(i + 1) * P], src[:, i, :])
                m.then_inc(xt_ps.sem, xt_ps.up())

            pe.wait_ge(s_load, 48)
            for h in range(NH):
                m = mm(bank[0][0:64, h * DC:(h + 1) * DC], wh("uqT")[:, h, :], wh("ukT")[:, h, :],
                       start=True, stop=True)
            m.then_inc(s_setp, 1)
            for h in range(NH):
                m = mm(bank[1][32 * (h % 4):32 * (h % 4) + 32, (h // 4) * D:(h // 4 + 1) * D],
                       wh("uvT")[:, h, :], wh("out")[:, h, :], start=True, stop=True)
            m.then_inc(s_setp, 1)
            pe.wait_ge(set_v.sem, SET_VEC)
            pe.wait_ge(s_seta, 3)

            with pe.Fori(0, B) as b:

                pe.wait_ge(batch_done.sem, batch_done.at(b, 0))
                pe.wait_ge(x_in.sem, x_in.at(b, 1))
                pe.sem_inc(hold_pe, 1)
                for i in range(NT):
                    m = turn(bank[0][:, i * P:(i + 1) * P], X[:, i, :])
                m.then_inc(xt_ps.sem, xt_ps.up())
                pe.wait_ge(xt_sb.sem, xt_sb.at(b, 1))
                mm(bank[1][:, :], w("wk2"), XT[:, :], start=True, stop=True).then_inc(proj_ps.sem, proj_ps.up())
                mm(bank[2][:, :], w("wq")[:, 0:P], XT[:, :], start=True, stop=True).then_inc(proj_ps.sem, proj_ps.up())
                mm(bank[3][:, :], w("wq")[:, P:2 * P], XT[:, :], start=True, stop=True).then_inc(proj_ps.sem, proj_ps.up())
                mm(bank[4][0:64, :], w("dq"), XT[:, :], start=True, stop=True).then_inc(proj_ps.sem, proj_ps.up())
                for i in range(NT):
                    mm(bank[0][:, i * 64:(i + 1) * 64], XT[:, i * P:(i + 1) * P], w("kv"), start=True, stop=True)
                for i in range(1, NT):
                    m = mm(bank[0][0:64, 256 + 32 * i:288 + 32 * i], XT[:, i * P - 64:i * P], w("kv")[:, 0:DC],
                           start=True, stop=True)
                m.then_inc(kv_ps.sem, kv_ps.up())
                pe.wait_ge(kv_in.sem, kv_in.at(b, 1))
                pe.sem_inc(hold_pe, 1)
                for i in range(NT):
                    m = turn(bank[1][:, i * P:(i + 1) * P], KD[:, i, :, :].rearrange("p a c -> p (a c)"))
                m.then_inc(kt_ps.sem, kt_ps.up())

                for i in range(NT):
                    Wi, W0 = index_width(i), first_width(i)
                    c0 = 96 - W0
                    if i == 0:
                        pe.wait_ge(proj_sb.sem, proj_sb.at(b, 4))
                        pe.wait_ge(kt_sb.sem, kt_sb.at(b, 1))
                    else:
                        pe.wait_ge(pt_sb.sem, pt_sb.at(b, 2 * i))
                        pe.wait_ge(g_sb.sem, g_sb.at(b, 4 * i))
                    for h in range(NIH):
                        o = 64 * (h % 2)
                        mm(bank[h][:, 0:Wi], QI[o:o + 64, h // 2, i * P:(i + 1) * P], KI[o:o + 64, 0:Wi],
                                      start=True, stop=True).then_inc(ix_ps.sem, ix_ps.up())
                    if i >= 1:
                        pe.wait_ge(at_used.sem, at_used.at(b, i))
                    mm(bank[4][:, :], CQ[:, i * P:(i + 1) * P], WQ[:, :, :].rearrange("p a c -> p (a c)"),
                                 start=True, stop=True).then_inc(q_ps.sem, q_ps.up())
                    pe.wait_ge(q_rows.sem, q_rows.at(b, i + 1))
                    pe.wait_ge(ix_relu.sem, ix_relu.at(b, 4 * i + 4))
                    pe.sem_inc(hold_pe, 1)
                    for p in range(4):
                        m = turn(bank[2][:, p * P:(p + 1) * P],
                                 QB[:, 2 * p:2 * p + 2, :, :].rearrange("p h k c -> p (h k c)"))
                    m.then_inc(qT_ps.sem, qT_ps.up())
                    if i == 0:
                        for p in range(4):
                            m = turn(bank[3][:, p * P:(p + 1) * P],
                                     QA[:, 2 * p:2 * p + 2, :, :].rearrange("p h k c -> p (h k c)"))
                        m.then_inc(qT_ps.sem, qT_ps.up())
                    pe.wait_ge(idx_ok.sem, idx_ok.at(b, i + 1))
                    for r in range(8):
                        if r >= 2:
                            pe.wait_ge(ib_sb.sem, ib_sb.at(b, 8 * i + r - 1))
                        for q in range(4):
                            t = 4 * r + q
                            m = mm(bank[r % 2][:, q * P:(q + 1) * P], idxh[:, t:t + 1].to_broadcast([P, P]), ident_h[:, :],
                                   start=True, stop=True)
                        m.then_inc(ib_ps.sem, ib_ps.up())
                    pe.wait_ge(qT_sb.sem, qT_sb.at(b, i + 2))
                    pe.wait_ge(ib_sb.sem, ib_sb.at(b, 8 * i + 8))
                    for g in range(2):
                        if g == 1:
                            pe.wait_ge(pl_ok.sem, pl_ok.at(b, 2 * i + 1))
                        for hh in range(4):
                            h = 4 * g + hh
                            o = 64 * (h % 2)
                            sc = bank[2 + hh % 2][:, 256 * (hh // 2):256 * (hh // 2) + 224]
                            mm(sc[:, c0:224], ident_bf[:, :], lmask_bf[:, min(i, 1), c0:224], start=True, stop=False)
                            if i == 0:
                                mm(sc[:, 0:96], QAT[o:o + 64, h // 2, :], KT[o:o + 64, 0:96], start=False, stop=True)
                                m = mm(sc[:, 96:224], QBT[o:o + 64, h // 2, :], KT[o:o + 64, 0:P],
                                       start=False, stop=True, skip_group_check=True)
                            else:
                                m = mm(sc[:, c0:224], QBT[o:o + 64, h // 2, :], KT[o:o + 64, i * P - 64:(i + 1) * P],
                                       start=False, stop=True)
                        m.then_inc(sl_ps.sem, sl_ps.up())
                        pe.wait_ge(pl_ok.sem, pl_ok.at(b, 2 * i + g + 1))
                        if g == 1:
                            pe.wait_ge(pt_sb.sem, pt_sb.at(b, 2 * i + 1))
                        pe.sem_inc(hold_pe, 1)
                        for hh in range(4):
                            turn(bank[0][0:W0, hh * P:(hh + 1) * P], PL[:, g, hh, c0:96])
                        for hh in range(4):
                            m = turn(bank[1][:, hh * P:(hh + 1) * P], PL[:, g, hh, 96:224])
                        m.then_inc(pt_ps.sem, pt_ps.up())
                        pe.wait_ge(pt_sb.sem, pt_sb.at(b, 2 * i + g + 1))
                        if g == 0 and i >= 1:
                            pe.wait_ge(oT_sb.sem, oT_sb.at(b, i))
                        pe.sem_inc(hold_pe, 1)
                        for hh in range(4):
                            h = 4 * g + hh
                            first = table[0:W0, 0, 0:DC] if i == 0 else prev_c[:, i - 1, :]
                            mm(bank[5][:, h * DC:(h + 1) * DC], PLT1[0:W0, hh, :], first, start=True, stop=False)
                            m = mm(bank[5][:, h * DC:(h + 1) * DC], PLT2[:, hh, :], table[:, i, 0:DC],
                                   start=False, stop=True)
                        m.then_inc(ol_ps.sem, ol_ps.up())
                    if i == 0:
                        pe.wait_ge(parts_ok.sem, parts_ok.at(b, 1))
                    for c in range(4):
                        pe.wait_ge(oh_ok.sem, oh_ok.at(b, 4 * i + c + 1))
                        if c >= 2:
                            pe.wait_ge(g_sb.sem, g_sb.at(b, 4 * i + c - 1))
                        for q in range(8):
                            t = 8 * c + q
                            for kt in range(i + 1):
                                kk = 64 if kt == i else P
                                for part in range(3):
                                    m = mm(bank[2 + c % 2][:, q * 64:(q + 1) * 64], onehot[0:kk, c % 2, kt, q * P:(q + 1) * P],
                                           tparts[0:kk, kt, part, :], start=(kt == 0 and part == 0),
                                           stop=(kt == i and part == 2))
                        m.then_inc(g_ps.sem, g_ps.up())
                    pe.wait_ge(gt_ok.sem, gt_ok.at(b, i + 1))
                    pe.sem_inc(hold_pe, 1)
                    for t in range(NCOL):
                        xx, a = t // 4, t % 4
                        for kind in range(2):
                            m = mm(bank[4][32 * a:32 * a + 32, 32 * xx:32 * xx + 32],
                                   QBD[:, t, kind, :, :].rearrange("p b h -> p (b h)"), GT[:, kind, t, :],
                                   start=(kind == 0), stop=(kind == 1))
                    m.then_inc(sr_ps.sem, sr_ps.up())
                    pe.wait_ge(pbd_ok.sem, pbd_ok.at(b, i + 1))
                    pe.sem_inc(hold_pe, 1)
                    for t in range(NCOL):
                        xx, a = t // 4, t % 4
                        m = mm(bank[4][32 * a:32 * a + 32, 256 + 32 * xx:288 + 32 * xx],
                               PBD[:, xx, a, :, :].rearrange("p b h -> p (b h)"), G[:, t, 0:DC], start=True, stop=True)
                    m.then_inc(ro_ps.sem, ro_ps.up())
                    pe.wait_ge(on_ok.sem, on_ok.at(b, i + 1))
                    pe.sem_inc(hold_pe, 1)
                    for k in range(2):
                        m = turn(bank[5][:, 256 + k * P:256 + (k + 1) * P],
                                 On[:, 0, 4 * k:4 * k + 4, :].rearrange("p h c -> p (h c)"))
                    m.then_inc(oT_ps.sem, oT_ps.up())
                    pe.wait_ge(oT_sb.sem, oT_sb.at(b, i + 1))
                    for k in range(2):
                        m = mm(bank[4][:, 0:P], OT[:, k, :], WVO[:, k, :], start=(k == 0), stop=(k == 1))
                    m.then_inc(at_ps.sem, at_ps.up())

                pe.wait_ge(ln_ok.sem, ln_ok.at(b, 1))
                pe.sem_inc(hold_pe, 1)
                t2(X1)
                pe.wait_ge(xt_sb.sem, xt_sb.at(b, 2))
                for i in range(NT):
                    m = mm(bank[7][:, i * NE:(i + 1) * NE], X1T[:, i * P:(i + 1) * P], w("gate"), start=True, stop=True)
                m.then_inc(rl_ps.sem, rl_ps.up())
                pe.wait_ge(comb_ok.sem, comb_ok.at(b, 1))
                pe.sem_inc(hold_pe, 1)
                for i in range(NT):
                    m = turn(bank[7][0:NE, i * P:(i + 1) * P], rt[:, 5, i, :])
                m.then_inc(ct_ps.sem, ct_ps.up())
                pe.wait_ge(ct_sb.sem, ct_sb.at(b, 1))
                for p in range(NE // 2):
                    if p >= 2:
                        pe.wait_ge(cb_sb.sem, cb_sb.at(b, p - 1))
                    pe.sem_inc(hold_pe, 1)
                    for e in range(2):
                        m = mm(bank[5 + p % 2][64 * e:64 * e + 64, :], ident[0:NE, 2 * p + e:2 * p + e + 1].to_broadcast([NE, 64]),
                               CT[:, :], start=True, stop=True)
                    m.then_inc(cb_ps.sem, cb_ps.up())
                pe.wait_ge(cb_sb.sem, cb_sb.at(b, 8))

                def second(u):
                    p, half = u // 2, u % 2
                    if p < 8:
                        pe.wait_ge(ht_ok.sem, ht_ok.at(b, u + 1))
                    else:
                        pe.wait_ge(hu_ok.sem, hu_ok.at(b, u + 1))
                    kk = P if p < 8 else 64
                    wt = w("w2")[:, p, :] if p < 8 else w("w2s")[0:64, :]
                    pe.sem_inc(hold_pe, 1)
                    for q in range(2):
                        i = 2 * half + q
                        m = mm(bank[7][:, i * P:(i + 1) * P], HT[0:kk, u % 2, q * P:(q + 1) * P], wt,
                               start=(u == 0 and q == 0), stop=(p == 8), skip_group_check=True)
                    m.then_inc(y_part.sem, y_part.up())

                for u in range(18):
                    p, half = u // 2, u % 2
                    if u >= 2:
                        pe.wait_ge(hu_ok.sem, hu_ok.at(b, u - 1))
                    rows = P if p < 8 else 64
                    wg = w("w1g")[:, p, :] if p < 8 else w("w1sg")
                    wu = w("w1u")[:, p, :] if p < 8 else w("w1su")
                    mm(bank[5 + u % 2][0:rows, 0:256], wg, X1T[:, half * 256:(half + 1) * 256], start=True, stop=True)
                    mm(bank[5 + u % 2][0:rows, 256:512], wu, X1T[:, half * 256:(half + 1) * 256],
                                  start=True, stop=True).then_inc(gu_ps.sem, gu_ps.up())
                    if u >= 1:
                        second(u - 1)
                second(17)

                pe.wait_ge(ln_ok.sem, ln_ok.at(b, 2))
                pe.sem_inc(hold_pe, 1)
                t2(X1)
                pe.wait_ge(xt_sb.sem, xt_sb.at(b, 3))
                for k in range(4):
                    if k >= 2:
                        pe.wait_ge(xz_sb.sem, xz_sb.at(b, k - 1))
                    mm(bank[4 + k % 2][:, :], w("inp")[:, k * P:(k + 1) * P], X1T[:, :], start=True, stop=True).then_inc(xz_ps.sem, xz_ps.up())
                pe.wait_ge(u_ok.sem, u_ok.at(b, 2))
                pe.sem_inc(hold_pe, 1)
                for j in range(2):
                    m = mm(bank[7][0:40, :], w("xp")[:, j, :], U[:, j, :], start=(j == 0), stop=(j == 1))
                m.then_inc(xd_ps.sem, xd_ps.up())
                pe.wait_ge(xd_sb.sem, xd_sb.at(b, 1))
                pe.sem_inc(hold_pe, 1)
                for j in range(2):
                    mm(bank[5 + j][:, :], w("dtw")[0:DTR, j * P:(j + 1) * P], XD[0:DTR, :], start=True, stop=True).then_inc(dt_ps.sem, dt_ps.up())
                pe.wait_ge(dtx_ok.sem, dtx_ok.at(b, 1))

                def add_up(n):
                    for j in range(2):
                        pe.wait_ge(hC_ok.sem, hC_ok.at(b, 2 * n + j + 1))
                        mm(bank[2 + j][:, :], ident, hC[:, n % 2, j, :], start=(n == 0), stop=(n == DS - 1)).then_inc(ysum.sem, ysum.up())

                for n in range(DS):
                    for k, row in enumerate((DTR + n, DTR + DS + n)):
                        if n >= 1:
                            pe.wait_ge(bc_sb.sem, bc_sb.at(b, 2 * n - 1 + k))
                        pe.sem_inc(hold_pe, 1)
                        mm(bank[5 + k][:, :], ident[0:40, row:row + 1].to_broadcast([40, P]), XD[:, :],
                                      start=True, stop=True).then_inc(bc_ps.sem, bc_ps.up())
                    if n >= 1:
                        add_up(n - 1)
                add_up(DS - 1)
                pe.wait_ge(yg_ok.sem, yg_ok.at(b, 1))
                for i in range(NT):
                    for j in range(2):
                        m = mm(bank[5][:, i * P:(i + 1) * P], YG[:, j, i * P:(i + 1) * P], w("op")[:, j, :],
                               start=(j == 0), stop=(j == 1))
                m.then_inc(op_ps.sem, op_ps.up())

                pe.wait_ge(ln_ok.sem, ln_ok.at(b, 3))
                pe.sem_inc(hold_pe, 1)
                t2(X1)
                pe.wait_ge(xt_sb.sem, xt_sb.at(b, 4))
                for i in range(NT):
                    m = mm(bank[7][:, i * NE2:(i + 1) * NE2], X1T[:, i * P:(i + 1) * P], w("wg"), start=True, stop=True)
                m.then_inc(rl_ps.sem, rl_ps.up())
                pe.wait_ge(mk_ok.sem, mk_ok.at(b, 1))
                for i in range(NT):
                    o = bank[7][:, 64 + i * NE2:64 + (i + 1) * NE2]
                    mm(o, tri_bf[:, :], mk_bf[:, i, :], start=True, stop=False)
                    for k in range(i):
                        mm(o, ones_bf[:, :], mk_bf[:, k, :], start=False, stop=False)
                    m = mm(o, ones_bf[:, :], cum_bf[:, :], start=False, stop=True)
                m.then_inc(loc_ps.sem, loc_ps.up())
                pe.wait_ge(gate_ok.sem, gate_ok.at(b, 1))
                pe.sem_inc(hold_pe, 1)
                for i in range(NT):
                    m = turn(bank[6][0:NE2, i * P:(i + 1) * P], gate[:, i, :])
                m.then_inc(gT_ps.sem, gT_ps.up())
                pe.wait_ge(gT_sb.sem, gT_sb.at(b, 1))
                pe.sem_inc(hold_pe, 1)
                for i in range(NT):
                    m = mm(bank[7][:, i * P:(i + 1) * P], GTs[:, i * P:(i + 1) * P], w("eb")[0:NE2, :], start=True, stop=True)
                m.then_inc(bias_ps.sem, bias_ps.up())
                for i in range(NT):
                    if i >= 2:
                        pe.wait_ge(e_used.sem, e_used.at(b, i - 1))
                    bk = (5, 6) if i % 2 == 0 else (3, 4)
                    for k in range(2):
                        m = mm(bank[bk[k]][:, :], X1T[:, i * P:(i + 1) * P], w("ew")[:, k * 512:(k + 1) * 512],
                               start=True, stop=True)
                    m.then_inc(e_ps.sem, e_ps.up())

        @block.scalar
        def _(act):
            A = act.activation
            act.wait_ge(s_load, 48)
            A(dl[:, 0, :], w("rawd"), ACT.Exp, scale=-1.0).then_inc(s_seta, 1)
            A(Aneg[:, :, :].rearrange("p a c -> p (a c)"), w("alog").rearrange("p a c -> p (a c)"),
              ACT.Exp).then_inc(s_seta, 1)
            act.wait_ge(set_v.sem, SET_SIN)
            A(dl[:, 4, :], dl[:, 3, :], ACT.Sin)
            A(dl[:, 5, :], dl[:, 3, :], ACT.Sin, scale=0.5).then_inc(s_seta, 1)
            act.wait_ge(set_v.sem, SET_VEC)

            with act.Fori(0, B) as b:

                def softplus_logs(src, steps, done):
                    A(steps[0], src, ACT.Abs).then_inc(act_s.sem, act_s.up())
                    act.wait_ge(act_s.sem, act_s.now(b))
                    A(steps[1], steps[0], ACT.Exp, scale=-1.0).then_inc(act_s.sem, act_s.up())
                    act.wait_ge(act_s.sem, act_s.now(b))
                    A(steps[2], steps[1], ACT.Ln, bias=one[:, :]).then_inc(done.sem, done.up())

                def norm_scale(k):
                    act.wait_ge(var_ok.sem, var_ok.at(b, k))
                    A(lnv[:, :], mv[:, :, 1], ACT.Ln, bias=eps[:, :]).then_inc(act_s.sem, act_s.up())
                    act.wait_ge(act_s.sem, act_s.now(b))
                    A(rstd[:, :], lnv[:, :], ACT.Exp, scale=-0.5).then_inc(rstd_ok.sem, rstd_ok.up())

                act.wait_ge(batch_done.sem, batch_done.at(b, 0))
                act.wait_ge(xt_ps.sem, xt_ps.at(b, 1))
                A(XT[:, :], bank[0][:, :], ACT.Copy).then_inc(xt_sb.sem, xt_sb.up())
                for k, dst in enumerate((KI[:, :], QI[:, 0, :], QI[:, 1, :], CQ[:, :])):
                    act.wait_ge(proj_ps.sem, proj_ps.at(b, k + 1))
                    src = bank[1 + k][0:64, :] if k == 3 else bank[1 + k][:, :]
                    A(dst, src, ACT.Copy).then_inc(proj_sb.sem, proj_sb.up())
                act.wait_ge(kv_ps.sem, kv_ps.at(b, 1))
                kr = bank[0][:, 0:256].rearrange("p (n c) -> p n c", n=NT)[:, :, 32:64]
                softplus_logs(kr, [kr_e[:, s, :, :] for s in range(3)], kr_sp)
                act.wait_ge(kt_ps.sem, kt_ps.at(b, 1))
                A(KT[:, :], bank[1][:, :], ACT.Copy).then_inc(kt_sb.sem, kt_sb.up())

                for i in range(NT):
                    Wi, W0 = index_width(i), first_width(i)
                    c0 = 96 - W0
                    for h in range(NIH):
                        act.wait_ge(ix_ps.sem, ix_ps.at(b, 4 * i + h + 1))
                        if i >= 1 and h == 0:
                            act.wait_ge(ix_used.sem, ix_used.at(b, i))
                        A(relu_s[:, h, 0:Wi], bank[h][:, 0:Wi], ACT.Relu).then_inc(ix_relu.sem, ix_relu.up())
                    act.wait_ge(q_ps.sem, q_ps.at(b, i + 1))
                    if i >= 1:
                        act.wait_ge(q_rows.sem, q_rows.at(b, i))
                    softplus_logs(bank[4][:, 0:256], [q_e[:, s, :] for s in range(3)], q_sp)
                    act.wait_ge(qT_ps.sem, qT_ps.at(b, i + 1 if i == 0 else i + 2))
                    A(QBT[:, :, :].rearrange("p a c -> p (a c)"), bank[2][:, :], ACT.Copy).then_inc(qT_sb.sem, qT_sb.up())
                    if i == 0:
                        act.wait_ge(qT_ps.sem, qT_ps.at(b, 2))
                        A(QAT[:, :, :].rearrange("p a c -> p (a c)"), bank[3][:, :], ACT.Copy).then_inc(qT_sb.sem, qT_sb.up())
                    for r in range(8):
                        act.wait_ge(ib_ps.sem, ib_ps.at(b, 8 * i + r + 1))
                        A(ib[:, 4 * r:4 * r + 4, :].rearrange("p a c -> p (a c)"), bank[r % 2][:, :], ACT.Copy).then_inc(ib_sb.sem, ib_sb.up())
                    for g in range(2):
                        act.wait_ge(ml_ok.sem, ml_ok.at(b, 2 * i + g + 1))
                        for hh in range(4):
                            h = 4 * g + hh
                            sc = bank[2 + hh % 2][:, 256 * (hh // 2) + c0:256 * (hh // 2) + 224]
                            m = A(PL[:, g, hh, c0:224], sc, ACT.Exp, scale=SCALE, bias=nml[:, h:h + 1],
                                  accum_out=ll[:, h:h + 1])
                        m.then_inc(pl_ok.sem, pl_ok.up())
                        act.wait_ge(pt_ps.sem, pt_ps.at(b, 2 * i + g + 1))
                        if g == 0 and i >= 1:
                            act.wait_ge(ol_ps.sem, ol_ps.at(b, 2 * i))
                        if g == 1:
                            act.wait_ge(ol_ps.sem, ol_ps.at(b, 2 * i + 1))
                        A(PLT1[0:W0, :, :].rearrange("p a c -> p (a c)"), bank[0][0:W0, :], ACT.Copy)
                        A(PLT2[:, :, :].rearrange("p a c -> p (a c)"), bank[1][:, :], ACT.Copy).then_inc(pt_sb.sem, pt_sb.up())
                    for c in range(4):
                        act.wait_ge(g_ps.sem, g_ps.at(b, 4 * i + c + 1))
                        if i >= 1 and c == 0:
                            act.wait_ge(ro_ps.sem, ro_ps.at(b, i))
                        A(G[:, 8 * c:8 * c + 8, :].rearrange("p a c -> p (a c)"), bank[2 + c % 2][:, :], ACT.Copy).then_inc(g_sb.sem, g_sb.up())
                    act.wait_ge(sr_d.sem, sr_d.at(b, i + 1))
                    A(PR[:, :, :], SRd[:, :, :], ACT.Exp, scale=SCALE).then_inc(pr_ok.sem, pr_ok.up())
                    act.wait_ge(ro_ps.sem, ro_ps.at(b, i + 1))
                    if i >= 1:
                        act.wait_ge(ro_st.sem, ro_st.at(b, 16 * i))
                    A(RO[:, :, 0:DC], bank[4][:, 256:512].rearrange("p (x c) -> p x c", x=8), ACT.Copy).then_inc(ro_sb.sem, ro_sb.up())
                    act.wait_ge(dm_ok.sem, dm_ok.at(b, i + 1))
                    A(em[:, :, :], dm[:, :, :], ACT.Exp, scale=SCALE).then_inc(em_ok.sem, em_ok.up())
                    act.wait_ge(oT_ps.sem, oT_ps.at(b, i + 1))
                    A(OT[:, :, :].rearrange("p a c -> p (a c)"), bank[5][:, 256:512], ACT.Copy).then_inc(oT_sb.sem, oT_sb.up())
                norm_scale(1)

                act.wait_ge(xt_ps.sem, xt_ps.at(b, 2))
                A(X1T[:, :], bank[6][:, :], ACT.Copy).then_inc(xt_sb.sem, xt_sb.up())
                act.wait_ge(rl_ps.sem, rl_ps.at(b, 1))
                A(rt[:, 0, :, :], bank[7][:, 0:NT * NE].rearrange("p (n e) -> p n e", n=NT), ACT.Exp, scale=-1.0).then_inc(rl_e.sem, rl_e.up())
                act.wait_ge(ct_ps.sem, ct_ps.at(b, 1))
                A(CT[:, :], bank[7][0:NE, :], ACT.Copy).then_inc(ct_sb.sem, ct_sb.up())
                for p in range(NE // 2):
                    act.wait_ge(cb_ps.sem, cb_ps.at(b, p + 1))
                    A(CB[:, p, :], bank[5 + p % 2][:, :], ACT.Copy).then_inc(cb_sb.sem, cb_sb.up())
                for u in range(18):
                    rows = P if u < 16 else 64
                    act.wait_ge(gu_ps.sem, gu_ps.at(b, u + 1))
                    if u >= 2:
                        act.wait_ge(hu_ok.sem, hu_ok.at(b, u - 1))
                    A(SG[0:rows, u % 2, :], bank[5 + u % 2][0:rows, 0:256], ACT.Silu).then_inc(sg_ok.sem, sg_ok.up())
                norm_scale(2)

                act.wait_ge(xt_ps.sem, xt_ps.at(b, 3))
                A(X1T[:, :], bank[6][:, :], ACT.Copy).then_inc(xt_sb.sem, xt_sb.up())
                for k in range(4):
                    act.wait_ge(xz_ps.sem, xz_ps.at(b, k + 1))
                    if k < 2:
                        A(XP[:, k, DCONV - 1:], bank[4 + k % 2][:, :], ACT.Copy).then_inc(xz_sb.sem, xz_sb.up())
                    else:
                        A(SZ[:, k - 2, :], bank[4 + k % 2][:, :], ACT.Silu).then_inc(xz_sb.sem, xz_sb.up())
                for j in range(2):
                    act.wait_ge(cv_ok.sem, cv_ok.at(b, j + 1))
                    A(U[:, j, :], CV[:, j, 1, :], ACT.Silu).then_inc(u_ok.sem, u_ok.up())
                act.wait_ge(xd_ps.sem, xd_ps.at(b, 1))
                A(XD[:, :], bank[7][0:40, :], ACT.Copy).then_inc(xd_sb.sem, xd_sb.up())
                act.wait_ge(dtx_ok.sem, dtx_ok.at(b, 1))
                A(dt_a, dt_x, ACT.Abs).then_inc(act_s.sem, act_s.up())
                act.wait_ge(act_s.sem, act_s.now(b))
                A(dt_b, dt_a, ACT.Exp, scale=-1.0).then_inc(dt_sp.sem, dt_sp.up())
                act.wait_ge(del_ok.sem, del_ok.at(b, 1))
                for n in range(DS):
                    for k, dst in enumerate((Bn, Cn)):
                        act.wait_ge(bc_ps.sem, bc_ps.at(b, 2 * n + k + 1))
                        if n >= 2:
                            free = dBu_ok if k == 0 else hC_ok
                            act.wait_ge(free.sem, free.at(b, 2 * (n - 1)))
                        A(dst[:, n % 2, :], bank[5 + k][:, :], ACT.Copy).then_inc(bc_sb.sem, bc_sb.up())
                    for j in range(2):
                        if n >= 2:
                            act.wait_ge(scan_ok.sem, scan_ok.at(b, 2 * (n - 2) + j + 1))
                        A(dA[:, n % 2, j, :], DEL[:, j, :], ACT.Exp, scale=Aneg[:, j, n:n + 1]).then_inc(dA_ok.sem, dA_ok.up())
                norm_scale(3)

                act.wait_ge(xt_ps.sem, xt_ps.at(b, 4))
                A(X1T[:, :], bank[6][:, :], ACT.Copy).then_inc(xt_sb.sem, xt_sb.up())
                act.wait_ge(pm_ok.sem, pm_ok.at(b, 1))
                A(pr[:, 1, :, :], pr[:, 0, :, :], ACT.Exp).then_inc(pe_ok.sem, pe_ok.up())
                act.wait_ge(gT_ps.sem, gT_ps.at(b, 1))
                A(GTs[:, :], bank[6][0:NE2, :], ACT.Copy).then_inc(gT_sb.sem, gT_sb.up())
                norm_scale(4)

        @block.gpsimd
        def _(pool):
            pool.wait_ge(set_v.sem, SET_VEC)
            pool.wait_ge(s_seta, 3)
            with pool.Fori(0, B) as b:

                pool.wait_ge(batch_done.sem, batch_done.at(b, 0))
                for i in range(NT):
                    pool.wait_ge(g_sb.sem, g_sb.at(b, 4 * i + 4))
                    if i >= 1:
                        pool.wait_ge(gt_ok.sem, gt_ok.at(b, i))
                    sn = trig[:, 1, 8, :].unsqueeze(1).to_broadcast([P, NCOL, HALF])
                    pool.tensor_tensor(g_s[:, :, 0:HALF], G[:, :, DC:DC + HALF], sn, ALU.mult)
                    pool.tensor_tensor(g_s[:, :, HALF:DR], G[:, :, DC + HALF:64], sn, ALU.mult).then_inc(g_sin.sem, g_sin.up())
                for u in range(16):
                    pool.wait_ge(hu_ok.sem, hu_ok.at(b, u + 1))
                    if u >= 2:
                        pool.wait_ge(y_part.sem, y_part.at(b, u - 1))
                    pool.wait_ge(cb_sb.sem, cb_sb.at(b, 8))
                    half = u % 2
                    pool.tensor_tensor(HT[:, u % 2, :], HU[:, u % 2, :], CB[:, u // 2, half * 256:(half + 1) * 256],
                                                  ALU.mult).then_inc(ht_ok.sem, ht_ok.up())
                pool.wait_ge(del_ok.sem, del_ok.at(b, 1))
                for n in range(DS):
                    pool.wait_ge(bc_sb.sem, bc_sb.at(b, 2 * n + 1))
                    for j in range(2):
                        if n >= 2:
                            pool.wait_ge(scan_ok.sem, scan_ok.at(b, 2 * (n - 2) + j + 1))
                        pool.tensor_tensor(dBu[:, n % 2, j, :], DU[:, j, :], Bn[:, n % 2, :], ALU.mult).then_inc(dBu_ok.sem, dBu_ok.up())

        @block.vector
        def _(dve):
            TT, TS, STT, CP = dve.tensor_tensor, dve.tensor_scalar, dve.scalar_tensor_tensor, dve.tensor_copy

            for t in (QBD, PBD, XP):
                ap = t[:, :, :] if t is XP else t[:, :, :, :, :]
                dve.memset(ap, 0.0)
            dve.memset(cum[:, :], 0.0)
            dve.memset(one[:, :], 1.0)
            dve.memset(eps[:, :], EPS)
            dve.memset(ones_bf[:, :], 1.0)
            dve.memset(cum_bf[:, :], 0.0)
            dve.wait_ge(s_load, 48)
            CP(ident_bf[:, :], ident)
            CP(ident_h[:, :], ident)
            CP(tri_bf[:, :], co("tri"))
            CP(lmask_bf[:, :, :], co("lmask"))
            TS(dtb2[:, :], w("dtb"), 2.0, None, ALU.mult)
            CP(WQ[:, 0, :], wh("qr"))
            dve.wait_ge(s_seta, 2)
            TS(Aneg[:, :, :], Aneg[:, :, :], -1.0, None, ALU.mult).then_inc(set_v.sem, set_v.up())
            dve.wait_ge(set_v.sem, set_v.k)
            TS(dl[:, 1, :], dl[:, 0, :], 1.0, None, ALU.add).then_inc(set_v.sem, set_v.up())
            dve.wait_ge(set_v.sem, set_v.k)
            dve.reciprocal(dl[:, 2, :], dl[:, 1, :]).then_inc(set_v.sem, set_v.up())
            dve.wait_ge(set_v.sem, set_v.k)
            TS(dl[:, 3, :], dl[:, 2, :], -2.0 * np.pi, np.pi, ALU.mult, ALU.add).then_inc(set_v.sem, set_v.up())
            dve.wait_ge(set_v.sem, set_v.k)
            TS(dl[:, 3, :], dl[:, 3, :], 3.1415925, -3.1415925, ALU.min, ALU.max).then_inc(set_v.sem, set_v.up())
            dve.wait_ge(set_v.sem, set_v.k)
            assert set_v.k == SET_SIN
            dve.wait_ge(s_setp, 2)
            CP(WQ[:, 1, :], bank[0][0:64, 0:256])
            CP(WVO[:, :, :].rearrange("p a c -> p (a c)"), bank[1][:, 0:256])
            dve.wait_ge(s_seta, 3)
            TT(dl[:, 6, :], dl[:, 5, :], dl[:, 5, :], ALU.mult).then_inc(set_v.sem, set_v.up())
            dve.wait_ge(set_v.sem, set_v.k)
            TS(dl[:, 6, :], dl[:, 6, :], 2.0, -1.0, ALU.mult, ALU.add)
            TS(dl[:, 7, :], dl[:, 4, :], -1.0, None, ALU.mult).then_inc(set_v.sem, set_v.up())
            dve.wait_ge(set_v.sem, set_v.k)
            cd = dl[:, 6, :].unsqueeze(1).to_broadcast([P, 9, HALF])
            sd = dl[:, 7, :].unsqueeze(1).to_broadcast([P, 9, HALF])
            TT(trig[:, 0, :, :], co("cosb"), cd, ALU.mult)
            TT(trig_t[:, 0, :, :], co("sinb"), sd, ALU.mult)
            TT(trig[:, 1, :, :], co("sinb"), cd, ALU.mult)
            TT(trig_t[:, 1, :, :], co("cosb"), sd, ALU.mult).then_inc(set_v.sem, set_v.up())
            dve.wait_ge(set_v.sem, set_v.k)
            TT(trig[:, 0, :, :], trig[:, 0, :, :], trig_t[:, 0, :, :], ALU.subtract)
            TT(trig[:, 1, :, :], trig[:, 1, :, :], trig_t[:, 1, :, :], ALU.add).then_inc(set_v.sem, set_v.up())
            dve.wait_ge(set_v.sem, set_v.k)
            assert set_v.k == SET_VEC
            dve.sem_inc(batch_done.sem, 1)

            with dve.Fori(0, B) as b:

                def norm(k, dst):
                    for i in range(NT):
                        m = dve.bn_stats(stats[:, i, :], Y[:, i, :])
                    m.then_inc(vec.sem, vec.up())
                    dve.wait_ge(vec.sem, vec.now(b))
                    dve.sem_inc(hold_dve, 1)
                    for i in range(NT):
                        m = dve.bn_aggr(mv[:, i, :], stats[:, i, :])
                    m.then_inc(var_ok.sem, var_ok.up())
                    dve.wait_ge(var_ok.sem, var_ok.now(b))
                    dve.wait_ge(rstd_ok.sem, rstd_ok.at(b, k))
                    for i in range(NT):
                        m = TS(dst[:, i, :], Y[:, i, :], mv[:, i, 0:1], rstd[:, i:i + 1], ALU.subtract, ALU.mult)
                    m.then_inc(ln_ok.sem, ln_ok.up())
                    dve.wait_ge(ln_ok.sem, ln_ok.now(b))

                def rotate(dst, src, n, cos, sin, tc, tsn):
                    for s, tmp in ((cos, tc), (sin, tsn)):
                        cc = s.unsqueeze(1).to_broadcast([P, n, HALF])
                        TT(tmp[:, :, 0:HALF], src[:, :, 0:HALF], cc, ALU.mult)
                        m = TT(tmp[:, :, HALF:DR], src[:, :, HALF:DR], cc, ALU.mult)
                    m.then_inc(vec.sem, vec.up())
                    dve.wait_ge(vec.sem, vec.now(b))
                    TT(dst[:, :, 0:HALF], tc[:, :, 0:HALF], tsn[:, :, HALF:DR], ALU.subtract)
                    return TT(dst[:, :, HALF:DR], tc[:, :, HALF:DR], tsn[:, :, 0:HALF], ALU.add)

                dve.wait_ge(kv_ps.sem, kv_ps.at(b, 1))
                dve.wait_ge(proj_sb.sem, proj_sb.at(b, 4))
                dve.wait_ge(kr_sp.sem, kr_sp.at(b, 1))
                kv = bank[0][:, 0:256].rearrange("p (n c) -> p n c", n=NT)
                CP(table[:, :, 0:DC], kv[:, :, 0:DC])
                CP(prev_c[:, :, :], bank[0][0:64, 288:384].rearrange("p (n c) -> p n c", n=3))
                for k in range(2):
                    CP(KD[:, :, k, 0:DC], kv[:, :, 0:DC])
                STT(out=table[:, :, DC:64], in0=kv[:, :, DC:64], scalar=0.0, in1=kr_e[:, 2, :, :],
                         op0=ALU.max, op1=ALU.add).then_inc(vec.sem, vec.up())
                dve.wait_ge(vec.sem, vec.now(b))
                for s in range(2):
                    for hf in range(2):
                        m = TT(krot[:, s, :, HALF * hf:HALF * hf + HALF], table[:, :, DC + HALF * hf:DC + HALF * hf + HALF],
                               trig[:, s, 0:NT, :], ALU.mult)
                m.then_inc(vec.sem, vec.up())
                dve.wait_ge(vec.sem, vec.now(b))
                for k in range(2):
                    TT(KD[:, :, k, DC:DC + HALF], krot[:, 0, :, 0:HALF], krot[:, 1, :, HALF:DR], ALU.subtract)
                    m = TT(KD[:, :, k, DC + HALF:64], krot[:, 0, :, HALF:DR], krot[:, 1, :, 0:HALF], ALU.add)
                m.then_inc(kv_in.sem, kv_in.up())
                CP(tparts[:, :, 0, :], table[:, :, :]).then_inc(vec.sem, vec.up())
                dve.wait_ge(vec.sem, vec.now(b))
                TT(tres[:, 0, :, :], table[:, :, :], tparts[:, :, 0, :], ALU.subtract).then_inc(vec.sem, vec.up())
                dve.wait_ge(vec.sem, vec.now(b))
                CP(tparts[:, :, 1, :], tres[:, 0, :, :]).then_inc(vec.sem, vec.up())
                dve.wait_ge(vec.sem, vec.now(b))
                TT(tres[:, 1, :, :], tres[:, 0, :, :], tparts[:, :, 1, :], ALU.subtract).then_inc(vec.sem, vec.up())
                dve.wait_ge(vec.sem, vec.now(b))
                CP(tparts[:, :, 2, :], tres[:, 1, :, :]).then_inc(parts_ok.sem, parts_ok.up())
                dve.wait_ge(parts_ok.sem, parts_ok.now(b))

                for i in range(NT):
                    Wi, W0 = index_width(i), first_width(i)
                    c0 = 96 - W0
                    dve.wait_ge(ix_relu.sem, ix_relu.at(b, 4 * i + 1))
                    TS(score[:, 0, 0:Wi], relu_s[:, 0, 0:Wi], w("idxw")[:, 0:1], None, ALU.mult).then_inc(vec.sem, vec.up())
                    dve.wait_ge(vec.sem, vec.now(b))
                    for h in range(1, NIH):
                        dve.wait_ge(ix_relu.sem, ix_relu.at(b, 4 * i + h + 1))
                        m = STT(out=score[:, 0, 0:Wi], in0=relu_s[:, h, 0:Wi], scalar=w("idxw")[:, h:h + 1],
                                in1=score[:, 0, 0:Wi], op0=ALU.mult, op1=ALU.add)
                        done = ix_used if h == NIH - 1 else vec
                        m.then_inc(done.sem, done.up())
                        dve.wait_ge(done.sem, done.now(b))
                    lo = 0 if i == 0 else Wi - P
                    mask = co("top0") if i == 0 else co("top1")
                    TT(score[:, 0, lo:Wi], score[:, 0, lo:Wi], mask, ALU.add).then_inc(vec.sem, vec.up())
                    dve.wait_ge(vec.sem, vec.now(b))
                    dve.sem_inc(hold_dve, 1)
                    for r in range(NREM // 8):
                        cur, nxt = score[:, r % 2, 0:Wi], score[:, (r + 1) % 2, 0:Wi]
                        dve.max(top[:, 8 * r:8 * r + 8], cur).then_inc(vec.sem, vec.up())
                        dve.wait_ge(vec.sem, vec.now(b))
                        dve.sem_inc(hold_dve, 1)
                        m = dve.max_index(idx[:, 8 * r:8 * r + 8], top[:, 8 * r:8 * r + 8], cur)
                        if r < 3:
                            m = dve.match_replace(nxt, top[:, 8 * r:8 * r + 8], cur, NEG_TOP)
                        m.then_inc(vec.sem, vec.up())
                        dve.wait_ge(vec.sem, vec.now(b))
                        dve.sem_inc(hold_dve, 1)
                    dve.transpose(idxT[:, :], idx[:, :]).then_inc(vec.sem, vec.up())
                    dve.wait_ge(vec.sem, vec.now(b))
                    CP(idxh[:, :], idxT[:, :]).then_inc(idx_ok.sem, idx_ok.up())
                    dve.wait_ge(idx_ok.sem, idx_ok.now(b))
                    dve.wait_ge(q_sp.sem, q_sp.at(b, i + 1))
                    STT(out=muq[:, :, :].rearrange("p h c -> p (h c)"), in0=bank[4][:, 0:256], scalar=0.0,
                             in1=q_e[:, 2, :], op0=ALU.max, op1=ALU.add).then_inc(vec.sem, vec.up())
                    dve.wait_ge(vec.sem, vec.now(b))
                    CP(QA[:, :, 0, :], bank[4][:, 256:512].rearrange("p (h c) -> p h c", h=NH))
                    CP(QB[:, :, 0, :], bank[4][:, 256:512].rearrange("p (h c) -> p h c", h=NH))
                    rotate(QA[:, :, 1, :], muq, NH, trig[:, 0, i, :], trig[:, 1, i, :], qr_c, qr_s).then_inc(vec.sem, vec.up())
                    dve.wait_ge(vec.sem, vec.now(b))
                    rotate(QB[:, :, 1, :], muq, NH, trig[:, 0, 4 + i, :], trig[:, 1, 4 + i, :], qr_c, qr_s).then_inc(q_rows.sem, q_rows.up())
                    dve.wait_ge(q_rows.sem, q_rows.now(b))
                    dve.transpose(QT[:, :, :, :], QA[:, :, :, :]).then_inc(vec.sem, vec.up())
                    dve.wait_ge(vec.sem, vec.now(b))
                    for bb in range(4):
                        m = CP(QBD[32 * bb:32 * bb + 32, :, :, bb, :].rearrange("p t k h -> p k h t"),
                               QT[32 * bb:32 * bb + 32, :, :, :].rearrange("p h k t -> p k h t"))
                    for g in range(2):
                        dve.wait_ge(sl_ps.sem, sl_ps.at(b, 2 * i + g + 1))
                        for k in range(2):
                            m = dve.tensor_reduce(ml[:, 4 * g + k:4 * g + k + 3:2],
                                                  bank[2 + k][:, :].rearrange("p (h c) -> p h c", h=2)[:, :, c0:224],
                                                  AX.X, ALU.max)
                        m.then_inc(vec.sem, vec.up())
                        dve.wait_ge(vec.sem, vec.now(b))
                        TS(nml[:, 4 * g:4 * g + 4], ml[:, 4 * g:4 * g + 4], -SCALE, None, ALU.mult).then_inc(ml_ok.sem, ml_ok.up())
                    for c in range(4):
                        dve.wait_ge(ib_sb.sem, ib_sb.at(b, 8 * i + 2 * c + 2))
                        if 4 * i + c >= 2:
                            dve.wait_ge(g_ps.sem, g_ps.at(b, 4 * i + c - 1))
                        for kt in range(i + 1):
                            kk = 64 if kt == i else P
                            m = TS(onehot[0:kk, c % 2, kt, :],
                                   ib[0:kk, 8 * c:8 * c + 8, :].rearrange("p a c -> p (a c)"), co("pos")[0:kk, kt:kt + 1], None,
                                   ALU.is_equal)
                        m.then_inc(oh_ok.sem, oh_ok.up())
                    dve.wait_ge(g_sb.sem, g_sb.at(b, 4 * i + 4))
                    cs = trig[:, 0, 8, :].unsqueeze(1).to_broadcast([P, NCOL, HALF])
                    TT(g_c[:, :, 0:HALF], G[:, :, DC:DC + HALF], cs, ALU.mult)
                    TT(g_c[:, :, HALF:DR], G[:, :, DC + HALF:64], cs, ALU.mult).then_inc(vec.sem, vec.up())
                    dve.wait_ge(vec.sem, vec.now(b))
                    dve.wait_ge(g_sin.sem, g_sin.at(b, i + 1))
                    TT(GR[:, :, 0:HALF], g_c[:, :, 0:HALF], g_s[:, :, HALF:DR], ALU.subtract)
                    TT(GR[:, :, HALF:DR], g_c[:, :, HALF:DR], g_s[:, :, 0:HALF], ALU.add)
                    dve.transpose(GT[:, 0, :, :], G[:, :, 0:DC]).then_inc(vec.sem, vec.up())
                    dve.wait_ge(vec.sem, vec.now(b))
                    dve.transpose(GT[:, 1, :, :], GR[:, :, :]).then_inc(gt_ok.sem, gt_ok.up())
                    dve.wait_ge(gt_ok.sem, gt_ok.now(b))
                    dve.wait_ge(sr_ps.sem, sr_ps.at(b, i + 1))
                    sp_ = bank[4][:, 0:256].rearrange("p (x j) -> p x j", x=8)
                    if i == 0:
                        TT(SR[:, :, :], sp_, co("rmask"), ALU.add).then_inc(vec.sem, vec.up())
                        dve.wait_ge(vec.sem, vec.now(b))
                        sp_ = SR[:, :, :]
                    else:
                        dve.wait_ge(ro_st.sem, ro_st.at(b, 16 * i))
                    dve.tensor_reduce(RO[:, :, 32], sp_, AX.X, ALU.max).then_inc(vec.sem, vec.up())
                    dve.wait_ge(vec.sem, vec.now(b))
                    TT(SRd[:, :, :], sp_, RO[:, :, 32:33].to_broadcast([P, 8, 32]), ALU.subtract).then_inc(sr_d.sem, sr_d.up())
                    dve.wait_ge(sr_d.sem, sr_d.now(b))
                    dve.wait_ge(pr_ok.sem, pr_ok.at(b, i + 1))
                    dve.tensor_reduce(RO[:, :, 33], PR[:, :, :], AX.X, ALU.add)
                    dve.transpose(PT[:, :, :], PR[:, :, :]).then_inc(vec.sem, vec.up())
                    dve.wait_ge(vec.sem, vec.now(b))
                    for a in range(4):
                        for bb in range(4):
                            m = CP(PBD[32 * bb:32 * bb + 32, :, a, bb, :], PT[32 * a:32 * a + 32, :, 8 * bb:8 * bb + 8])
                    m.then_inc(pbd_ok.sem, pbd_ok.up())
                    dve.wait_ge(rb_in.sem, rb_in.at(b, i + 1))
                    dve.wait_ge(ol_ps.sem, ol_ps.at(b, 2 * i + 2))
                    TT(mj[:, :], ml[:, :], RB[:, :, 32], ALU.max).then_inc(vec.sem, vec.up())
                    dve.wait_ge(vec.sem, vec.now(b))
                    TT(dm[:, 0, :], ml[:, :], mj[:, :], ALU.subtract)
                    TT(dm[:, 1, :], RB[:, :, 32], mj[:, :], ALU.subtract).then_inc(dm_ok.sem, dm_ok.up())
                    dve.wait_ge(dm_ok.sem, dm_ok.now(b))
                    dve.wait_ge(em_ok.sem, em_ok.at(b, i + 1))
                    TT(den[:, 0, :], ll[:, :], em[:, 0, :], ALU.mult)
                    TT(den[:, 1, :], RB[:, :, 33], em[:, 1, :], ALU.mult).then_inc(vec.sem, vec.up())
                    dve.wait_ge(vec.sem, vec.now(b))
                    TT(den[:, 2, :], den[:, 0, :], den[:, 1, :], ALU.add).then_inc(vec.sem, vec.up())
                    dve.wait_ge(vec.sem, vec.now(b))
                    dve.reciprocal(den[:, 3, :], den[:, 2, :]).then_inc(vec.sem, vec.up())
                    dve.wait_ge(vec.sem, vec.now(b))
                    TT(fac[:, :, :], em[:, :, :], den[:, 3, :].unsqueeze(1).to_broadcast([P, 2, NH]), ALU.mult).then_inc(vec.sem, vec.up())
                    dve.wait_ge(vec.sem, vec.now(b))
                    TT(On[:, 0, :, :], bank[5][:, 0:256].rearrange("p (h c) -> p h c", h=NH),
                       fac[:, 0, :].unsqueeze(2).to_broadcast([P, NH, DC]), ALU.mult)
                    TT(On[:, 1, :, :], RB[:, :, 0:DC], fac[:, 1, :].unsqueeze(2).to_broadcast([P, NH, DC]), ALU.mult).then_inc(vec.sem, vec.up())
                    dve.wait_ge(vec.sem, vec.now(b))
                    TT(On[:, 0, :, :], On[:, 0, :, :], On[:, 1, :, :], ALU.add).then_inc(on_ok.sem, on_ok.up())
                    dve.wait_ge(on_ok.sem, on_ok.now(b))
                    dve.wait_ge(at_ps.sem, at_ps.at(b, i + 1))
                    TT(Y[:, i, :], bank[4][:, 0:P], X[:, i, :], ALU.add).then_inc(at_used.sem, at_used.up())
                    dve.wait_ge(at_used.sem, at_used.now(b))
                norm(1, X1)

                dve.wait_ge(rl_e.sem, rl_e.at(b, 1))
                TS(rt[:, 1, :, :], rt[:, 0, :, :], 1.0, None, ALU.add).then_inc(vec.sem, vec.up())
                dve.wait_ge(vec.sem, vec.now(b))
                dve.reciprocal(rt[:, 2, :, :], rt[:, 1, :, :]).then_inc(vec.sem, vec.up())
                dve.wait_ge(vec.sem, vec.now(b))
                TT(rt[:, 3, :, :], rt[:, 2, :, :], w("gb").unsqueeze(1).to_broadcast([P, NT, NE]), ALU.add).then_inc(vec.sem, vec.up())
                dve.wait_ge(vec.sem, vec.now(b))
                dve.sem_inc(hold_dve, 1)
                for i in range(NT):
                    m = dve.max(r8[:, i, :], rt[:, 3, i, :])
                m.then_inc(vec.sem, vec.up())
                dve.wait_ge(vec.sem, vec.now(b))
                dve.sem_inc(hold_dve, 1)
                for i in range(NT):
                    m = dve.max_index(ri[:, i, :], r8[:, i, :], rt[:, 3, i, :])
                m.then_inc(vec.sem, vec.up())
                dve.wait_ge(vec.sem, vec.now(b))
                CP(rif[:, :, :], ri[:, :, :]).then_inc(vec.sem, vec.up())
                dve.wait_ge(vec.sem, vec.now(b))
                for i in range(NT):
                    m = TT(req[:, i, :, :], co("iota")[:, 0:NE].unsqueeze(2).to_broadcast([P, NE, TOP_E]),
                           rif[:, i, 0:TOP_E].unsqueeze(1).to_broadcast([P, NE, TOP_E]), ALU.is_equal)
                m.then_inc(vec.sem, vec.up())
                dve.wait_ge(vec.sem, vec.now(b))
                dve.tensor_reduce(rt[:, 4, :, :], req[:, :, :, :], AX.X, ALU.add).then_inc(vec.sem, vec.up())
                dve.wait_ge(vec.sem, vec.now(b))
                TT(rt[:, 4, :, :], rt[:, 4, :, :], rt[:, 2, :, :], ALU.mult).then_inc(vec.sem, vec.up())
                dve.wait_ge(vec.sem, vec.now(b))
                dve.tensor_reduce(rs[:, 0, :], rt[:, 4, :, :], AX.X, ALU.add).then_inc(vec.sem, vec.up())
                dve.wait_ge(vec.sem, vec.now(b))
                dve.reciprocal(rs[:, 1, :], rs[:, 0, :]).then_inc(vec.sem, vec.up())
                dve.wait_ge(vec.sem, vec.now(b))
                STT(out=rt[:, 5, :, :], in0=rt[:, 4, :, :], scalar=ROUTE,
                         in1=rs[:, 1, :].unsqueeze(2).to_broadcast([P, NT, NE]), op0=ALU.mult, op1=ALU.mult).then_inc(comb_ok.sem, comb_ok.up())
                dve.wait_ge(comb_ok.sem, comb_ok.now(b))
                for u in range(18):
                    dve.wait_ge(sg_ok.sem, sg_ok.at(b, u + 1))
                    rows = P if u < 16 else 64
                    dst = HU if u < 16 else HT
                    if 2 <= u < 16:
                        dve.wait_ge(ht_ok.sem, ht_ok.at(b, u - 1))
                    if u >= 16:
                        dve.wait_ge(y_part.sem, y_part.at(b, u - 1))
                    TT(dst[0:rows, u % 2, :], SG[0:rows, u % 2, :], bank[5 + u % 2][0:rows, 256:512], ALU.mult).then_inc(hu_ok.sem, hu_ok.up())
                dve.wait_ge(y_part.sem, y_part.at(b, 18))
                TT(Y[:, :, :], bank[7][:, :].rearrange("p (n d) -> p n d", n=NT), X1[:, :, :], ALU.add).then_inc(vec.sem, vec.up())
                dve.wait_ge(vec.sem, vec.now(b))
                norm(2, X1)

                for j in range(2):
                    dve.wait_ge(xz_sb.sem, xz_sb.at(b, j + 1))
                    cw = w("cw")[:, j, :]
                    TS(CV[:, j, 0, :], XP[:, j, 0:L], cw[:, 0:1], w("cb")[:, j:j + 1], ALU.mult, ALU.add).then_inc(vec.sem, vec.up())
                    dve.wait_ge(vec.sem, vec.now(b))
                    for k in range(1, DCONV):
                        m = STT(out=CV[:, j, k % 2, :], in0=XP[:, j, k:k + L], scalar=cw[:, k:k + 1],
                                in1=CV[:, j, (k + 1) % 2, :], op0=ALU.mult, op1=ALU.add)
                        done = cv_ok if k == DCONV - 1 else vec
                        m.then_inc(done.sem, done.up())
                        dve.wait_ge(done.sem, done.now(b))
                for j in range(2):
                    dve.wait_ge(dt_ps.sem, dt_ps.at(b, j + 1))
                    m = TS(dt_x[:, j, :], bank[5 + j][:, :], dtb2[:, j:j + 1], None, ALU.add)
                m.then_inc(dtx_ok.sem, dtx_ok.up())
                dve.wait_ge(dtx_ok.sem, dtx_ok.now(b))
                dve.wait_ge(dt_sp.sem, dt_sp.at(b, 1))
                TS(dt_a, dt_b, 2.0, None, ALU.add).then_inc(vec.sem, vec.up())
                dve.wait_ge(vec.sem, vec.now(b))
                dve.reciprocal(dt_c, dt_a).then_inc(vec.sem, vec.up())
                dve.wait_ge(vec.sem, vec.now(b))
                TT(dt_a, dt_b, dt_c, ALU.mult).then_inc(vec.sem, vec.up())
                dve.wait_ge(vec.sem, vec.now(b))
                TT(dt_c, dt_a, dt_a, ALU.mult).then_inc(vec.sem, vec.up())
                dve.wait_ge(vec.sem, vec.now(b))
                TS(dt_b, dt_c, LOG1P[4], None, ALU.mult).then_inc(vec.sem, vec.up())
                dve.wait_ge(vec.sem, vec.now(b))
                for c in LOG1P[3:0:-1]:
                    STT(out=dt_b, in0=dt_b, scalar=c, in1=dt_c, op0=ALU.add, op1=ALU.mult).then_inc(vec.sem, vec.up())
                    dve.wait_ge(vec.sem, vec.now(b))
                STT(out=dt_b, in0=dt_b, scalar=LOG1P[0], in1=dt_a, op0=ALU.add, op1=ALU.mult).then_inc(vec.sem, vec.up())
                dve.wait_ge(vec.sem, vec.now(b))
                STT(out=DEL[:, :, :], in0=dt_x, scalar=0.0, in1=dt_b, op0=ALU.max, op1=ALU.add).then_inc(vec.sem, vec.up())
                dve.wait_ge(vec.sem, vec.now(b))
                dve.wait_ge(u_ok.sem, u_ok.at(b, 2))
                TT(DU[:, :, :], DEL[:, :, :], U[:, :, :], ALU.mult).then_inc(del_ok.sem, del_ok.up())
                dve.wait_ge(del_ok.sem, del_ok.now(b))
                for n in range(DS):
                    for j in range(2):
                        dve.wait_ge(dA_ok.sem, dA_ok.at(b, 2 * n + j + 1))
                        dve.wait_ge(dBu_ok.sem, dBu_ok.at(b, 2 * n + j + 1))
                        dve.tensor_tensor_scan(hs[:, n % 2, j, :], dA[:, n % 2, j, :], dBu[:, n % 2, j, :], 0.0,
                                                    ALU.mult, ALU.add).then_inc(scan_ok.sem, scan_ok.up())
                        dve.wait_ge(scan_ok.sem, scan_ok.now(b))
                        dve.wait_ge(bc_sb.sem, bc_sb.at(b, 2 * n + 2))
                        if n >= 2:
                            dve.wait_ge(ysum.sem, ysum.at(b, 2 * (n - 2) + j + 1))
                        TT(hC[:, n % 2, j, :], hs[:, n % 2, j, :], Cn[:, n % 2, :], ALU.mult).then_inc(hC_ok.sem, hC_ok.up())
                dve.wait_ge(ysum.sem, ysum.at(b, 2 * DS))
                for j in range(2):
                    m = STT(out=CV[:, j, 0, :], in0=U[:, j, :], scalar=w("Dp")[:, j:j + 1], in1=bank[2 + j][:, :],
                            op0=ALU.mult, op1=ALU.add)
                m.then_inc(vec.sem, vec.up())
                dve.wait_ge(vec.sem, vec.now(b))
                TT(YG[:, :, :], CV[:, :, 0, :], SZ[:, :, :], ALU.mult).then_inc(yg_ok.sem, yg_ok.up())
                dve.wait_ge(yg_ok.sem, yg_ok.now(b))
                dve.wait_ge(op_ps.sem, op_ps.at(b, 1))
                TT(Y[:, :, :], bank[5][:, :].rearrange("p (n d) -> p n d", n=NT), X1[:, :, :], ALU.add).then_inc(vec.sem, vec.up())
                dve.wait_ge(vec.sem, vec.now(b))
                norm(3, X1)

                dve.wait_ge(rl_ps.sem, rl_ps.at(b, 2))
                lg = bank[7][:, 0:NT * NE2].rearrange("p (n e) -> p n e", n=NT)
                dve.tensor_reduce(ps1[:, 0, :], lg, AX.X, ALU.max).then_inc(vec.sem, vec.up())
                dve.wait_ge(vec.sem, vec.now(b))
                TT(pr[:, 0, :, :], lg, ps1[:, 0, :].unsqueeze(2).to_broadcast([P, NT, NE2]), ALU.subtract).then_inc(pm_ok.sem, pm_ok.up())
                dve.wait_ge(pm_ok.sem, pm_ok.now(b))
                dve.wait_ge(pe_ok.sem, pe_ok.at(b, 1))
                dve.tensor_reduce(ps1[:, 1, :], pr[:, 1, :, :], AX.X, ALU.add).then_inc(vec.sem, vec.up())
                dve.wait_ge(vec.sem, vec.now(b))
                dve.reciprocal(ps1[:, 2, :], ps1[:, 1, :]).then_inc(vec.sem, vec.up())
                dve.wait_ge(vec.sem, vec.now(b))
                TT(pr[:, 2, :, :], pr[:, 1, :, :], ps1[:, 2, :].unsqueeze(2).to_broadcast([P, NT, NE2]), ALU.mult).then_inc(vec.sem, vec.up())
                dve.wait_ge(vec.sem, vec.now(b))
                dve.sem_inc(hold_dve, 1)
                for i in range(NT):
                    m = dve.max(r8[:, i, :], pr[:, 2, i, :])
                m.then_inc(vec.sem, vec.up())
                dve.wait_ge(vec.sem, vec.now(b))
                dve.sem_inc(hold_dve, 1)
                for i in range(NT):
                    m = dve.max_index(ri[:, i, :], r8[:, i, :], pr[:, 2, i, :])
                m.then_inc(vec.sem, vec.up())
                dve.wait_ge(vec.sem, vec.now(b))
                CP(rif[:, :, :], ri[:, :, :]).then_inc(vec.sem, vec.up())
                dve.wait_ge(vec.sem, vec.now(b))
                TT(mk[:, :, :], co("iota")[:, 0:NE2].unsqueeze(1).to_broadcast([P, NT, NE2]),
                        rif[:, :, 0:1].to_broadcast([P, NT, NE2]), ALU.is_equal).then_inc(vec.sem, vec.up())
                dve.wait_ge(vec.sem, vec.now(b))
                CP(mk_bf[:, :, :], mk[:, :, :]).then_inc(mk_ok.sem, mk_ok.up())
                dve.wait_ge(mk_ok.sem, mk_ok.now(b))
                TT(pr[:, 3, :, :], pr[:, 2, :, :], mk[:, :, :], ALU.mult).then_inc(vec.sem, vec.up())
                dve.wait_ge(vec.sem, vec.now(b))
                dve.wait_ge(loc_ps.sem, loc_ps.at(b, 1))
                TS(keep[:, :, :], bank[7][:, 64:64 + NT * NE2].rearrange("p (n e) -> p n e", n=NT), float(CAP), None,
                        ALU.is_lt).then_inc(vec.sem, vec.up())
                dve.wait_ge(vec.sem, vec.now(b))
                TT(gate[:, :, :], pr[:, 3, :, :], keep[:, :, :], ALU.mult).then_inc(gate_ok.sem, gate_ok.up())
                dve.wait_ge(gate_ok.sem, gate_ok.now(b))
                dve.tensor_reduce(csum[:, :], mk[:, :, :].rearrange("p n e -> p e n"), AX.X, ALU.add).then_inc(vec.sem, vec.up())
                dve.wait_ge(vec.sem, vec.now(b))
                TT(cum[:, :], cum[:, :], csum[:, :], ALU.add).then_inc(vec.sem, vec.up())
                dve.wait_ge(vec.sem, vec.now(b))
                CP(cum_bf[:, :], cum[:, :]).then_inc(vec.sem, vec.up())
                dve.wait_ge(vec.sem, vec.now(b))
                dve.wait_ge(bias_ps.sem, bias_ps.at(b, 1))
                TT(Y[:, :, :], bank[7][:, :].rearrange("p (n d) -> p n d", n=NT), X1[:, :, :], ALU.add).then_inc(vec.sem, vec.up())
                dve.wait_ge(vec.sem, vec.now(b))
                for i in range(NT):
                    dve.wait_ge(e_ps.sem, e_ps.at(b, i + 1))
                    bk = (5, 6) if i % 2 == 0 else (3, 4)
                    for e in range(NE2):
                        m = STT(out=Y[:, i, :], in0=bank[bk[e // 4]][:, (e % 4) * P:(e % 4 + 1) * P],
                                scalar=gate[:, i, e:e + 1], in1=Y[:, i, :], op0=ALU.mult, op1=ALU.add)
                        done = e_used if e == NE2 - 1 else vec
                        m.then_inc(done.sem, done.up())
                        dve.wait_ge(done.sem, done.now(b))
                dve.wait_ge(out_stored.sem, out_stored.at(b, 0))
                for i in range(NT):
                    m = dve.bn_stats(stats[:, i, :], Y[:, i, :])
                m.then_inc(vec.sem, vec.up())
                dve.wait_ge(vec.sem, vec.now(b))
                dve.sem_inc(hold_dve, 1)
                for i in range(NT):
                    m = dve.bn_aggr(mv[:, i, :], stats[:, i, :])
                m.then_inc(var_ok.sem, var_ok.up())
                dve.wait_ge(var_ok.sem, var_ok.now(b))
                dve.wait_ge(rstd_ok.sem, rstd_ok.at(b, 4))
                for i in range(NT):
                    m = TS(OUT[:, i, :], Y[:, i, :], mv[:, i, 0:1], rstd[:, i:i + 1], ALU.subtract, ALU.mult)
                m.then_inc(batch_done.sem, batch_done.up())

        for name, s in signals.items():
            assert s.k == s.per, f"{name} rises {s.k} times in a batch row, not {s.per}"


PER = {"vec": 203, "act": 15}
SET_SIN = 5
SET_VEC = 9


def pack(pieces, rows):
    where, cols, off = {}, [], 0
    for name, a in pieces.items():
        a = np.asarray(a)
        where[name] = (off, a.shape[0], a.shape[1:])
        flat = a.reshape(a.shape[0], -1)
        if a.shape[0] < rows:
            flat = np.concatenate([flat, np.zeros((rows - a.shape[0], flat.shape[1]), flat.dtype)], 0)
        cols.append(flat)
        off += flat.shape[1]
    return np.ascontiguousarray(np.concatenate(cols, 1)), where


def constants():
    p = np.arange(P)[:, None]
    c = np.arange(P)[None, :]
    theta = (1.0 / np.float32(10000.0) ** (2.0 * np.arange(HALF, dtype=np.float32) / DR)).astype(np.float32)
    pos = np.zeros((P, 9), np.float32)
    for i in range(NT):
        pos[:, i] = P * i + np.arange(P)
        pos[:, 4 + i] = 2 * (P * i + np.arange(P)) - (LW - 1)
    pos[:, 8] = LW + np.arange(P) % 32
    ang = (pos[:, :, None] * theta[None, None, :]).astype(np.float32).astype(np.float64)
    lm = np.full((P, 2, 224), NEG, np.float32)
    a96, s128 = np.arange(96)[None, :], np.arange(P)[None, :]
    lm[:, 0, 0:96][(p < 64) | ((p <= TOPK - 2) & (a96 > p))] = 0
    lm[:, 0, 96:224][(p >= 64) & (s128 <= p) & (s128 >= p - (LW - 1))] = 0
    w192 = np.arange(192)[None, :] - 64
    lm[:, 1, 32:224][(w192 <= p) & (w192 >= p - (LW - 1))] = 0
    a, bb, xx, j = (np.arange(P) // 32)[:, None, None], (np.arange(P) // 8 % 4)[:, None, None], \
        np.arange(8)[None, :, None], np.arange(32)[None, None, :]
    t = 32 * bb + 4 * xx + a
    f = np.float32
    return {
        "ident": np.eye(P, dtype=f), "tri": (p < c).astype(f), "lmask": lm,
        "top0": np.where(c[:, 0:64] <= p - 64, 0, NEG_TOP).astype(f), "top1": np.where(c <= p, 0, NEG_TOP).astype(f),
        "rmask": np.where(j <= t - LW, 0, NEG).astype(f),
        "cosb": np.cos(ang).astype(f), "sinb": np.sin(ang).astype(f),
        "pos": (p + P * np.arange(NT)[None, :]).astype(f), "iota": np.broadcast_to(np.arange(NE), (P, NE)).astype(f),
    }


def kernel(**inputs):
    import concourse.bacc as _bacc
    from concourse.bass_utils import run_bass_kernel_spmd as _run

    a = {k: np.asarray(v) for k, v in inputs.items()}
    g = lambda n: a["L0_attn_" + n]
    f = lambda n: a["L0_ffn_" + n]
    m = lambda n: a["L1_attn_" + n]
    rows = lambda v: np.broadcast_to(v[None, :], (P, v.shape[0]))
    w13 = f("w13").transpose(2, 0, 1)
    w128, at128 = pack({
        "wk2": np.concatenate([g("idx_wk"), g("idx_wk")], 1), "wq": g("idx_wq"), "dq": g("W_dq"),
        "kv": np.concatenate([g("W_dkv"), g("W_kr")], 1), "idxw": rows(g("idx_w")), "rawd": rows(g("raw_delta")),
        "gate": f("gate_w").T, "gb": rows(f("gate_b")),
        "w1g": w13[:, :, 0:64].reshape(D, NE // 2, P), "w1u": w13[:, :, 64:].reshape(D, NE // 2, P),
        "w1sg": f("w13_s").T[:, 0:64], "w1su": f("w13_s").T[:, 64:],
        "w2": f("w2").transpose(0, 2, 1).reshape(NE // 2, P, D).transpose(1, 0, 2), "w2s": f("w2_s").T,
        "inp": m("in_proj_w").T, "cw": m("conv_w")[:, 0, :].reshape(2, P, DCONV).transpose(1, 0, 2),
        "cb": m("conv_b").reshape(2, P).T, "xp": m("x_proj_w").T.reshape(2, P, 40).transpose(1, 0, 2),
        "dtw": m("dt_proj_w").T, "dtb": m("dt_proj_b").reshape(2, P).T,
        "alog": m("A_log").reshape(2, P, DS).transpose(1, 0, 2), "Dp": m("D").reshape(2, P).T,
        "op": m("out_proj_w").T.reshape(2, P, D).transpose(1, 0, 2),
        "wg": a["L1_ffn_wg"], "ew": a["L1_ffn_W"].transpose(2, 0, 1).reshape(D, NE2 * D), "eb": a["L1_ffn_b"],
    }, P)
    w64, at64 = pack({
        "qr": g("W_qr"), "uqT": g("W_uq").reshape(DQ, NH, DH).transpose(2, 1, 0),
        "ukT": g("W_uk").reshape(DC, NH, DH).transpose(2, 1, 0), "uvT": g("W_uv").reshape(DC, NH, DH).transpose(2, 1, 0),
        "out": g("W_out").reshape(NH, DH, D).transpose(1, 0, 2),
    }, 64)
    consts, atc = pack(constants(), P)
    arrays = {"x": np.ascontiguousarray(g("x")), "w128": w128, "w64": w64, "consts": consts}
    nc = _bacc.Bacc("TRN2", target_bir_lowering=False, num_devices=1)
    aps = [nc.dram_tensor(k, v.shape, mybir.dt.from_np(v.dtype), kind="ExternalInput").ap() for k, v in arrays.items()]
    o = nc.dram_tensor("out", (B, L, D), F32, kind="ExternalOutput").ap()
    nc.disable_value_cache = True
    build(nc, *aps, o, at128, at64, atc)
    r = _run(nc, [arrays], core_ids=[0])
    return r.results[0]["out"]
```

```python
from contextlib import ExitStack

import numpy as np

import concourse.bass as bass
from concourse import mybir

F32 = mybir.dt.float32
F16 = mybir.dt.float16
BF16 = mybir.dt.bfloat16
U32 = mybir.dt.uint32
ALU = mybir.AluOpType
ACT = mybir.ActivationFunctionType
AX = mybir.AxisListType

B, L, D = 4, 512, 128
P = 128
NT = L // P
NH, DH, DR, DC, DQ = 8, 64, 32, 32, 64
HALF = DR // 2
NIH = 4
TOPK, LW = 96, 64
NREM = TOPK - LW
NCOL = P // 4
SCALE = float(DH + DR) ** -0.5
NEG_TOP = -3.0e38
NEG = -1.0e30
NE, INTER, TOP_E = 16, 64, 4
ROUTE = 2.5
DI, DS, DCONV, DTR = 256, 16, 4, 8
NE2 = 8
CAP = B * L // NE2
EPS = 1e-5
LOG1P = (2.000000007877749, 0.6666631593507906, 0.4002485372356232, 0.2796141883332212, 0.28174657270344106)


class Signal:

    def __init__(self, sem, per, unit=1, first=0):
        self.sem, self.per, self.unit, self.first, self.k = sem, per, unit, first, 0

    def up(self):
        self.k = self.k % self.per + 1
        return self.unit

    def now(self, b):
        return self.at(b, self.k)

    def at(self, b, k):
        return b * (self.per * self.unit) + (self.first + k) * self.unit


def index_width(i):
    return P * i + P - LW


def first_width(i):
    return TOPK if i == 0 else LW


def build(nc, x, w128, w64, consts, setup_c, out, at128, at64, atc, ats):
    with ExitStack() as ctx:
        def sb(name, shape, dt=F32):
            return ctx.enter_context(nc.sbuf_tensor(name, shape, dt))

        def semaphore(name):
            return ctx.enter_context(nc.semaphore(name))

        def signal(name, per, unit=1, first=0):
            s = Signal(semaphore(name), per, unit, first)
            signals[name] = s
            return s

        signals = {}
        bank = [ctx.enter_context(nc.psum_tensor(f"bank{n}", [P, 512], F32)) for n in range(8)]

        W = sb("W", [P, w128.shape[1]])
        CO = sb("CO", [P, consts.shape[1]])
        big = sb("big", [P, 4, 2, L])
        flat = big[:, :, :, :].rearrange("p k j t -> p (k j t)")
        n_c, n_w = setup_c.shape[1], w64.shape[1]
        CS, WH = flat[:, 0:n_c], flat[0:64, n_c:n_c + n_w]

        def piece(t, table, name):
            off, rows, shape = table[name]
            ap = t[0:rows, off:off + int(np.prod(shape))]
            if len(shape) == 2:
                ap = ap.rearrange("p (a c) -> p a c", a=shape[0])
            if len(shape) == 3:
                ap = ap.rearrange("p (a b c) -> p a b c", a=shape[0], b=shape[1])
            return ap

        def w(name):
            return piece(W, at128, name)

        def wh(name):
            return piece(WH, at64, name)

        def co(name):
            return piece(CO, atc, name)

        def once(name):
            return piece(CS, ats, name)

        ident = co("ident")
        ident_bf = sb("ident_bf", [P, P], BF16)
        ident_h = sb("ident_h", [P, P], F16)
        tri_bf = sb("tri_bf", [P, P], BF16)
        ones_bf = sb("ones_bf", [P, P], BF16)
        lmask_bf = sb("lmask_bf", [P, 2, 224], BF16)
        WQ = sb("WQ", [64, 2, 256])
        WVO = sb("WVO", [P, 2, D])
        trig = sb("trig", [P, 2, 9, HALF])
        dl = sb("dl", [P, 8, HALF])
        Aneg = sb("Aneg", [P, 2, DS])
        dtb2 = sb("dtb2", [P, 2])
        one = sb("one", [P, 1])
        eps = sb("eps", [P, 1])
        cum = sb("cum", [P, NE2])
        cum_bf = sb("cum_bf", [P, NE2], BF16)
        X = sb("X", [P, NT, D])
        XT = sb("XT", [P, L])
        KI = sb("KI", [P, L])
        KT = sb("KT", [P, L])
        QI = sb("QI", [P, 2, L])
        CQ = sb("CQ", [64, L])
        table = sb("table", [P, NT, 64])
        tparts = sb("tparts", [P, NT, 3, 64], BF16)
        prev_c = sb("prev_c", [64, 3, DC])
        relu_s = sb("relu_s", [P, 2, 448])
        score = sb("score", [P, 2, 448])
        tres = score[:, :, :].rearrange("p a c -> p (a c)")[:, 0:512].rearrange("p (s n c) -> p s n c", s=2, n=NT)
        top = sb("top", [P, NREM])
        idx = sb("idx", [P, NREM], U32)
        idxT = sb("idxT", [P, NCOL], U32)
        idxh = sb("idxh", [P, NCOL], F16)
        q_e = sb("q_e", [P, 3, 256])
        kr_e = q_e[:, :, 0:NT * DR].rearrange("p s (n c) -> p s n c", n=NT)
        SR = sb("SR", [P, 8, 32])
        SRd = sb("SRd", [P, 8, 32])
        PR = sb("PR", [P, 8, 32])
        PT = sb("PT", [P, 8, 32])
        muq, qr_c, qr_s = SR, SRd, PT
        krot = PR[:, :, :].rearrange("p (s n) c -> p s n c", s=2)
        QA = sb("QA", [P, NH, 2, 32])
        QB = sb("QB", [P, NH, 2, 32])
        KD = QB[:, :, :, :].rearrange("p (n a) k c -> p n a (k c)", n=NT)
        QBT = sb("QBT", [P, 4, P])
        QT = sb("QT", [P, NH, 2, NCOL])
        QBD = sb("QBD", [P, NCOL, 2, 4, NH])
        ib = sb("ib", [P, 2, 4 * P], F16)
        onehot = sb("onehot", [P, 2, NT, 4 * P], BF16)
        QAT = onehot[:, 1, :, :].rearrange("p n c -> p (n c)").bitcast(F32)[:, 0:4 * P].rearrange("p (a c) -> p a c", a=4)
        G = sb("G", [P, NCOL, 64])
        g_c = sb("g_c", [P, 8, DR])
        g_s = sb("g_s", [P, 2, 8, DR])
        GR = sb("GR", [P, 8, DR])
        GT = sb("GT", [P, 2, NCOL, 32])
        PBD = sb("PBD", [P, 8, 4, 4, NH])
        RO = sb("RO", [P, 8, 34])
        RB = sb("RB", [P, NH, 34])
        PL = relu_s[:, :, :].rearrange("p a (b c) -> p (a b) c", b=2)
        PLT1 = sb("PLT1", [TOPK, 4, P])
        PLT2 = sb("PLT2", [P, 4, P])
        ml = sb("ml", [P, NH])
        nml = sb("nml", [P, NH])
        ll = sb("ll", [P, NH])
        mj = sb("mj", [P, NH])
        dm = sb("dm", [P, 2, NH])
        em = sb("em", [P, 2, NH])
        den = sb("den", [P, 4, NH])
        fac = sb("fac", [P, 2, NH])
        On = sb("On", [P, 2, NH, DC])
        OT = sb("OT", [P, 2, P])
        Y1 = sb("Y1", [P, NT, D])
        stats = sb("stats", [P, NT, 6])
        mv = sb("mv", [P, NT, 2])
        lnv = sb("lnv", [P, NT])
        rstd = sb("rstd", [P, NT])
        XR = sb("XR", [P, NT, D])
        XRT = sb("XRT", [P, L])
        Y2 = sb("Y2", [P, NT, D])
        r8 = sb("r8", [P, NT, 8])
        ri = sb("ri", [P, NT, 8], U32)
        rif = sb("rif", [P, NT, 8])
        rs = sb("rs", [P, 2, NT])
        CT = sb("CT", [NE, L])
        CB = big[:, :, :, :].rearrange("p k j t -> p (k j) t")
        SG = sb("SG", [P, 2, L])
        HT = sb("HT", [P, L])
        rt = HT[:, 0:6 * NT * NE].rearrange("p (k n e) -> p k n e", k=6, n=NT)
        req = SG[:, 1, 0:NT * NE * TOP_E].rearrange("p (n e k) -> p n e k", n=NT, e=NE)
        XP = sb("XP", [P, 2, L + DCONV - 1])
        SZ = sb("SZ", [P, 2, L])
        CV = sb("CV", [P, 2, L])
        U = sb("U", [P, 2, L])
        XD = sb("XD", [DTR + 2 * DS, L])
        DEL = sb("DEL", [P, 2, L])
        DU = sb("DU", [P, 2, L])
        dA, dBu = big[:, 0:2, :, :], big[:, 2:4, :, :]
        dt_x, dt_a, dt_b, dt_c = (big[:, k, :, :] for k in range(4))
        ez, eu = big[:, 0, :, :], big[:, 1, :, :]
        BC = sb("BC", [P, 2, 2, L])
        hs = SG
        hC = (XP[:, :, DCONV - 1:], CV)
        YG = CV
        pr = sb("pr", [P, 4, NT, NE2])
        ps1 = sb("ps1", [P, 3, NT])
        mk = sb("mk", [P, NT, NE2])
        mk_bf = sb("mk_bf", [P, NT, NE2], BF16)
        keep = sb("keep", [P, NT, NE2])
        gate = sb("gate", [P, NT, NE2])
        csum = sb("csum", [P, NE2])
        GTs = CT[0:NE2, :]
        OUT = CV[:, :, :].rearrange("p j t -> p (j t)")[:, 0:NT * D].rearrange("p (n d) -> p n d", n=NT)
        scr = nc.dram_tensor("rows_bounce", [2, P, NH * 34], F32, kind="Internal").ap()
        comb_rows = nc.dram_tensor("comb_rows", [NE, L], F32, kind="Internal").ap()
        bc_rows = nc.dram_tensor("bc_rows", [2 * DS, L], F32, kind="Internal").ap()

        s_load = semaphore("weights_loaded")
        set_v = Signal(semaphore("setup_vector"), SET_VEC)
        s_seta = semaphore("setup_scalar")
        s_setp = semaphore("setup_tensor")
        hold_dve, hold_pe = semaphore("hold_vector"), semaphore("hold_tensor")
        x_in = signal("x_in", 1, 16)
        attn_done = signal("attn_done", 1, first=1)
        rest_done = signal("rest_done", 1, first=1)
        out_stored = signal("out_stored", 1, 16, first=1)
        vec = signal("vector_step", PER["vec"])
        vec2 = signal("vector_step_rest", PER["vec2"])
        act_s = signal("scalar_step", PER["act"])
        act2 = signal("scalar_step_rest", PER["act2"])
        xt_ps = signal("xt_in_psum", 1)
        xt_sb = signal("xt_in_sbuf", 1)
        proj_ps = signal("proj_in_psum", 4)
        proj_sb = signal("proj_in_sbuf", 4)
        kv_ps = signal("kv_in_psum", 1)
        kr_sp = signal("kr_logs_ready", 1)
        kv_in = signal("kv_dup_ready", 1)
        kt_ps = signal("kt_in_psum", 1)
        kt_sb = signal("kt_in_sbuf", 1)
        parts_ok = signal("table_parts_ready", 1)
        ix_ps = signal("index_scores_in_psum", 4 * NT)
        ix_relu = signal("index_relu_ready", 4 * NT)
        ix_used = signal("index_relu_used", 4 * NT)
        q_ps = signal("q_in_psum", NT)
        q_sp = signal("q_logs_ready", NT)
        q_rows = signal("q_rows_ready", NT)
        qT_ps = signal("qt_in_psum", NT + 1)
        qT_sb = signal("qt_in_sbuf", NT + 1)
        idx_ok = signal("idx_columns_ready", NT)
        ib_ps = signal("idx_spread_in_psum", 8 * NT)
        ib_sb = signal("idx_spread_in_sbuf", 8 * NT)
        oh_ok = signal("onehot_round_ready", 8 * NT)
        g_round = signal("rows_round_in_psum", 8 * NT)
        g_sb = signal("rows_in_sbuf", 4 * NT)
        g_sin = signal("rows_sin_ready", 4 * NT)
        g_rot = signal("rows_turned", 4 * NT)
        gt_ok = signal("picked_keys_ready", NT)
        sr_ps = signal("picked_scores_in_psum", NT)
        sr_d = signal("picked_scores_shifted", NT)
        pr_ok = signal("picked_probs_ready", NT)
        pbd_ok = signal("picked_probs_spread", NT)
        ro_ps = signal("picked_out_in_psum", NT)
        ro_sb = signal("picked_out_in_sbuf", NT)
        ro_st = signal("picked_out_stored", 16 * NT, 16)
        rb_in = signal("picked_out_back", NT, 16)
        sl_ps = signal("local_scores_in_psum", 2 * NT)
        ml_ok = signal("local_max_ready", 2 * NT)
        pl_ok = signal("local_probs_ready", 2 * NT)
        pt_ps = signal("local_probs_t_in_psum", 2 * NT)
        pt_sb = signal("local_probs_t_in_sbuf", 2 * NT)
        ol_ps = signal("local_out_in_psum", 2 * NT)
        dm_ok = signal("max_gaps_ready", NT)
        em_ok = signal("merge_weights_ready", NT)
        on_ok = signal("attn_rows_ready", NT)
        oT_ps = signal("attn_t_in_psum", NT)
        oT_sb = signal("attn_t_in_sbuf", NT)
        at_ps = signal("attn_out_in_psum", NT)
        at_used = signal("attn_out_added", NT)
        var_ok = signal("variances_ready", 4)
        rstd_ok = signal("rstd_ready", 4)
        ln_ok = signal("normed_rows_ready", 2)
        rT_ps = signal("rest_xt_in_psum", 3)
        rT_sb = signal("rest_xt_in_sbuf", 3)
        rl_ps = signal("router_logits_in_psum", 2)
        rl_e = signal("router_exp_ready", 1)
        comb_ok = signal("comb_ready", 1)
        ct_ps = signal("comb_t_in_psum", 1)
        ct_sb = signal("comb_t_in_sbuf", 1)
        ct_st = signal("comb_stored", 1, 16)
        cb_sb = signal("comb_spread", 2, 16)
        gu_ps = signal("gate_up_in_psum", 9)
        sg_ok = signal("gate_exp_in_sbuf", 9)
        hu_ok = signal("hidden_ready", 9)
        ht_ok = signal("hidden_scaled", 8)
        y_part = signal("expert_out_part", 9)
        xz_ps = signal("xz_in_psum", 4)
        xz_sb = signal("xz_in_sbuf", 4)
        sz_ok = signal("z_gate_ready", 2)
        cv_ok = signal("conv_ready", 2)
        ue_ok = signal("u_exp_ready", 2)
        u_ok = signal("u_ready", 2)
        xd_ps = signal("xdbl_in_psum", 1)
        xd_sb = signal("xdbl_in_sbuf", 1)
        xd_st = signal("bc_rows_stored", 1, 16)
        dt_ps = signal("dt_in_psum", 2)
        dtx_ok = signal("dt_biased", 1)
        dt_sp = signal("dt_exp_ready", 1)
        del_ok = signal("delta_ready", 1)
        b_in = [signal(f"b_row_in_slot_{k}", DS // 2, 16) for k in range(2)]
        c_in = [signal(f"c_row_in_slot_{k}", DS // 2, 16) for k in range(2)]
        dA_ok = signal("decay_ready", 2 * DS)
        dBu_ok = signal("drive_ready", 2 * DS)
        scan_ok = signal("states_ready", 2 * DS)
        hC_ok = signal("readout_ready", 2 * DS)
        ysum = signal("readout_summed", 2 * DS)
        yg_ok = signal("gated_ready", 1)
        op_ps = signal("scan_out_in_psum", 1)
        pm_ok = signal("gate_shifted", 1)
        pe_ok = signal("gate_exp_ready", 1)
        mk_ok = signal("choice_ready", 1)
        loc_ps = signal("slots_in_psum", 1)
        gate_ok = signal("gates_ready", 1)
        gT_ps = signal("gates_t_in_psum", 1)
        gT_sb = signal("gates_t_in_sbuf", 1)
        bias_ps = signal("bias_in_psum", 1)
        e_ps = signal("top1_out_in_psum", NT)
        e_used = signal("top1_out_used", NT)

        def weave(first, second):
            live = [first, second]
            while live:
                for g in list(live):
                    if next(g, "end") == "end":
                        live.remove(g)

        def rows_loop(eng, attention, close, rest):
            weave(attention(0), iter(()))
            close(0)
            with eng.Fori(1, B) as b:
                weave(attention(b), rest(b - 1))
                close(b)
            weave(rest(B - 1), iter(()))

        block = ctx.enter_context(nc.Block())

        @block.sync
        def _(sp):
            def attention(b):
                sp.wait_ge(attn_done.sem, attn_done.at(b, 0))
                sp.dma_start(X[:, :, :], x[b].rearrange("(n p) d -> p n d", p=P)).then_inc(x_in.sem, x_in.up())
                for _ in range(KEY_PHASES):
                    yield
                for i in range(NT):
                    for _ in range(TILE_PHASES - 1):
                        yield
                    sp.wait_ge(ro_sb.sem, ro_sb.at(b, i + 1))
                    to = scr[i % 2].rearrange("(b x a) (h e) -> a b h x e", b=4, a=4, h=NH)
                    for a in range(4):
                        for bb in range(4):
                            p0 = 32 * a + 8 * bb
                            sp.dma_start(to[a, bb], RO[p0:p0 + 8, :, :]).then_inc(ro_st.sem, ro_st.up())
                    sp.wait_ge(ro_st.sem, ro_st.at(b, 16 * (i + 1)))
                    if i >= 1:
                        sp.wait_ge(on_ok.sem, on_ok.at(b, i))
                    sp.dma_start(RB[:, :, :].rearrange("p h e -> p (h e)"), scr[i % 2]).then_inc(rb_in.sem, rb_in.up())
                    yield
                for _ in range(MERGE_PHASES):
                    yield

            def close(b):
                pass

            def rest(b):
                sp.wait_ge(rest_done.sem, rest_done.at(b, 0))
                for _ in range(ROUTE_PHASES - 1):
                    yield
                sp.wait_ge(ct_sb.sem, ct_sb.at(b, 1))
                sp.dma_start(comb_rows, CT[:, :]).then_inc(ct_st.sem, ct_st.up())
                sp.wait_ge(ct_st.sem, ct_st.at(b, 1))
                for e in range(2):
                    src = comb_rows.rearrange("(p e) t -> e p t", e=2)[e].unsqueeze(0).to_broadcast([64, NE // 2, L])
                    sp.dma_start(CB[64 * e:64 * e + 64, :, :], src).then_inc(cb_sb.sem, cb_sb.up())
                yield
                for _ in range(EXPERT_PHASES + NORM_PHASES + SCAN_IN_PHASES - 3):
                    yield
                sp.wait_ge(xd_sb.sem, xd_sb.at(b, 1))
                sp.dma_start(bc_rows, XD[DTR:DTR + 2 * DS, :]).then_inc(xd_st.sem, xd_st.up())
                sp.wait_ge(xd_st.sem, xd_st.at(b, 1))
                for n in range(DS):
                    if n == 2:
                        yield
                        yield
                        yield
                    if n >= 2:
                        sp.wait_ge(dBu_ok.sem, dBu_ok.at(b, 2 * (n - 1)))
                        sp.wait_ge(hC_ok.sem, hC_ok.at(b, 2 * (n - 1)))
                    for k in range(2):
                        src = bc_rows[k * DS + n:k * DS + n + 1, :].to_broadcast([P, L])
                        row_in = (b_in, c_in)[k][n % 2]
                        sp.dma_start(BC[:, n % 2, k, :], src).then_inc(row_in.sem, row_in.up())
                    if n >= 2:
                        yield
                for _ in range(2 + SCAN_OUT_PHASES + NORM_PHASES + TOP1_PHASES):
                    yield
                sp.wait_ge(rest_done.sem, rest_done.at(b, 1))
                sp.dma_start(out[b].rearrange("(n p) d -> p n d", p=P), OUT).then_inc(out_stored.sem, out_stored.up())

            sp.dma_start(CO[:, :], consts).then_inc(s_load, 16)
            sp.dma_start(CS, setup_c).then_inc(s_load, 16)
            sp.dma_start(W[:, :], w128).then_inc(s_load, 16)
            sp.dma_start(WH, w64).then_inc(s_load, 16)
            sp.sem_inc(out_stored.sem, 16)
            rows_loop(sp, attention, close, rest)
            sp.wait_ge(out_stored.sem, 16 * (B + 1))

        @block.tensor
        def _(pe):
            mm = pe.matmul

            def turn(o, i_, k=P):
                return pe.transpose(o, i_, ident[0:k, 0:k])

            def merge(b, i, step):
                if step == 1:
                    pe.wait_ge(on_ok.sem, on_ok.at(b, i + 1))
                    pe.sem_inc(hold_pe, 1)
                    for k in range(2):
                        m = turn(bank[4][:, 256 + k * P:256 + (k + 1) * P],
                                 On[:, 0, 4 * k:4 * k + 4, :].rearrange("p h c -> p (h c)"))
                    m.then_inc(oT_ps.sem, oT_ps.up())
                    pe.wait_ge(oT_sb.sem, oT_sb.at(b, i + 1))
                    for k in range(2):
                        m = mm(bank[4][:, 0:P], OT[:, k, :], WVO[:, k, :], start=(k == 0), stop=(k == 1))
                    m.then_inc(at_ps.sem, at_ps.up())

            def attention(b):

                pe.wait_ge(attn_done.sem, attn_done.at(b, 0))
                pe.wait_ge(x_in.sem, x_in.at(b, 1))
                pe.sem_inc(hold_pe, 1)
                for i in range(NT):
                    m = turn(bank[0][:, i * P:(i + 1) * P], X[:, i, :])
                m.then_inc(xt_ps.sem, xt_ps.up())
                yield
                pe.wait_ge(xt_sb.sem, xt_sb.at(b, 1))
                mm(bank[1][:, :], w("wk2"), XT[:, :], start=True, stop=True).then_inc(proj_ps.sem, proj_ps.up())
                mm(bank[2][:, :], w("wq")[:, 0:P], XT[:, :], start=True, stop=True).then_inc(proj_ps.sem, proj_ps.up())
                mm(bank[3][:, :], w("wq")[:, P:2 * P], XT[:, :], start=True, stop=True).then_inc(proj_ps.sem, proj_ps.up())
                mm(bank[4][0:64, :], w("dq"), XT[:, :], start=True, stop=True).then_inc(proj_ps.sem, proj_ps.up())
                for i in range(NT):
                    mm(bank[0][:, i * 64:(i + 1) * 64], XT[:, i * P:(i + 1) * P], w("kv"), start=True, stop=True)
                for i in range(1, NT):
                    m = mm(bank[0][0:64, 256 + 32 * i:288 + 32 * i], XT[:, i * P - 64:i * P], w("kv")[:, 0:DC],
                           start=True, stop=True)
                m.then_inc(kv_ps.sem, kv_ps.up())
                yield
                pe.wait_ge(kv_in.sem, kv_in.at(b, 1))
                pe.wait_ge(proj_sb.sem, proj_sb.at(b, 4))
                pe.sem_inc(hold_pe, 1)
                for i in range(NT):
                    m = turn(bank[1][:, i * P:(i + 1) * P], KD[:, i, :, :].rearrange("p a c -> p (a c)"))
                m.then_inc(kt_ps.sem, kt_ps.up())
                yield

                for i in range(NT):
                    Wi, W0 = index_width(i), first_width(i)
                    c0 = 96 - W0
                    if i == 0:
                        pe.wait_ge(kt_sb.sem, kt_sb.at(b, 1))
                    else:
                        pe.wait_ge(ro_sb.sem, ro_sb.at(b, i))
                        pe.wait_ge(g_sb.sem, g_sb.at(b, 4 * i))
                    for h in range(NIH):
                        o = 64 * (h % 2)
                        mm(bank[h][:, 0:Wi], QI[o:o + 64, h // 2, i * P:(i + 1) * P], KI[o:o + 64, 0:Wi],
                                      start=True, stop=True).then_inc(ix_ps.sem, ix_ps.up())
                    pe.wait_ge(ix_relu.sem, ix_relu.at(b, 4 * i + 1))
                    mm(bank[0][:, :], CQ[:, i * P:(i + 1) * P], WQ[:, :, :].rearrange("p a c -> p (a c)"),
                                 start=True, stop=True).then_inc(q_ps.sem, q_ps.up())
                    yield
                    yield
                    if i >= 1:
                        merge(b, i - 1, 1)
                    yield
                    pe.wait_ge(q_rows.sem, q_rows.at(b, i + 1))
                    pe.wait_ge(ix_relu.sem, ix_relu.at(b, 4 * i + 4))
                    pe.sem_inc(hold_pe, 1)
                    for p in range(4):
                        m = turn(bank[2][:, p * P:(p + 1) * P],
                                 QB[:, 2 * p:2 * p + 2, :, :].rearrange("p h k c -> p (h k c)"))
                    m.then_inc(qT_ps.sem, qT_ps.up())
                    if i == 0:
                        for p in range(4):
                            m = turn(bank[3][:, p * P:(p + 1) * P],
                                     QA[:, 2 * p:2 * p + 2, :, :].rearrange("p h k c -> p (h k c)"))
                        m.then_inc(qT_ps.sem, qT_ps.up())
                    yield

                    def local_scores(g):
                        for hh in range(4):
                            h = 4 * g + hh
                            o = 64 * (h % 2)
                            sc = bank[2 + hh % 2][:, 256 * (hh // 2):256 * (hh // 2) + 224]
                            mm(sc[:, c0:224], ident_bf[:, :], lmask_bf[:, min(i, 1), c0:224], start=True, stop=False)
                            if i == 0:
                                mm(sc[:, 0:96], QAT[o:o + 64, h // 2, :], KT[o:o + 64, 0:96], start=False, stop=True)
                                m = mm(sc[:, 96:224], QBT[o:o + 64, h // 2, :], KT[o:o + 64, 0:P],
                                       start=False, stop=True, skip_group_check=True)
                            else:
                                m = mm(sc[:, c0:224], QBT[o:o + 64, h // 2, :], KT[o:o + 64, i * P - 64:(i + 1) * P],
                                       start=False, stop=True)
                        m.then_inc(sl_ps.sem, sl_ps.up())

                    def local_turn(g):
                        pe.wait_ge(pl_ok.sem, pl_ok.at(b, 2 * i + g + 1))
                        if g == 1:
                            pe.wait_ge(pt_sb.sem, pt_sb.at(b, 2 * i + 1))
                        pe.sem_inc(hold_pe, 1)
                        for hh in range(4):
                            turn(bank[0][0:W0, hh * P:(hh + 1) * P], PL[:, hh, c0:96])
                        for hh in range(4):
                            m = turn(bank[1][:, hh * P:(hh + 1) * P], PL[:, hh, 96:224])
                        m.then_inc(pt_ps.sem, pt_ps.up())

                    def local_out(g):
                        pe.wait_ge(pt_sb.sem, pt_sb.at(b, 2 * i + g + 1))
                        if g == 0 and i >= 1:
                            pe.wait_ge(at_used.sem, at_used.at(b, i))
                        pe.sem_inc(hold_pe, 1)
                        for hh in range(4):
                            h = 4 * g + hh
                            first = table[0:W0, 0, 0:DC] if i == 0 else prev_c[:, i - 1, :]
                            mm(bank[4][:, h * DC:(h + 1) * DC], PLT1[0:W0, hh, :], first, start=True, stop=False)
                            m = mm(bank[4][:, h * DC:(h + 1) * DC], PLT2[:, hh, :], table[:, i, 0:DC],
                                   start=False, stop=True)
                        m.then_inc(ol_ps.sem, ol_ps.up())

                    pe.wait_ge(qT_sb.sem, qT_sb.at(b, i + 2))
                    local_scores(0)
                    yield
                    local_turn(0)
                    local_scores(1)
                    yield
                    local_out(0)
                    local_turn(1)
                    yield

                    def spread(r):
                        if r < 2:
                            pe.wait_ge(pt_sb.sem, pt_sb.at(b, 2 * i + 2))
                            pe.wait_ge(idx_ok.sem, idx_ok.at(b, i + 1))
                        else:
                            pe.wait_ge(ib_sb.sem, ib_sb.at(b, 8 * i + r - 1))
                        for q in range(4):
                            t = 4 * r + q
                            m = mm(bank[r % 2][:, q * P:(q + 1) * P], idxh[:, t:t + 1].to_broadcast([P, P]),
                                   ident_h[:, :], start=True, stop=True)
                        m.then_inc(ib_ps.sem, ib_ps.up())

                    def pick(r):
                        c = r // 2
                        pe.wait_ge(oh_ok.sem, oh_ok.at(b, 8 * i + r + 1))
                        if r % 2 == 0:
                            if c >= 2:
                                pe.wait_ge(g_sb.sem, g_sb.at(b, 4 * i + c - 1))
                            else:
                                pe.wait_ge(pl_ok.sem, pl_ok.at(b, 2 * i + 2))
                        for q in range(4):
                            for kt in range(i + 1):
                                kk = 64 if kt == i else P
                                for part in range(3):
                                    m = mm(bank[2 + c % 2][:, (4 * (r % 2) + q) * 64:(4 * (r % 2) + q + 1) * 64],
                                           onehot[0:kk, r % 2, kt, q * P:(q + 1) * P],
                                           tparts[0:kk, kt, part, :], start=(kt == 0 and part == 0),
                                           stop=(kt == i and part == 2))
                        m.then_inc(g_round.sem, g_round.up())

                    local_out(1)
                    spread(0)
                    spread(1)
                    yield
                    if i == 0:
                        pe.wait_ge(parts_ok.sem, parts_ok.at(b, 1))
                    for c in range(4):
                        pick(2 * c)
                        if c < 3:
                            spread(2 * c + 2)
                        pick(2 * c + 1)
                        if c < 3:
                            spread(2 * c + 3)
                        yield
                    pe.wait_ge(gt_ok.sem, gt_ok.at(b, i + 1))
                    pe.wait_ge(ib_sb.sem, ib_sb.at(b, 8 * i + 8))
                    pe.sem_inc(hold_pe, 1)
                    for t in range(NCOL):
                        xx, a = t // 4, t % 4
                        for kind in range(2):
                            m = mm(bank[0][32 * a:32 * a + 32, 32 * xx:32 * xx + 32],
                                   QBD[:, t, kind, :, :].rearrange("p b h -> p (b h)"), GT[:, kind, t, :],
                                   start=(kind == 0), stop=(kind == 1))
                    m.then_inc(sr_ps.sem, sr_ps.up())
                    yield
                    yield
                    pe.wait_ge(pbd_ok.sem, pbd_ok.at(b, i + 1))
                    pe.sem_inc(hold_pe, 1)
                    for t in range(NCOL):
                        xx, a = t // 4, t % 4
                        m = mm(bank[1][32 * a:32 * a + 32, 32 * xx:32 * xx + 32],
                               PBD[:, xx, a, :, :].rearrange("p b h -> p (b h)"), G[:, t, 0:DC], start=True, stop=True)
                    m.then_inc(ro_ps.sem, ro_ps.up())
                    yield
                yield
                merge(b, NT - 1, 1)
                yield

            def close(b):
                pass

            def turn_rows(b, k):
                if k > 1:
                    pe.wait_ge(ln_ok.sem, ln_ok.at(b, k - 1))
                else:
                    pe.wait_ge(attn_done.sem, attn_done.at(b, 1))
                pe.sem_inc(hold_pe, 1)
                for i in range(NT):
                    m = turn(bank[5][:, i * P:(i + 1) * P], XR[:, i, :])
                m.then_inc(rT_ps.sem, rT_ps.up())

            def rest(b):

                pe.wait_ge(rest_done.sem, rest_done.at(b, 0))
                turn_rows(b, 1)
                pe.wait_ge(rT_sb.sem, rT_sb.at(b, 1))
                for i in range(NT):
                    m = mm(bank[7][:, i * NE:(i + 1) * NE], XRT[:, i * P:(i + 1) * P], w("gate"), start=True, stop=True)
                m.then_inc(rl_ps.sem, rl_ps.up())
                yield
                yield
                pe.wait_ge(comb_ok.sem, comb_ok.at(b, 1))
                pe.sem_inc(hold_pe, 1)
                for i in range(NT):
                    m = turn(bank[7][0:NE, i * P:(i + 1) * P], rt[:, 5, i, :])
                m.then_inc(ct_ps.sem, ct_ps.up())
                yield

                def second(p):
                    free = ht_ok if p < 8 else hu_ok
                    pe.wait_ge(free.sem, free.at(b, p + 1))
                    kk = P if p < 8 else 64
                    wt = w("w2")[:, p, :] if p < 8 else w("w2s")[0:64, :]
                    pe.sem_inc(hold_pe, 1)
                    for i in range(NT):
                        m = mm(bank[7][:, i * P:(i + 1) * P], HT[0:kk, i * P:(i + 1) * P], wt,
                               start=(p == 0 and i == 0), stop=(p == 8), skip_group_check=True)
                    m.then_inc(y_part.sem, y_part.up())

                for p in range(9):
                    pe.wait_ge(ct_sb.sem, ct_sb.at(b, 1))
                    if p >= 1:
                        pe.wait_ge(hu_ok.sem, hu_ok.at(b, p))
                    rows = P if p < 8 else 64
                    wg = w("w1g")[:, p, :] if p < 8 else w("w1sg")
                    wu = w("w1u")[:, p, :] if p < 8 else w("w1su")
                    mm(bank[5][0:rows, :], wg, XRT[:, :], start=True, stop=True)
                    mm(bank[6][0:rows, :], wu, XRT[:, :], start=True, stop=True).then_inc(gu_ps.sem, gu_ps.up())
                    yield
                    if p >= 1:
                        second(p - 1)
                yield
                second(8)
                yield
                yield

                turn_rows(b, 2)
                yield
                pe.wait_ge(rT_sb.sem, rT_sb.at(b, 2))
                for k in range(2):
                    mm(bank[5 + k][:, :], w("inp")[:, k * P:(k + 1) * P], XRT[:, :], start=True, stop=True).then_inc(xz_ps.sem, xz_ps.up())
                yield
                for k in range(2, 4):
                    pe.wait_ge(xz_sb.sem, xz_sb.at(b, k - 1))
                    mm(bank[3 + k][:, :], w("inp")[:, k * P:(k + 1) * P], XRT[:, :], start=True, stop=True).then_inc(xz_ps.sem, xz_ps.up())
                yield
                yield
                yield
                pe.wait_ge(u_ok.sem, u_ok.at(b, 2))
                pe.sem_inc(hold_pe, 1)
                for j in range(2):
                    m = mm(bank[7][0:40, :], w("xp")[:, j, :], U[:, j, :], start=(j == 0), stop=(j == 1))
                m.then_inc(xd_ps.sem, xd_ps.up())
                pe.wait_ge(xd_sb.sem, xd_sb.at(b, 1))
                pe.wait_ge(sz_ok.sem, sz_ok.at(b, 2))
                pe.sem_inc(hold_pe, 1)
                for j in range(2):
                    mm(bank[5 + j][:, :], w("dtw")[0:DTR, j * P:(j + 1) * P], XD[0:DTR, :], start=True, stop=True).then_inc(dt_ps.sem, dt_ps.up())
                yield
                yield
                yield
                for n in range(DS + 1):
                    if n == 1:
                        pe.wait_ge(dtx_ok.sem, dtx_ok.at(b, 1))
                    if n >= 1:
                        for j in range(2):
                            pe.wait_ge(hC_ok.sem, hC_ok.at(b, 2 * (n - 1) + j + 1))
                            mm(bank[5 + j][:, :], ident, hC[(n - 1) % 2][:, j, :], start=(n == 1), stop=(n == DS)).then_inc(ysum.sem, ysum.up())
                    if n < DS:
                        yield
                yield
                pe.wait_ge(yg_ok.sem, yg_ok.at(b, 1))
                for i in range(NT):
                    for j in range(2):
                        m = mm(bank[7][:, i * P:(i + 1) * P], YG[:, j, i * P:(i + 1) * P], w("op")[:, j, :],
                               start=(j == 0), stop=(j == 1))
                m.then_inc(op_ps.sem, op_ps.up())
                yield
                yield

                turn_rows(b, 3)
                pe.wait_ge(rT_sb.sem, rT_sb.at(b, 3))
                for i in range(NT):
                    m = mm(bank[7][:, i * NE2:(i + 1) * NE2], XRT[:, i * P:(i + 1) * P], w("wg"), start=True, stop=True)
                m.then_inc(rl_ps.sem, rl_ps.up())
                yield
                yield
                pe.wait_ge(mk_ok.sem, mk_ok.at(b, 1))
                for i in range(NT):
                    o = bank[7][:, 64 + i * NE2:64 + (i + 1) * NE2]
                    mm(o, tri_bf[:, :], mk_bf[:, i, :], start=True, stop=False)
                    for k in range(i):
                        mm(o, ones_bf[:, :], mk_bf[:, k, :], start=False, stop=False)
                    m = mm(o, ones_bf[:, :], cum_bf[:, :], start=False, stop=True)
                m.then_inc(loc_ps.sem, loc_ps.up())
                yield
                pe.wait_ge(gate_ok.sem, gate_ok.at(b, 1))
                pe.sem_inc(hold_pe, 1)
                for i in range(NT):
                    m = turn(bank[5][0:NE2, i * P:(i + 1) * P], gate[:, i, :])
                m.then_inc(gT_ps.sem, gT_ps.up())
                yield
                pe.wait_ge(gT_sb.sem, gT_sb.at(b, 1))
                pe.sem_inc(hold_pe, 1)
                for i in range(NT):
                    m = mm(bank[7][:, i * P:(i + 1) * P], GTs[:, i * P:(i + 1) * P], w("eb")[0:NE2, :], start=True, stop=True)
                m.then_inc(bias_ps.sem, bias_ps.up())
                for i in range(NT):
                    if i >= 1:
                        pe.wait_ge(e_used.sem, e_used.at(b, i))
                    for k in range(2):
                        m = mm(bank[5 + k][:, :], XRT[:, i * P:(i + 1) * P], w("ew")[:, k * 512:(k + 1) * 512],
                               start=True, stop=True)
                    m.then_inc(e_ps.sem, e_ps.up())
                    yield
                yield
                yield

            pe.wait_ge(s_load, 64)
            for h in range(NH):
                m = mm(bank[0][0:64, h * DC:(h + 1) * DC], wh("uqT")[:, h, :], wh("ukT")[:, h, :],
                       start=True, stop=True)
            m.then_inc(s_setp, 1)
            for h in range(NH):
                m = mm(bank[1][32 * (h % 4):32 * (h % 4) + 32, (h // 4) * D:(h // 4 + 1) * D],
                       wh("uvT")[:, h, :], wh("out")[:, h, :], start=True, stop=True)
            m.then_inc(s_setp, 1)
            pe.wait_ge(set_v.sem, SET_VEC)
            pe.wait_ge(s_seta, 3)
            rows_loop(pe, attention, close, rest)

        @block.scalar
        def _(act):
            A = act.activation

            def attention(b):

                def softplus_logs(src, steps, done):
                    A(steps[0], src, ACT.Abs).then_inc(act_s.sem, act_s.up())
                    act.wait_ge(act_s.sem, act_s.now(b))
                    A(steps[1], steps[0], ACT.Exp, scale=-1.0).then_inc(act_s.sem, act_s.up())
                    act.wait_ge(act_s.sem, act_s.now(b))
                    A(steps[2], steps[1], ACT.Ln, bias=one[:, :]).then_inc(done.sem, done.up())

                act.wait_ge(attn_done.sem, attn_done.at(b, 0))
                act.wait_ge(xt_ps.sem, xt_ps.at(b, 1))
                A(XT[:, :], bank[0][:, :], ACT.Copy).then_inc(xt_sb.sem, xt_sb.up())
                yield
                for k, dst in enumerate((KI[:, :], QI[:, 0, :], QI[:, 1, :], CQ[:, :])):
                    act.wait_ge(proj_ps.sem, proj_ps.at(b, k + 1))
                    src = bank[1 + k][0:64, :] if k == 3 else bank[1 + k][:, :]
                    A(dst, src, ACT.Copy).then_inc(proj_sb.sem, proj_sb.up())
                act.wait_ge(kv_ps.sem, kv_ps.at(b, 1))
                kr = bank[0][:, 0:256].rearrange("p (n c) -> p n c", n=NT)[:, :, 32:64]
                softplus_logs(kr, [kr_e[:, s, :, :] for s in range(3)], kr_sp)
                yield
                act.wait_ge(kt_ps.sem, kt_ps.at(b, 1))
                A(KT[:, :], bank[1][:, :], ACT.Copy).then_inc(kt_sb.sem, kt_sb.up())
                yield

                for i in range(NT):
                    Wi, W0 = index_width(i), first_width(i)
                    c0 = 96 - W0
                    for h in range(NIH):
                        act.wait_ge(ix_ps.sem, ix_ps.at(b, 4 * i + h + 1))
                        if 4 * i + h >= 2:
                            act.wait_ge(ix_used.sem, ix_used.at(b, 4 * i + h - 1))
                        A(relu_s[:, h % 2, 0:Wi], bank[h][:, 0:Wi], ACT.Relu).then_inc(ix_relu.sem, ix_relu.up())
                    act.wait_ge(q_ps.sem, q_ps.at(b, i + 1))
                    if i >= 1:
                        act.wait_ge(q_rows.sem, q_rows.at(b, i))
                    softplus_logs(bank[0][:, 0:256], [q_e[:, s, :] for s in range(3)], q_sp)
                    yield
                    if i >= 1:
                        act.wait_ge(dm_ok.sem, dm_ok.at(b, i))
                        A(em[:, :, :], dm[:, :, :], ACT.Exp, scale=SCALE).then_inc(em_ok.sem, em_ok.up())
                    yield
                    if i >= 1:
                        act.wait_ge(oT_ps.sem, oT_ps.at(b, i))
                        A(OT[:, :, :].rearrange("p a c -> p (a c)"), bank[4][:, 256:512], ACT.Copy).then_inc(oT_sb.sem, oT_sb.up())
                    yield
                    act.wait_ge(qT_ps.sem, qT_ps.at(b, 1 if i == 0 else i + 2))
                    A(QBT[:, :, :].rearrange("p a c -> p (a c)"), bank[2][:, :], ACT.Copy).then_inc(qT_sb.sem, qT_sb.up())
                    if i == 0:
                        act.wait_ge(qT_ps.sem, qT_ps.at(b, 2))
                        A(QAT[:, :, :].rearrange("p a c -> p (a c)"), bank[3][:, :], ACT.Copy).then_inc(qT_sb.sem, qT_sb.up())
                    yield

                    def local_probs(g):
                        act.wait_ge(ml_ok.sem, ml_ok.at(b, 2 * i + g + 1))
                        if g == 1:
                            act.wait_ge(pt_ps.sem, pt_ps.at(b, 2 * i + 1))
                        for hh in range(4):
                            h = 4 * g + hh
                            sc = bank[2 + hh % 2][:, 256 * (hh // 2) + c0:256 * (hh // 2) + 224]
                            m = A(PL[:, hh, c0:224], sc, ACT.Exp, scale=SCALE, bias=nml[:, h:h + 1],
                                  accum_out=ll[:, h:h + 1])
                        m.then_inc(pl_ok.sem, pl_ok.up())

                    def local_keys(g):
                        act.wait_ge(pt_ps.sem, pt_ps.at(b, 2 * i + g + 1))
                        if g == 0 and i >= 1:
                            act.wait_ge(ol_ps.sem, ol_ps.at(b, 2 * i))
                        if g == 1:
                            act.wait_ge(ol_ps.sem, ol_ps.at(b, 2 * i + 1))
                        A(PLT1[0:W0, :, :].rearrange("p a c -> p (a c)"), bank[0][0:W0, :], ACT.Copy)
                        A(PLT2[:, :, :].rearrange("p a c -> p (a c)"), bank[1][:, :], ACT.Copy).then_inc(pt_sb.sem, pt_sb.up())

                    local_probs(0)
                    yield
                    local_keys(0)
                    local_probs(1)
                    yield
                    local_keys(1)
                    yield

                    def spread(r):
                        act.wait_ge(ib_ps.sem, ib_ps.at(b, 8 * i + r + 1))
                        if r >= 2:
                            act.wait_ge(oh_ok.sem, oh_ok.at(b, 8 * i + r - 1))
                        A(ib[:, r % 2, :], bank[r % 2][:, :], ACT.Copy).then_inc(ib_sb.sem, ib_sb.up())

                    spread(0)
                    spread(1)
                    yield
                    for c in range(4):
                        if c < 3:
                            spread(2 * c + 2)
                            spread(2 * c + 3)
                        act.wait_ge(g_round.sem, g_round.at(b, 8 * i + 2 * c + 2))
                        if i >= 1 and c == 0:
                            act.wait_ge(ro_ps.sem, ro_ps.at(b, i))
                        A(G[:, 8 * c:8 * c + 8, :].rearrange("p a c -> p (a c)"), bank[2 + c % 2][:, :], ACT.Copy).then_inc(g_sb.sem, g_sb.up())
                        yield
                    yield
                    act.wait_ge(sr_d.sem, sr_d.at(b, i + 1))
                    A(PR[:, :, :], SRd[:, :, :], ACT.Exp, scale=SCALE).then_inc(pr_ok.sem, pr_ok.up())
                    yield
                    act.wait_ge(ro_ps.sem, ro_ps.at(b, i + 1))
                    if i >= 1:
                        act.wait_ge(ro_st.sem, ro_st.at(b, 16 * i))
                    A(RO[:, :, 0:DC], bank[1][:, 0:256].rearrange("p (x c) -> p x c", x=8), ACT.Copy).then_inc(ro_sb.sem, ro_sb.up())
                    yield
                act.wait_ge(dm_ok.sem, dm_ok.at(b, NT))
                A(em[:, :, :], dm[:, :, :], ACT.Exp, scale=SCALE).then_inc(em_ok.sem, em_ok.up())
                yield
                act.wait_ge(oT_ps.sem, oT_ps.at(b, NT))
                A(OT[:, :, :].rearrange("p a c -> p (a c)"), bank[4][:, 256:512], ACT.Copy).then_inc(oT_sb.sem, oT_sb.up())
                yield

            def norm_scale(b, k):
                act.wait_ge(var_ok.sem, var_ok.at(b, k))
                A(lnv[:, :], mv[:, :, 1], ACT.Ln, bias=eps[:, :]).then_inc(act2.sem, act2.up())
                act.wait_ge(act2.sem, act2.at(b, act2.k))
                A(rstd[:, :], lnv[:, :], ACT.Exp, scale=-0.5).then_inc(rstd_ok.sem, rstd_ok.up())

            def close(b):
                norm_scale(b, 1)

            def rest(b):

                act.wait_ge(rest_done.sem, rest_done.at(b, 0))
                act.wait_ge(rT_ps.sem, rT_ps.at(b, 1))
                A(XRT[:, :], bank[5][:, :], ACT.Copy).then_inc(rT_sb.sem, rT_sb.up())
                act.wait_ge(rl_ps.sem, rl_ps.at(b, 1))
                A(rt[:, 0, :, :], bank[7][:, 0:NT * NE].rearrange("p (n e) -> p n e", n=NT), ACT.Exp, scale=-1.0).then_inc(rl_e.sem, rl_e.up())
                yield
                yield
                act.wait_ge(ct_ps.sem, ct_ps.at(b, 1))
                A(CT[:, :], bank[7][0:NE, :], ACT.Copy).then_inc(ct_sb.sem, ct_sb.up())
                yield
                for p in range(9):
                    rows = P if p < 8 else 64
                    act.wait_ge(gu_ps.sem, gu_ps.at(b, p + 1))
                    A(SG[0:rows, 0, :], bank[5][0:rows, :], ACT.Exp, scale=-1.0).then_inc(sg_ok.sem, sg_ok.up())
                    yield
                yield
                norm_scale(b, 2)
                yield
                yield

                act.wait_ge(rT_ps.sem, rT_ps.at(b, 2))
                A(XRT[:, :], bank[5][:, :], ACT.Copy).then_inc(rT_sb.sem, rT_sb.up())
                yield
                for k in range(2):
                    act.wait_ge(xz_ps.sem, xz_ps.at(b, k + 1))
                    A(XP[:, k, DCONV - 1:], bank[5 + k][:, :], ACT.Copy).then_inc(xz_sb.sem, xz_sb.up())
                yield
                for k in range(2):
                    act.wait_ge(xz_ps.sem, xz_ps.at(b, k + 3))
                    A(ez[:, k, :], bank[5 + k][:, :], ACT.Exp, scale=-1.0).then_inc(xz_sb.sem, xz_sb.up())
                yield
                for j in range(2):
                    act.wait_ge(cv_ok.sem, cv_ok.at(b, j + 1))
                    A(eu[:, j, :], CV[:, j, :], ACT.Exp, scale=-1.0).then_inc(ue_ok.sem, ue_ok.up())
                yield
                yield
                act.wait_ge(xd_ps.sem, xd_ps.at(b, 1))
                A(XD[:, :], bank[7][0:40, :], ACT.Copy).then_inc(xd_sb.sem, xd_sb.up())
                yield
                act.wait_ge(dtx_ok.sem, dtx_ok.at(b, 1))
                A(dt_a, dt_x, ACT.Abs).then_inc(act2.sem, act2.up())
                act.wait_ge(act2.sem, act2.at(b, act2.k))
                A(dt_b, dt_a, ACT.Exp, scale=-1.0).then_inc(dt_sp.sem, dt_sp.up())
                yield
                yield
                act.wait_ge(del_ok.sem, del_ok.at(b, 1))
                for n in range(DS):
                    for j in range(2):
                        if n >= 2:
                            act.wait_ge(scan_ok.sem, scan_ok.at(b, 2 * (n - 2) + j + 1))
                        A(dA[:, n % 2, j, :], DEL[:, j, :], ACT.Exp, scale=Aneg[:, j, n:n + 1]).then_inc(dA_ok.sem, dA_ok.up())
                    yield
                yield
                norm_scale(b, 3)
                yield
                yield

                act.wait_ge(rT_ps.sem, rT_ps.at(b, 3))
                A(XRT[:, :], bank[5][:, :], ACT.Copy).then_inc(rT_sb.sem, rT_sb.up())
                yield
                act.wait_ge(pm_ok.sem, pm_ok.at(b, 1))
                A(pr[:, 1, :, :], pr[:, 0, :, :], ACT.Exp).then_inc(pe_ok.sem, pe_ok.up())
                yield
                yield
                act.wait_ge(gT_ps.sem, gT_ps.at(b, 1))
                A(GTs[:, :], bank[5][0:NE2, :], ACT.Copy).then_inc(gT_sb.sem, gT_sb.up())
                yield
                for i in range(NT):
                    yield
                norm_scale(b, 4)
                yield
                yield

            act.wait_ge(s_load, 64)
            A(dl[:, 0, :], w("rawd"), ACT.Exp, scale=-1.0).then_inc(s_seta, 1)
            A(Aneg[:, :, :].rearrange("p a c -> p (a c)"), w("alog").rearrange("p a c -> p (a c)"),
              ACT.Exp).then_inc(s_seta, 1)
            act.wait_ge(set_v.sem, SET_SIN)
            A(dl[:, 4, :], dl[:, 3, :], ACT.Sin)
            A(dl[:, 5, :], dl[:, 3, :], ACT.Sin, scale=0.5).then_inc(s_seta, 1)
            act.wait_ge(set_v.sem, SET_VEC)
            act.preload_act_table_set("natural_log_exp_and_others")
            weave(attention(0), iter(()))
            close(0)
            with act.Fori(1, B) as b:
                act.preload_act_table_set("natural_log_exp_and_others")
                weave(attention(b), rest(b - 1))
                close(b)
            act.preload_act_table_set("natural_log_exp_and_others")
            weave(rest(B - 1), iter(()))

        @block.gpsimd
        def _(pool):
            def attention(b):

                pool.wait_ge(attn_done.sem, attn_done.at(b, 0))
                for _ in range(KEY_PHASES):
                    yield
                for i in range(NT):
                    for _ in range(8):
                        yield
                    for c in range(4):
                        pool.wait_ge(g_sb.sem, g_sb.at(b, 4 * i + c + 1))
                        if 4 * i + c >= 2:
                            pool.wait_ge(g_rot.sem, g_rot.at(b, 4 * i + c - 1))
                        sn = trig[:, 1, 8, :].unsqueeze(1).to_broadcast([P, 8, HALF])
                        part = G[:, 8 * c:8 * c + 8, :]
                        pool.tensor_tensor(g_s[:, c % 2, :, 0:HALF], part[:, :, DC:DC + HALF], sn, ALU.mult)
                        pool.tensor_tensor(g_s[:, c % 2, :, HALF:DR], part[:, :, DC + HALF:64], sn, ALU.mult).then_inc(g_sin.sem, g_sin.up())
                        yield
                    for _ in range(TILE_PHASES - 12):
                        yield
                for _ in range(MERGE_PHASES):
                    yield

            def close(b):
                pass

            def rest(b):

                pool.wait_ge(rest_done.sem, rest_done.at(b, 0))
                for _ in range(ROUTE_PHASES + 1):
                    yield
                for p in range(8):
                    pool.wait_ge(hu_ok.sem, hu_ok.at(b, p + 1))
                    if p >= 1:
                        pool.wait_ge(y_part.sem, y_part.at(b, p))
                    pool.wait_ge(cb_sb.sem, cb_sb.at(b, 2))
                    pool.tensor_tensor(HT[:, :], SG[:, 1, :], CB[:, p, :], ALU.mult).then_inc(ht_ok.sem, ht_ok.up())
                    yield
                for _ in range(EXPERT_PHASES - 9 + NORM_PHASES + SCAN_IN_PHASES):
                    yield
                for n in range(DS):
                    pool.wait_ge(del_ok.sem, del_ok.at(b, 1))
                    row_in = b_in[n % 2]
                    pool.wait_ge(row_in.sem, row_in.at(b, n // 2 + 1))
                    for j in range(2):
                        if n >= 2:
                            pool.wait_ge(scan_ok.sem, scan_ok.at(b, 2 * (n - 2) + j + 1))
                        pool.tensor_tensor(dBu[:, n % 2, j, :], DU[:, j, :], BC[:, n % 2, 0, :], ALU.mult).then_inc(dBu_ok.sem, dBu_ok.up())
                    yield
                for _ in range(SCAN_OUT_PHASES + NORM_PHASES + TOP1_PHASES):
                    yield

            pool.wait_ge(set_v.sem, SET_VEC)
            pool.wait_ge(s_seta, 3)
            rows_loop(pool, attention, close, rest)

        @block.vector
        def _(dve):
            TT, TS, STT, CP = dve.tensor_tensor, dve.tensor_scalar, dve.scalar_tensor_tensor, dve.tensor_copy

            def attention(b):

                def rotate(dst, src, n, cos, sin, tc, tsn, done):
                    for s, tmp in ((cos, tc), (sin, tsn)):
                        cc = s.unsqueeze(1).to_broadcast([P, n, HALF])
                        TT(tmp[:, :, 0:HALF], src[:, :, 0:HALF], cc, ALU.mult)
                        m = TT(tmp[:, :, HALF:DR], src[:, :, HALF:DR], cc, ALU.mult)
                    m.then_inc(vec.sem, vec.up())
                    dve.wait_ge(vec.sem, vec.now(b))
                    TT(dst[:, :, 0:HALF], tc[:, :, 0:HALF], tsn[:, :, HALF:DR], ALU.subtract)
                    TT(dst[:, :, HALF:DR], tc[:, :, HALF:DR], tsn[:, :, 0:HALF], ALU.add).then_inc(done.sem, done.up())
                    dve.wait_ge(done.sem, done.now(b))

                def merge_a(i):
                    dve.wait_ge(rb_in.sem, rb_in.at(b, i + 1))
                    TT(mj[:, :], ml[:, :], RB[:, :, 32], ALU.max).then_inc(vec.sem, vec.up())
                    dve.wait_ge(vec.sem, vec.now(b))
                    TT(dm[:, 0, :], ml[:, :], mj[:, :], ALU.subtract)
                    TT(dm[:, 1, :], RB[:, :, 32], mj[:, :], ALU.subtract).then_inc(dm_ok.sem, dm_ok.up())
                    dve.wait_ge(dm_ok.sem, dm_ok.now(b))

                def merge_b(i):
                    dve.wait_ge(em_ok.sem, em_ok.at(b, i + 1))
                    dve.wait_ge(ol_ps.sem, ol_ps.at(b, 2 * i + 2))
                    TT(den[:, 0, :], ll[:, :], em[:, 0, :], ALU.mult)
                    TT(den[:, 1, :], RB[:, :, 33], em[:, 1, :], ALU.mult).then_inc(vec.sem, vec.up())
                    dve.wait_ge(vec.sem, vec.now(b))
                    TT(den[:, 2, :], den[:, 0, :], den[:, 1, :], ALU.add).then_inc(vec.sem, vec.up())
                    dve.wait_ge(vec.sem, vec.now(b))
                    dve.reciprocal(den[:, 3, :], den[:, 2, :]).then_inc(vec.sem, vec.up())
                    dve.wait_ge(vec.sem, vec.now(b))
                    TT(fac[:, :, :], em[:, :, :], den[:, 3, :].unsqueeze(1).to_broadcast([P, 2, NH]), ALU.mult).then_inc(vec.sem, vec.up())
                    dve.wait_ge(vec.sem, vec.now(b))
                    TT(On[:, 0, :, :], bank[4][:, 0:256].rearrange("p (h c) -> p h c", h=NH),
                       fac[:, 0, :].unsqueeze(2).to_broadcast([P, NH, DC]), ALU.mult)
                    TT(On[:, 1, :, :], RB[:, :, 0:DC], fac[:, 1, :].unsqueeze(2).to_broadcast([P, NH, DC]), ALU.mult).then_inc(vec.sem, vec.up())
                    dve.wait_ge(vec.sem, vec.now(b))
                    TT(On[:, 0, :, :], On[:, 0, :, :], On[:, 1, :, :], ALU.add).then_inc(on_ok.sem, on_ok.up())
                    dve.wait_ge(on_ok.sem, on_ok.now(b))

                def merge_c(i):
                    dve.wait_ge(at_ps.sem, at_ps.at(b, i + 1))
                    TT(Y1[:, i, :], bank[4][:, 0:P], X[:, i, :], ALU.add).then_inc(at_used.sem, at_used.up())

                dve.wait_ge(attn_done.sem, attn_done.at(b, 0))
                yield
                yield
                dve.wait_ge(kv_ps.sem, kv_ps.at(b, 1))
                dve.wait_ge(proj_sb.sem, proj_sb.at(b, 4))
                dve.wait_ge(kr_sp.sem, kr_sp.at(b, 1))
                kv = bank[0][:, 0:256].rearrange("p (n c) -> p n c", n=NT)
                CP(table[:, :, 0:DC], kv[:, :, 0:DC])
                CP(prev_c[:, :, :], bank[0][0:64, 288:384].rearrange("p (n c) -> p n c", n=3))
                for k in range(2):
                    CP(KD[:, :, k, 0:DC], kv[:, :, 0:DC])
                STT(out=table[:, :, DC:64], in0=kv[:, :, DC:64], scalar=0.0, in1=kr_e[:, 2, :, :],
                         op0=ALU.max, op1=ALU.add).then_inc(vec.sem, vec.up())
                dve.wait_ge(vec.sem, vec.now(b))
                for s in range(2):
                    for hf in range(2):
                        m = TT(krot[:, s, :, HALF * hf:HALF * hf + HALF], table[:, :, DC + HALF * hf:DC + HALF * hf + HALF],
                               trig[:, s, 0:NT, :], ALU.mult)
                m.then_inc(vec.sem, vec.up())
                dve.wait_ge(vec.sem, vec.now(b))
                for k in range(2):
                    TT(KD[:, :, k, DC:DC + HALF], krot[:, 0, :, 0:HALF], krot[:, 1, :, HALF:DR], ALU.subtract)
                    m = TT(KD[:, :, k, DC + HALF:64], krot[:, 0, :, HALF:DR], krot[:, 1, :, 0:HALF], ALU.add)
                m.then_inc(kv_in.sem, kv_in.up())
                CP(tparts[:, :, 0, :], table[:, :, :]).then_inc(vec.sem, vec.up())
                dve.wait_ge(vec.sem, vec.now(b))
                TT(tres[:, 0, :, :], table[:, :, :], tparts[:, :, 0, :], ALU.subtract).then_inc(vec.sem, vec.up())
                dve.wait_ge(vec.sem, vec.now(b))
                CP(tparts[:, :, 1, :], tres[:, 0, :, :]).then_inc(vec.sem, vec.up())
                dve.wait_ge(vec.sem, vec.now(b))
                TT(tres[:, 1, :, :], tres[:, 0, :, :], tparts[:, :, 1, :], ALU.subtract).then_inc(vec.sem, vec.up())
                dve.wait_ge(vec.sem, vec.now(b))
                CP(tparts[:, :, 2, :], tres[:, 1, :, :]).then_inc(parts_ok.sem, parts_ok.up())
                dve.wait_ge(parts_ok.sem, parts_ok.now(b))
                yield

                for i in range(NT):
                    Wi, W0 = index_width(i), first_width(i)
                    c0 = 96 - W0
                    if i >= 1:
                        merge_a(i - 1)
                    dve.wait_ge(ix_relu.sem, ix_relu.at(b, 4 * i + 1))
                    TS(score[:, 0, 0:Wi], relu_s[:, 0, 0:Wi], w("idxw")[:, 0:1], None, ALU.mult).then_inc(ix_used.sem, ix_used.up())
                    dve.wait_ge(ix_used.sem, ix_used.now(b))
                    for h in range(1, NIH):
                        dve.wait_ge(ix_relu.sem, ix_relu.at(b, 4 * i + h + 1))
                        STT(out=score[:, 0, 0:Wi], in0=relu_s[:, h % 2, 0:Wi], scalar=w("idxw")[:, h:h + 1],
                                 in1=score[:, 0, 0:Wi], op0=ALU.mult, op1=ALU.add).then_inc(ix_used.sem, ix_used.up())
                        dve.wait_ge(ix_used.sem, ix_used.now(b))
                    lo = 0 if i == 0 else Wi - P
                    mask = co("top0") if i == 0 else co("top1")
                    TT(score[:, 0, lo:Wi], score[:, 0, lo:Wi], mask, ALU.add).then_inc(vec.sem, vec.up())
                    dve.wait_ge(vec.sem, vec.now(b))
                    yield
                    for r in range(NREM // 8):
                        cur, nxt = score[:, r % 2, 0:Wi], score[:, (r + 1) % 2, 0:Wi]
                        dve.sem_inc(hold_dve, 1)
                        dve.max(top[:, 8 * r:8 * r + 8], cur).then_inc(vec.sem, vec.up())
                        dve.wait_ge(vec.sem, vec.now(b))
                        dve.sem_inc(hold_dve, 1)
                        m = dve.max_index(idx[:, 8 * r:8 * r + 8], top[:, 8 * r:8 * r + 8], cur)
                        if r < 3:
                            m = dve.match_replace(nxt, top[:, 8 * r:8 * r + 8], cur, NEG_TOP)
                        m.then_inc(vec.sem, vec.up())
                        dve.wait_ge(vec.sem, vec.now(b))
                        if r == 1:
                            if i >= 1:
                                merge_b(i - 1)
                            yield
                    dve.transpose(idxT[:, :], idx[:, :]).then_inc(vec.sem, vec.up())
                    dve.wait_ge(vec.sem, vec.now(b))
                    CP(idxh[:, :], idxT[:, :]).then_inc(idx_ok.sem, idx_ok.up())
                    dve.wait_ge(idx_ok.sem, idx_ok.now(b))
                    yield
                    dve.wait_ge(q_sp.sem, q_sp.at(b, i + 1))
                    STT(out=muq[:, :, :].rearrange("p h c -> p (h c)"), in0=bank[0][:, 0:256], scalar=0.0,
                             in1=q_e[:, 2, :], op0=ALU.max, op1=ALU.add).then_inc(vec.sem, vec.up())
                    dve.wait_ge(vec.sem, vec.now(b))
                    CP(QA[:, :, 0, :], bank[0][:, 256:512].rearrange("p (h c) -> p h c", h=NH))
                    CP(QB[:, :, 0, :], bank[0][:, 256:512].rearrange("p (h c) -> p h c", h=NH))
                    rotate(QA[:, :, 1, :], muq, NH, trig[:, 0, i, :], trig[:, 1, i, :], qr_c, qr_s, vec)
                    rotate(QB[:, :, 1, :], muq, NH, trig[:, 0, 4 + i, :], trig[:, 1, 4 + i, :], qr_c, qr_s, q_rows)
                    yield
                    if i >= 1:
                        merge_c(i - 1)
                    dve.transpose(QT[:, :, :, :], QA[:, :, :, :]).then_inc(vec.sem, vec.up())
                    dve.wait_ge(vec.sem, vec.now(b))
                    for bb in range(4):
                        m = CP(QBD[32 * bb:32 * bb + 32, :, :, bb, :].rearrange("p t k h -> p k h t"),
                               QT[32 * bb:32 * bb + 32, :, :, :].rearrange("p h k t -> p k h t"))

                    def local_max(g):
                        dve.wait_ge(sl_ps.sem, sl_ps.at(b, 2 * i + g + 1))
                        for k in range(2):
                            m = dve.tensor_reduce(ml[:, 4 * g + k:4 * g + k + 3:2],
                                                  bank[2 + k][:, :].rearrange("p (h c) -> p h c", h=2)[:, :, c0:224],
                                                  AX.X, ALU.max)
                        m.then_inc(vec.sem, vec.up())
                        dve.wait_ge(vec.sem, vec.now(b))
                        TS(nml[:, 4 * g:4 * g + 4], ml[:, 4 * g:4 * g + 4], -SCALE, None, ALU.mult).then_inc(ml_ok.sem, ml_ok.up())

                    local_max(0)
                    yield
                    local_max(1)
                    yield
                    yield
                    yield

                    def onehots(r):
                        dve.wait_ge(ib_sb.sem, ib_sb.at(b, 8 * i + r + 1))
                        if 8 * i + r >= 2:
                            dve.wait_ge(g_round.sem, g_round.at(b, 8 * i + r - 1))
                        for kt in range(i + 1):
                            kk = 64 if kt == i else P
                            m = TS(onehot[0:kk, r % 2, kt, :], ib[0:kk, r % 2, :], co("pos")[0:kk, kt:kt + 1], None,
                                   ALU.is_equal)
                        m.then_inc(oh_ok.sem, oh_ok.up())

                    def turned(c):
                        dve.wait_ge(g_sb.sem, g_sb.at(b, 4 * i + c + 1))
                        cs = trig[:, 0, 8, :].unsqueeze(1).to_broadcast([P, 8, HALF])
                        part = G[:, 8 * c:8 * c + 8, :]
                        TT(g_c[:, :, 0:HALF], part[:, :, DC:DC + HALF], cs, ALU.mult)
                        TT(g_c[:, :, HALF:DR], part[:, :, DC + HALF:64], cs, ALU.mult).then_inc(vec.sem, vec.up())
                        dve.wait_ge(vec.sem, vec.now(b))
                        dve.wait_ge(g_sin.sem, g_sin.at(b, 4 * i + c + 1))
                        TT(GR[:, :, 0:HALF], g_c[:, :, 0:HALF], g_s[:, c % 2, :, HALF:DR], ALU.subtract)
                        TT(GR[:, :, HALF:DR], g_c[:, :, HALF:DR], g_s[:, c % 2, :, 0:HALF], ALU.add).then_inc(g_rot.sem, g_rot.up())
                        dve.wait_ge(g_rot.sem, g_rot.now(b))
                        dve.transpose(GT[:, 0, 8 * c:8 * c + 8, :], part[:, :, 0:DC])
                        done = gt_ok if c == 3 else vec
                        dve.transpose(GT[:, 1, 8 * c:8 * c + 8, :], GR[:, :, :]).then_inc(done.sem, done.up())
                        dve.wait_ge(done.sem, done.now(b))

                    for c in range(4):
                        onehots(2 * c)
                        onehots(2 * c + 1)
                        if c >= 1:
                            turned(c - 1)
                        yield
                    turned(3)
                    yield
                    dve.wait_ge(sr_ps.sem, sr_ps.at(b, i + 1))
                    sp_ = bank[0][:, 0:256].rearrange("p (x j) -> p x j", x=8)
                    if i == 0:
                        TT(SR[:, :, :], sp_, co("rmask"), ALU.add).then_inc(vec.sem, vec.up())
                        dve.wait_ge(vec.sem, vec.now(b))
                        sp_ = SR[:, :, :]
                    else:
                        dve.wait_ge(ro_st.sem, ro_st.at(b, 16 * i))
                    dve.tensor_reduce(RO[:, :, 32], sp_, AX.X, ALU.max).then_inc(vec.sem, vec.up())
                    dve.wait_ge(vec.sem, vec.now(b))
                    TT(SRd[:, :, :], sp_, RO[:, :, 32:33].to_broadcast([P, 8, 32]), ALU.subtract).then_inc(sr_d.sem, sr_d.up())
                    dve.wait_ge(sr_d.sem, sr_d.now(b))
                    yield
                    dve.wait_ge(pr_ok.sem, pr_ok.at(b, i + 1))
                    dve.tensor_reduce(RO[:, :, 33], PR[:, :, :], AX.X, ALU.add)
                    dve.transpose(PT[:, :, :], PR[:, :, :]).then_inc(vec.sem, vec.up())
                    dve.wait_ge(vec.sem, vec.now(b))
                    for a in range(4):
                        for bb in range(4):
                            m = CP(PBD[32 * bb:32 * bb + 32, :, a, bb, :], PT[32 * a:32 * a + 32, :, 8 * bb:8 * bb + 8])
                    m.then_inc(pbd_ok.sem, pbd_ok.up())
                    yield
                merge_a(NT - 1)
                yield
                merge_b(NT - 1)
                yield

            def norm_sums(b, Y):
                dve.sem_inc(hold_dve, 1)
                for i in range(NT):
                    m = dve.bn_stats(stats[:, i, :], Y[:, i, :])
                m.then_inc(vec2.sem, vec2.up())
                dve.wait_ge(vec2.sem, vec2.at(b, vec2.k))
                dve.sem_inc(hold_dve, 1)
                for i in range(NT):
                    m = dve.bn_aggr(mv[:, i, :], stats[:, i, :])
                m.then_inc(var_ok.sem, var_ok.up())
                dve.wait_ge(var_ok.sem, var_ok.at(b, var_ok.k))

            def norm_rows(b, Y, k, dst, done):
                dve.wait_ge(rstd_ok.sem, rstd_ok.at(b, k))
                for i in range(NT):
                    m = TS(dst[:, i, :], Y[:, i, :], mv[:, i, 0:1], rstd[:, i:i + 1], ALU.subtract, ALU.mult)
                m.then_inc(done.sem, done.up())
                dve.wait_ge(done.sem, done.at(b, done.k))

            def close(b):
                dve.wait_ge(at_ps.sem, at_ps.at(b, NT))
                TT(Y1[:, NT - 1, :], bank[4][:, 0:P], X[:, NT - 1, :], ALU.add).then_inc(at_used.sem, at_used.up())
                dve.wait_ge(at_used.sem, at_used.at(b, NT))
                norm_sums(b, Y1)
                dve.wait_ge(rest_done.sem, rest_done.at(b, 0))
                norm_rows(b, Y1, 1, XR, attn_done)

            def rest(b):

                dve.wait_ge(rest_done.sem, rest_done.at(b, 0))
                dve.wait_ge(rl_e.sem, rl_e.at(b, 1))
                TS(rt[:, 1, :, :], rt[:, 0, :, :], 1.0, None, ALU.add).then_inc(vec2.sem, vec2.up())
                dve.wait_ge(vec2.sem, vec2.now(b))
                dve.reciprocal(rt[:, 2, :, :], rt[:, 1, :, :]).then_inc(vec2.sem, vec2.up())
                dve.wait_ge(vec2.sem, vec2.now(b))
                TT(rt[:, 3, :, :], rt[:, 2, :, :], w("gb").unsqueeze(1).to_broadcast([P, NT, NE]), ALU.add).then_inc(vec2.sem, vec2.up())
                dve.wait_ge(vec2.sem, vec2.now(b))
                yield
                dve.sem_inc(hold_dve, 1)
                for i in range(NT):
                    m = dve.max(r8[:, i, :], rt[:, 3, i, :])
                m.then_inc(vec2.sem, vec2.up())
                dve.wait_ge(vec2.sem, vec2.now(b))
                dve.sem_inc(hold_dve, 1)
                for i in range(NT):
                    m = dve.max_index(ri[:, i, :], r8[:, i, :], rt[:, 3, i, :])
                m.then_inc(vec2.sem, vec2.up())
                dve.wait_ge(vec2.sem, vec2.now(b))
                CP(rif[:, :, :], ri[:, :, :]).then_inc(vec2.sem, vec2.up())
                dve.wait_ge(vec2.sem, vec2.now(b))
                for i in range(NT):
                    m = TT(req[:, i, :, :], co("iota")[:, 0:NE].unsqueeze(2).to_broadcast([P, NE, TOP_E]),
                           rif[:, i, 0:TOP_E].unsqueeze(1).to_broadcast([P, NE, TOP_E]), ALU.is_equal)
                m.then_inc(vec2.sem, vec2.up())
                dve.wait_ge(vec2.sem, vec2.now(b))
                yield
                dve.tensor_reduce(rt[:, 4, :, :], req[:, :, :, :], AX.X, ALU.add).then_inc(vec2.sem, vec2.up())
                dve.wait_ge(vec2.sem, vec2.now(b))
                TT(rt[:, 4, :, :], rt[:, 4, :, :], rt[:, 2, :, :], ALU.mult).then_inc(vec2.sem, vec2.up())
                dve.wait_ge(vec2.sem, vec2.now(b))
                dve.tensor_reduce(rs[:, 0, :], rt[:, 4, :, :], AX.X, ALU.add).then_inc(vec2.sem, vec2.up())
                dve.wait_ge(vec2.sem, vec2.now(b))
                dve.reciprocal(rs[:, 1, :], rs[:, 0, :]).then_inc(vec2.sem, vec2.up())
                dve.wait_ge(vec2.sem, vec2.now(b))
                STT(out=rt[:, 5, :, :], in0=rt[:, 4, :, :], scalar=ROUTE,
                         in1=rs[:, 1, :].unsqueeze(2).to_broadcast([P, NT, NE]), op0=ALU.mult, op1=ALU.mult).then_inc(comb_ok.sem, comb_ok.up())
                dve.wait_ge(comb_ok.sem, comb_ok.now(b))
                yield
                yield

                def hidden(p):
                    rows = P if p < 8 else 64
                    dve.wait_ge(sg_ok.sem, sg_ok.at(b, p + 1))
                    TS(SG[0:rows, 0, :], SG[0:rows, 0, :], 1.0, None, ALU.add).then_inc(vec2.sem, vec2.up())
                    dve.wait_ge(vec2.sem, vec2.now(b))
                    if p >= 1:
                        dve.wait_ge(ht_ok.sem, ht_ok.at(b, p))
                    dve.reciprocal(SG[0:rows, 1, :], SG[0:rows, 0, :]).then_inc(vec2.sem, vec2.up())
                    dve.wait_ge(vec2.sem, vec2.now(b))
                    TT(SG[0:rows, 1, :], SG[0:rows, 1, :], bank[5][0:rows, :], ALU.mult).then_inc(vec2.sem, vec2.up())
                    dve.wait_ge(vec2.sem, vec2.now(b))
                    if p == 8:
                        dve.wait_ge(y_part.sem, y_part.at(b, 8))
                    dst = SG[:, 1, :] if p < 8 else HT[0:rows, :]
                    TT(dst, SG[0:rows, 1, :], bank[6][0:rows, :], ALU.mult).then_inc(hu_ok.sem, hu_ok.up())
                    dve.wait_ge(hu_ok.sem, hu_ok.now(b))

                for p in range(9):
                    hidden(p)
                    yield
                dve.wait_ge(y_part.sem, y_part.at(b, 9))
                TT(Y2[:, :, :], bank[7][:, :].rearrange("p (n d) -> p n d", n=NT), XR[:, :, :], ALU.add).then_inc(vec2.sem, vec2.up())
                dve.wait_ge(vec2.sem, vec2.now(b))
                norm_sums(b, Y2)
                yield
                norm_rows(b, Y2, 2, XR, ln_ok)
                yield

                yield
                yield
                dve.wait_ge(out_stored.sem, out_stored.at(b, 0))
                for j in range(2):
                    dve.wait_ge(xz_sb.sem, xz_sb.at(b, j + 1))
                    cw = w("cw")[:, j, :]
                    TS(CV[:, j, :], XP[:, j, 0:L], cw[:, 0:1], w("cb")[:, j:j + 1], ALU.mult, ALU.add).then_inc(vec2.sem, vec2.up())
                    dve.wait_ge(vec2.sem, vec2.now(b))
                    for k in range(1, DCONV):
                        done = cv_ok if k == DCONV - 1 else vec2
                        STT(out=CV[:, j, :], in0=XP[:, j, k:k + L], scalar=cw[:, k:k + 1], in1=CV[:, j, :],
                                 op0=ALU.mult, op1=ALU.add).then_inc(done.sem, done.up())
                        dve.wait_ge(done.sem, done.now(b))
                yield
                for j in range(2):
                    dve.wait_ge(xz_sb.sem, xz_sb.at(b, j + 3))
                    TS(ez[:, j, :], ez[:, j, :], 1.0, None, ALU.add).then_inc(vec2.sem, vec2.up())
                    dve.wait_ge(vec2.sem, vec2.now(b))
                    dve.reciprocal(SZ[:, j, :], ez[:, j, :]).then_inc(vec2.sem, vec2.up())
                    dve.wait_ge(vec2.sem, vec2.now(b))
                    TT(SZ[:, j, :], SZ[:, j, :], bank[5 + j][:, :], ALU.mult).then_inc(sz_ok.sem, sz_ok.up())
                    dve.wait_ge(sz_ok.sem, sz_ok.now(b))
                yield
                for j in range(2):
                    dve.wait_ge(ue_ok.sem, ue_ok.at(b, j + 1))
                    TS(eu[:, j, :], eu[:, j, :], 1.0, None, ALU.add).then_inc(vec2.sem, vec2.up())
                    dve.wait_ge(vec2.sem, vec2.now(b))
                    dve.reciprocal(U[:, j, :], eu[:, j, :]).then_inc(vec2.sem, vec2.up())
                    dve.wait_ge(vec2.sem, vec2.now(b))
                    TT(U[:, j, :], U[:, j, :], CV[:, j, :], ALU.mult).then_inc(u_ok.sem, u_ok.up())
                    dve.wait_ge(u_ok.sem, u_ok.now(b))
                yield
                yield
                for j in range(2):
                    dve.wait_ge(dt_ps.sem, dt_ps.at(b, j + 1))
                    m = TS(dt_x[:, j, :], bank[5 + j][:, :], dtb2[:, j:j + 1], None, ALU.add)
                m.then_inc(dtx_ok.sem, dtx_ok.up())
                dve.wait_ge(dtx_ok.sem, dtx_ok.now(b))
                yield
                dve.wait_ge(dt_sp.sem, dt_sp.at(b, 1))
                TS(dt_a, dt_b, 2.0, None, ALU.add).then_inc(vec2.sem, vec2.up())
                dve.wait_ge(vec2.sem, vec2.now(b))
                dve.reciprocal(dt_c, dt_a).then_inc(vec2.sem, vec2.up())
                dve.wait_ge(vec2.sem, vec2.now(b))
                TT(dt_a, dt_b, dt_c, ALU.mult).then_inc(vec2.sem, vec2.up())
                dve.wait_ge(vec2.sem, vec2.now(b))
                TT(dt_c, dt_a, dt_a, ALU.mult).then_inc(vec2.sem, vec2.up())
                dve.wait_ge(vec2.sem, vec2.now(b))
                TS(dt_b, dt_c, LOG1P[4], None, ALU.mult).then_inc(vec2.sem, vec2.up())
                dve.wait_ge(vec2.sem, vec2.now(b))
                yield
                for c in LOG1P[3:0:-1]:
                    STT(out=dt_b, in0=dt_b, scalar=c, in1=dt_c, op0=ALU.add, op1=ALU.mult).then_inc(vec2.sem, vec2.up())
                    dve.wait_ge(vec2.sem, vec2.now(b))
                STT(out=dt_b, in0=dt_b, scalar=LOG1P[0], in1=dt_a, op0=ALU.add, op1=ALU.mult).then_inc(vec2.sem, vec2.up())
                dve.wait_ge(vec2.sem, vec2.now(b))
                STT(out=DEL[:, :, :], in0=dt_x, scalar=0.0, in1=dt_b, op0=ALU.max, op1=ALU.add).then_inc(vec2.sem, vec2.up())
                dve.wait_ge(vec2.sem, vec2.now(b))
                TT(DU[:, :, :], DEL[:, :, :], U[:, :, :], ALU.mult).then_inc(del_ok.sem, del_ok.up())
                dve.wait_ge(del_ok.sem, del_ok.now(b))
                for n in range(DS):
                    for j in range(2):
                        dve.wait_ge(dA_ok.sem, dA_ok.at(b, 2 * n + j + 1))
                        dve.wait_ge(dBu_ok.sem, dBu_ok.at(b, 2 * n + j + 1))
                        dve.tensor_tensor_scan(hs[:, j, :], dA[:, n % 2, j, :], dBu[:, n % 2, j, :], 0.0,
                                                    ALU.mult, ALU.add).then_inc(scan_ok.sem, scan_ok.up())
                        dve.wait_ge(scan_ok.sem, scan_ok.now(b))
                        row_in = c_in[n % 2]
                        dve.wait_ge(row_in.sem, row_in.at(b, n // 2 + 1))
                        if n >= 2:
                            dve.wait_ge(ysum.sem, ysum.at(b, 2 * (n - 2) + j + 1))
                        TT(hC[n % 2][:, j, :], hs[:, j, :], BC[:, n % 2, 1, :], ALU.mult).then_inc(hC_ok.sem, hC_ok.up())
                        dve.wait_ge(hC_ok.sem, hC_ok.now(b))
                    yield
                dve.wait_ge(ysum.sem, ysum.at(b, 2 * DS))
                for j in range(2):
                    m = STT(out=CV[:, j, :], in0=U[:, j, :], scalar=w("Dp")[:, j:j + 1], in1=bank[5 + j][:, :],
                            op0=ALU.mult, op1=ALU.add)
                m.then_inc(vec2.sem, vec2.up())
                dve.wait_ge(vec2.sem, vec2.now(b))
                TT(YG[:, :, :], CV[:, :, :], SZ[:, :, :], ALU.mult).then_inc(yg_ok.sem, yg_ok.up())
                dve.wait_ge(yg_ok.sem, yg_ok.now(b))
                yield
                dve.wait_ge(op_ps.sem, op_ps.at(b, 1))
                TT(Y2[:, :, :], bank[7][:, :].rearrange("p (n d) -> p n d", n=NT), XR[:, :, :], ALU.add).then_inc(vec2.sem, vec2.up())
                dve.wait_ge(vec2.sem, vec2.now(b))
                norm_sums(b, Y2)
                yield
                norm_rows(b, Y2, 3, XR, ln_ok)
                yield
                yield

                dve.wait_ge(rl_ps.sem, rl_ps.at(b, 2))
                lg = bank[7][:, 0:NT * NE2].rearrange("p (n e) -> p n e", n=NT)
                dve.tensor_reduce(ps1[:, 0, :], lg, AX.X, ALU.max).then_inc(vec2.sem, vec2.up())
                dve.wait_ge(vec2.sem, vec2.now(b))
                TT(pr[:, 0, :, :], lg, ps1[:, 0, :].unsqueeze(2).to_broadcast([P, NT, NE2]), ALU.subtract).then_inc(pm_ok.sem, pm_ok.up())
                dve.wait_ge(pm_ok.sem, pm_ok.now(b))
                yield
                dve.wait_ge(pe_ok.sem, pe_ok.at(b, 1))
                dve.tensor_reduce(ps1[:, 1, :], pr[:, 1, :, :], AX.X, ALU.add).then_inc(vec2.sem, vec2.up())
                dve.wait_ge(vec2.sem, vec2.now(b))
                dve.reciprocal(ps1[:, 2, :], ps1[:, 1, :]).then_inc(vec2.sem, vec2.up())
                dve.wait_ge(vec2.sem, vec2.now(b))
                TT(pr[:, 2, :, :], pr[:, 1, :, :], ps1[:, 2, :].unsqueeze(2).to_broadcast([P, NT, NE2]), ALU.mult).then_inc(vec2.sem, vec2.up())
                dve.wait_ge(vec2.sem, vec2.now(b))
                dve.sem_inc(hold_dve, 1)
                for i in range(NT):
                    m = dve.max(r8[:, i, :], pr[:, 2, i, :])
                m.then_inc(vec2.sem, vec2.up())
                dve.wait_ge(vec2.sem, vec2.now(b))
                dve.sem_inc(hold_dve, 1)
                for i in range(NT):
                    m = dve.max_index(ri[:, i, :], r8[:, i, :], pr[:, 2, i, :])
                m.then_inc(vec2.sem, vec2.up())
                dve.wait_ge(vec2.sem, vec2.now(b))
                CP(rif[:, :, :], ri[:, :, :]).then_inc(vec2.sem, vec2.up())
                dve.wait_ge(vec2.sem, vec2.now(b))
                TT(mk[:, :, :], co("iota")[:, 0:NE2].unsqueeze(1).to_broadcast([P, NT, NE2]),
                        rif[:, :, 0:1].to_broadcast([P, NT, NE2]), ALU.is_equal).then_inc(vec2.sem, vec2.up())
                dve.wait_ge(vec2.sem, vec2.now(b))
                CP(mk_bf[:, :, :], mk[:, :, :]).then_inc(mk_ok.sem, mk_ok.up())
                dve.wait_ge(mk_ok.sem, mk_ok.now(b))
                yield
                TT(pr[:, 3, :, :], pr[:, 2, :, :], mk[:, :, :], ALU.mult).then_inc(vec2.sem, vec2.up())
                dve.wait_ge(vec2.sem, vec2.now(b))
                dve.wait_ge(loc_ps.sem, loc_ps.at(b, 1))
                TS(keep[:, :, :], bank[7][:, 64:64 + NT * NE2].rearrange("p (n e) -> p n e", n=NT), float(CAP), None,
                        ALU.is_lt).then_inc(vec2.sem, vec2.up())
                dve.wait_ge(vec2.sem, vec2.now(b))
                TT(gate[:, :, :], pr[:, 3, :, :], keep[:, :, :], ALU.mult).then_inc(gate_ok.sem, gate_ok.up())
                dve.wait_ge(gate_ok.sem, gate_ok.now(b))
                dve.tensor_reduce(csum[:, :], mk[:, :, :].rearrange("p n e -> p e n"), AX.X, ALU.add).then_inc(vec2.sem, vec2.up())
                dve.wait_ge(vec2.sem, vec2.now(b))
                TT(cum[:, :], cum[:, :], csum[:, :], ALU.add).then_inc(vec2.sem, vec2.up())
                dve.wait_ge(vec2.sem, vec2.now(b))
                CP(cum_bf[:, :], cum[:, :]).then_inc(vec2.sem, vec2.up())
                dve.wait_ge(vec2.sem, vec2.now(b))
                yield
                dve.wait_ge(bias_ps.sem, bias_ps.at(b, 1))
                TT(Y2[:, :, :], bank[7][:, :].rearrange("p (n d) -> p n d", n=NT), XR[:, :, :], ALU.add).then_inc(vec2.sem, vec2.up())
                dve.wait_ge(vec2.sem, vec2.now(b))
                for i in range(NT):
                    dve.wait_ge(e_ps.sem, e_ps.at(b, i + 1))
                    for e in range(NE2):
                        m = STT(out=Y2[:, i, :], in0=bank[5 + e // 4][:, (e % 4) * P:(e % 4 + 1) * P],
                                scalar=gate[:, i, e:e + 1], in1=Y2[:, i, :], op0=ALU.mult, op1=ALU.add)
                        done = e_used if e == NE2 - 1 else vec2
                        m.then_inc(done.sem, done.up())
                        dve.wait_ge(done.sem, done.now(b))
                    yield
                norm_sums(b, Y2)
                yield
                norm_rows(b, Y2, 4, OUT, rest_done)
                yield

            for t in (QBD[:, :, :, :, :], PBD[:, :, :, :, :], XP[:, :, :]):
                dve.memset(t, 0.0)
            dve.memset(cum[:, :], 0.0)
            dve.memset(one[:, :], 1.0)
            dve.memset(eps[:, :], EPS)
            dve.memset(ones_bf[:, :], 1.0)
            dve.memset(cum_bf[:, :], 0.0)
            dve.wait_ge(s_load, 64)
            CP(ident_bf[:, :], ident)
            CP(ident_h[:, :], ident)
            CP(tri_bf[:, :], once("tri"))
            CP(lmask_bf[:, :, :], once("lmask"))
            TS(dtb2[:, :], w("dtb"), 2.0, None, ALU.mult)
            CP(WQ[:, 0, :], wh("qr"))
            dve.wait_ge(s_seta, 2)
            TS(Aneg[:, :, :], Aneg[:, :, :], -1.0, None, ALU.mult).then_inc(set_v.sem, set_v.up())
            dve.wait_ge(set_v.sem, set_v.k)
            TS(dl[:, 1, :], dl[:, 0, :], 1.0, None, ALU.add).then_inc(set_v.sem, set_v.up())
            dve.wait_ge(set_v.sem, set_v.k)
            dve.reciprocal(dl[:, 2, :], dl[:, 1, :]).then_inc(set_v.sem, set_v.up())
            dve.wait_ge(set_v.sem, set_v.k)
            TS(dl[:, 3, :], dl[:, 2, :], -2.0 * np.pi, np.pi, ALU.mult, ALU.add).then_inc(set_v.sem, set_v.up())
            dve.wait_ge(set_v.sem, set_v.k)
            TS(dl[:, 3, :], dl[:, 3, :], 3.1415925, -3.1415925, ALU.min, ALU.max).then_inc(set_v.sem, set_v.up())
            dve.wait_ge(set_v.sem, set_v.k)
            assert set_v.k == SET_SIN
            dve.wait_ge(s_setp, 2)
            CP(WQ[:, 1, :], bank[0][0:64, 0:256])
            CP(WVO[:, :, :].rearrange("p a c -> p (a c)"), bank[1][:, 0:256])
            dve.wait_ge(s_seta, 3)
            TT(dl[:, 6, :], dl[:, 5, :], dl[:, 5, :], ALU.mult).then_inc(set_v.sem, set_v.up())
            dve.wait_ge(set_v.sem, set_v.k)
            TS(dl[:, 6, :], dl[:, 6, :], 2.0, -1.0, ALU.mult, ALU.add)
            TS(dl[:, 7, :], dl[:, 4, :], -1.0, None, ALU.mult).then_inc(set_v.sem, set_v.up())
            dve.wait_ge(set_v.sem, set_v.k)
            cd = dl[:, 6, :].unsqueeze(1).to_broadcast([P, 9, HALF])
            sd = dl[:, 7, :].unsqueeze(1).to_broadcast([P, 9, HALF])
            trig_t = Y1[:, :, :].rearrange("p n d -> p (n d)")[:, 0:18 * HALF].rearrange("p (s a c) -> p s a c", s=2, a=9)
            TT(trig[:, 0, :, :], once("cosb"), cd, ALU.mult)
            TT(trig_t[:, 0, :, :], once("sinb"), sd, ALU.mult)
            TT(trig[:, 1, :, :], once("sinb"), cd, ALU.mult)
            TT(trig_t[:, 1, :, :], once("cosb"), sd, ALU.mult).then_inc(set_v.sem, set_v.up())
            dve.wait_ge(set_v.sem, set_v.k)
            TT(trig[:, 0, :, :], trig[:, 0, :, :], trig_t[:, 0, :, :], ALU.subtract)
            TT(trig[:, 1, :, :], trig[:, 1, :, :], trig_t[:, 1, :, :], ALU.add).then_inc(set_v.sem, set_v.up())
            dve.wait_ge(set_v.sem, set_v.k)
            assert set_v.k == SET_VEC
            dve.sem_inc(attn_done.sem, 1)
            dve.sem_inc(rest_done.sem, 1)
            rows_loop(dve, attention, close, rest)

        for name, s in signals.items():
            assert s.k == s.per, f"{name} rises {s.k} times in a batch row, not {s.per}"


PER = {"vec": 135, "vec2": 111, "act": 10, "act2": 5}
SET_SIN = 5
SET_VEC = 9
KEY_PHASES, TILE_PHASES, MERGE_PHASES = 3, 15, 2
ROUTE_PHASES, EXPERT_PHASES, NORM_PHASES, SCAN_IN_PHASES, SCAN_OUT_PHASES, TOP1_PHASES = 3, 10, 2, 8, 1, 10


def pack(pieces, rows):
    where, cols, off = {}, [], 0
    for name, a in pieces.items():
        a = np.asarray(a)
        where[name] = (off, a.shape[0], a.shape[1:])
        flat = a.reshape(a.shape[0], -1)
        if a.shape[0] < rows:
            flat = np.concatenate([flat, np.zeros((rows - a.shape[0], flat.shape[1]), flat.dtype)], 0)
        cols.append(flat)
        off += flat.shape[1]
    return np.ascontiguousarray(np.concatenate(cols, 1)), where


def constants():
    p = np.arange(P)[:, None]
    c = np.arange(P)[None, :]
    theta = (1.0 / np.float32(10000.0) ** (2.0 * np.arange(HALF, dtype=np.float32) / DR)).astype(np.float32)
    pos = np.zeros((P, 9), np.float32)
    for i in range(NT):
        pos[:, i] = P * i + np.arange(P)
        pos[:, 4 + i] = 2 * (P * i + np.arange(P)) - (LW - 1)
    pos[:, 8] = LW + np.arange(P) % 32
    ang = (pos[:, :, None] * theta[None, None, :]).astype(np.float32).astype(np.float64)
    lm = np.full((P, 2, 224), NEG, np.float32)
    a96, s128 = np.arange(96)[None, :], np.arange(P)[None, :]
    lm[:, 0, 0:96][(p < 64) | ((p <= TOPK - 2) & (a96 > p))] = 0
    lm[:, 0, 96:224][(p >= 64) & (s128 <= p) & (s128 >= p - (LW - 1))] = 0
    w192 = np.arange(192)[None, :] - 64
    lm[:, 1, 32:224][(w192 <= p) & (w192 >= p - (LW - 1))] = 0
    a, bb, xx, j = (np.arange(P) // 32)[:, None, None], (np.arange(P) // 8 % 4)[:, None, None], \
        np.arange(8)[None, :, None], np.arange(32)[None, None, :]
    t = 32 * bb + 4 * xx + a
    f = np.float32
    return {
        "ident": np.eye(P, dtype=f), "tri": (p < c).astype(f), "lmask": lm,
        "top0": np.where(c[:, 0:64] <= p - 64, 0, NEG_TOP).astype(f), "top1": np.where(c <= p, 0, NEG_TOP).astype(f),
        "rmask": np.where(j <= t - LW, 0, NEG).astype(f),
        "cosb": np.cos(ang).astype(f), "sinb": np.sin(ang).astype(f),
        "pos": (p + P * np.arange(NT)[None, :]).astype(f), "iota": np.broadcast_to(np.arange(NE), (P, NE)).astype(f),
    }


def kernel(**inputs):
    import concourse.bacc as _bacc
    from concourse.bass_utils import run_bass_kernel_spmd as _run

    a = {k: np.asarray(v) for k, v in inputs.items()}
    g = lambda n: a["L0_attn_" + n]
    f = lambda n: a["L0_ffn_" + n]
    m = lambda n: a["L1_attn_" + n]
    rows = lambda v: np.broadcast_to(v[None, :], (P, v.shape[0]))
    w13 = f("w13").transpose(2, 0, 1)
    w128, at128 = pack({
        "wk2": np.concatenate([g("idx_wk"), g("idx_wk")], 1), "wq": g("idx_wq"), "dq": g("W_dq"),
        "kv": np.concatenate([g("W_dkv"), g("W_kr")], 1), "idxw": rows(g("idx_w")), "rawd": rows(g("raw_delta")),
        "gate": f("gate_w").T, "gb": rows(f("gate_b")),
        "w1g": w13[:, :, 0:64].reshape(D, NE // 2, P), "w1u": w13[:, :, 64:].reshape(D, NE // 2, P),
        "w1sg": f("w13_s").T[:, 0:64], "w1su": f("w13_s").T[:, 64:],
        "w2": f("w2").transpose(0, 2, 1).reshape(NE // 2, P, D).transpose(1, 0, 2), "w2s": f("w2_s").T,
        "inp": m("in_proj_w").T, "cw": m("conv_w")[:, 0, :].reshape(2, P, DCONV).transpose(1, 0, 2),
        "cb": m("conv_b").reshape(2, P).T, "xp": m("x_proj_w").T.reshape(2, P, 40).transpose(1, 0, 2),
        "dtw": m("dt_proj_w").T, "dtb": m("dt_proj_b").reshape(2, P).T,
        "alog": m("A_log").reshape(2, P, DS).transpose(1, 0, 2), "Dp": m("D").reshape(2, P).T,
        "op": m("out_proj_w").T.reshape(2, P, D).transpose(1, 0, 2),
        "wg": a["L1_ffn_wg"], "ew": a["L1_ffn_W"].transpose(2, 0, 1).reshape(D, NE2 * D), "eb": a["L1_ffn_b"],
    }, P)
    w64, at64 = pack({
        "qr": g("W_qr"), "uqT": g("W_uq").reshape(DQ, NH, DH).transpose(2, 1, 0),
        "ukT": g("W_uk").reshape(DC, NH, DH).transpose(2, 1, 0), "uvT": g("W_uv").reshape(DC, NH, DH).transpose(2, 1, 0),
        "out": g("W_out").reshape(NH, DH, D).transpose(1, 0, 2),
    }, 64)
    every = constants()
    first = ("tri", "lmask", "cosb", "sinb")
    consts, atc = pack({k: v for k, v in every.items() if k not in first}, P)
    setup_c, ats = pack({k: every[k] for k in first}, P)
    arrays = {"x": np.ascontiguousarray(g("x")), "w128": w128, "w64": w64, "consts": consts, "setup_c": setup_c}
    nc = _bacc.Bacc("TRN2", target_bir_lowering=False, num_devices=1)
    aps = [nc.dram_tensor(k, v.shape, mybir.dt.from_np(v.dtype), kind="ExternalInput").ap() for k, v in arrays.items()]
    o = nc.dram_tensor("out", (B, L, D), F32, kind="ExternalOutput").ap()
    nc.disable_value_cache = True
    build(nc, *aps, o, at128, at64, atc, ats)
    r = _run(nc, [arrays], core_ids=[0])
    return r.results[0]["out"]
```

```python
from contextlib import ExitStack, contextmanager

import numpy as np

import concourse.bass as bass
from concourse import mybir

F32 = mybir.dt.float32
F16 = mybir.dt.float16
BF16 = mybir.dt.bfloat16
U32 = mybir.dt.uint32
ALU = mybir.AluOpType
ACT = mybir.ActivationFunctionType
AX = mybir.AxisListType

B, L, D = 4, 512, 128
P = 128
NT = L // P
NH, DH, DR, DC, DQ = 8, 64, 32, 32, 64
HALF = DR // 2
NIH = 4
TOPK, LW = 96, 64
NREM = TOPK - LW
NCOL = P // 4
SCALE = float(DH + DR) ** -0.5
NEG_TOP = -3.0e38
NEG = -1.0e30
NE, INTER, TOP_E = 16, 64, 4
ROUTE = 2.5
DI, DS, DCONV, DTR = 256, 16, 4, 8
NE2 = 8
CAP = B * L // NE2
EPS = 1e-5
LOG1P = (2.000000007877749, 0.6666631593507906, 0.4002485372356232, 0.2796141883332212, 0.28174657270344106)


class Signal:

    def __init__(self, sem, per, unit=1, first=0):
        self.sem, self.per, self.unit, self.first, self.k = sem, per, unit, first, 0

    def up(self):
        self.k = self.k % self.per + 1
        return self.unit

    def now(self, b):
        return self.at(b, self.k)

    def at(self, b, k):
        row, ahead = b if isinstance(b, tuple) else (b, 0)
        return row * (self.per * self.unit) + (self.first + k + ahead * self.per) * self.unit


def index_width(i):
    return P * i + P - LW


def first_width(i):
    return TOPK if i == 0 else LW


def build(nc, x, w128, w64, consts, setup_c, out, at128, at64, atc, ats):
    with ExitStack() as ctx:
        def sb(name, shape, dt=F32):
            return ctx.enter_context(nc.sbuf_tensor(name, shape, dt))

        def semaphore(name):
            return ctx.enter_context(nc.semaphore(name))

        def signal(name, per, unit=1, first=0):
            s = Signal(semaphore(name), per, unit, first)
            signals[name] = s
            return s

        signals = {}
        bank = [ctx.enter_context(nc.psum_tensor(f"bank{n}", [P, 512], F32)) for n in range(8)]

        W = sb("W", [P, w128.shape[1]])
        CO = sb("CO", [P, consts.shape[1]])
        big = sb("big", [P, 4, 2, L])
        flat = big[:, :, :, :].rearrange("p k j t -> p (k j t)")
        n_c, n_w = setup_c.shape[1], w64.shape[1]
        CS, WH = flat[:, 0:n_c], flat[0:64, n_c:n_c + n_w]

        def piece(t, table, name):
            off, rows, shape = table[name]
            ap = t[0:rows, off:off + int(np.prod(shape))]
            if len(shape) == 2:
                ap = ap.rearrange("p (a c) -> p a c", a=shape[0])
            if len(shape) == 3:
                ap = ap.rearrange("p (a b c) -> p a b c", a=shape[0], b=shape[1])
            return ap

        def w(name):
            return piece(W, at128, name)

        def wh(name):
            return piece(WH, at64, name)

        def co(name):
            return piece(CO, atc, name)

        def once(name):
            return piece(CS, ats, name)

        ident = co("ident")
        ident_bf = sb("ident_bf", [P, P], BF16)
        ident_h = sb("ident_h", [P, P], F16)
        tri_bf = sb("tri_bf", [P, P], BF16)
        ones_bf = sb("ones_bf", [P, P], BF16)
        lmask_bf = sb("lmask_bf", [P, 2, 224], BF16)
        WQ = sb("WQ", [64, 2, 256])
        WVO = sb("WVO", [P, 2, D])
        trig = sb("trig", [P, 2, 9, HALF])
        dl = sb("dl", [P, 8, HALF])
        Aneg = sb("Aneg", [P, 2, DS])
        dtb2 = sb("dtb2", [P, 2])
        one = sb("one", [P, 1])
        two = sb("two", [P, 1])
        eps = sb("eps", [P, 1])
        cum = sb("cum", [P, NE2])
        cum_bf = sb("cum_bf", [P, NE2], BF16)
        X = sb("X", [P, NT, D])
        XT = sb("XT", [P, L])
        KI = sb("KI", [P, L])
        KT = sb("KT", [P, L])
        QI = sb("QI", [P, 2, L])
        CQ = sb("CQ", [64, L])
        table = sb("table", [P, NT, 64])
        tparts = sb("tparts", [P, NT, 3, 64], BF16)
        prev_c = sb("prev_c", [64, 3, DC])
        relu_s = sb("relu_s", [P, NIH, 448])
        score = sb("score", [P, 2, 448])
        tres = score[:, :, :].rearrange("p a c -> p (a c)")[:, 0:512].rearrange("p (s n c) -> p s n c", s=2, n=NT)
        top = sb("top", [P, NREM])
        idx = sb("idx", [P, NREM], U32)
        idxT = sb("idxT", [P, NCOL], U32)
        idxh = sb("idxh", [P, NCOL], F16)
        q_e = sb("q_e", [P, 3, 256])
        kr_e = q_e[:, :, 0:NT * DR].rearrange("p s (n c) -> p s n c", n=NT)
        SR = sb("SR", [P, 8, 32])
        SRd = sb("SRd", [P, 8, 32])
        PR = sb("PR", [P, 8, 32])
        PT = sb("PT", [P, 8, 32])
        muq, qr_c, qr_s = SR, SRd, PT
        krot = PR[:, :, :].rearrange("p (s n) c -> p s n c", s=2)
        QA = sb("QA", [P, NH, 2, 32])
        QB = sb("QB", [P, NH, 2, 32])
        KD = QB[:, :, :, :].rearrange("p (n a) k c -> p n a (k c)", n=NT)
        QBT = sb("QBT", [P, 4, P])
        QT = sb("QT", [P, NH, 2, NCOL])
        QBD = sb("QBD", [P, NCOL, 2, 4, NH])
        ib = sb("ib", [P, 2, 4 * P], F16)
        onehot = sb("onehot", [P, 2, NT, 4 * P], BF16)
        QAT = onehot[:, 1, :, :].rearrange("p n c -> p (n c)").bitcast(F32)[:, 0:4 * P].rearrange("p (a c) -> p a c", a=4)
        G = sb("G", [P, NCOL, 64])
        g_c = sb("g_c", [P, 8, DR])
        g_s = sb("g_s", [P, 2, 8, DR])
        GR = sb("GR", [P, 8, DR])
        GT = sb("GT", [P, 2, NCOL, 32])
        PBD = sb("PBD", [P, 8, 4, 4, NH])
        RO = sb("RO", [P, 8, 34])
        RB = sb("RB", [P, NH, 34])
        PL = relu_s[:, 0:2, :].rearrange("p a (b c) -> p (a b) c", b=2)
        PLT1 = sb("PLT1", [TOPK, 4, P])
        PLT2 = sb("PLT2", [P, 4, P])
        ml = sb("ml", [P, NH])
        nml = sb("nml", [P, NH])
        ll = sb("ll", [P, NH])
        mj = sb("mj", [P, NH])
        dm = sb("dm", [P, 2, NH])
        em = sb("em", [P, 2, NH])
        den = sb("den", [P, 4, NH])
        fac = sb("fac", [P, 2, NH])
        On = sb("On", [P, 2, NH, DC])
        OT = sb("OT", [P, 2, P])
        Y1 = sb("Y1", [P, NT, D])
        stats = sb("stats", [P, NT, 6])
        mv = sb("mv", [P, NT, 2])
        lnv = sb("lnv", [P, NT])
        rstd = sb("rstd", [P, NT])
        XR = sb("XR", [P, NT, D])
        XRT = sb("XRT", [P, L])
        Y2 = sb("Y2", [P, NT, D])
        r8 = sb("r8", [P, NT, 8])
        ri = sb("ri", [P, NT, 8], U32)
        rif = sb("rif", [P, NT, 8])
        rs = sb("rs", [P, 2, NT])
        CT = sb("CT", [NE, L])
        CB = big[:, :, :, :].rearrange("p k j t -> p (k j) t")
        SG = sb("SG", [P, 2, L])
        HT = sb("HT", [P, L])
        rt = HT[:, 0:6 * NT * NE].rearrange("p (k n e) -> p k n e", k=6, n=NT)
        req = SG[:, 1, 0:NT * NE * TOP_E].rearrange("p (n e k) -> p n e k", n=NT, e=NE)
        XP = sb("XP", [P, 2, L + DCONV - 1])
        SZ = sb("SZ", [P, 2, L])
        CV = sb("CV", [P, 2, L])
        U = sb("U", [P, 2, L])
        XD = sb("XD", [DTR + 2 * DS, L])
        DEL = sb("DEL", [P, 2, L])
        DU = sb("DU", [P, 2, L])
        dA, dBu = big[:, 0:2, :, :], big[:, 2:4, :, :]
        dt_x, dt_a, dt_b, dt_c = (big[:, k, :, :] for k in range(4))
        ez, eu = big[:, 0, :, :], big[:, 1, :, :]
        BC = sb("BC", [P, 2, 2, L])
        hs = SG
        hC = (XP[:, :, DCONV - 1:], CV)
        YG = CV
        pr = sb("pr", [P, 4, NT, NE2])
        ps1 = sb("ps1", [P, 3, NT])
        mk = sb("mk", [P, NT, NE2])
        mk_bf = sb("mk_bf", [P, NT, NE2], BF16)
        keep = sb("keep", [P, NT, NE2])
        gate = sb("gate", [P, NT, NE2])
        csum = sb("csum", [P, NE2])
        SG_turn = (SG, G[:, 0:2 * L // 64, :].rearrange("p (k n) c -> p k (n c)", k=2))
        HT_turn = (HT[:, :], KI[:, :])
        gated = big[:, 0, :, :].rearrange("p j (e d) -> p (j e) d", e=4)
        gsum = big[:, 1, 0, 0:D]
        GTs = CT[0:NE2, :]
        OUT = CV[:, :, :].rearrange("p j t -> p (j t)")[:, 0:NT * D].rearrange("p (n d) -> p n d", n=NT)
        scr = nc.dram_tensor("rows_bounce", [2, P, NH * 34], F32, kind="Internal").ap()
        comb_rows = nc.dram_tensor("comb_rows", [NE, L], F32, kind="Internal").ap()
        bc_rows = nc.dram_tensor("bc_rows", [2 * DS, L], F32, kind="Internal").ap()

        s_load = semaphore("weights_loaded")
        s_later = semaphore("later_weights_loaded")
        set_v = Signal(semaphore("setup_vector"), SET_VEC)
        s_seta = semaphore("setup_scalar")
        s_setp = semaphore("setup_tensor")
        hold_dve, hold_pe = semaphore("hold_vector"), semaphore("hold_tensor")
        hold_pool, hold_sp = semaphore("hold_gpsimd"), semaphore("hold_sync")
        x_in = signal("x_in", 1, 16)
        x_copied = signal("x_copied", 1)
        attn_done = signal("attn_done", 1, first=1)
        rest_done = signal("rest_done", 1, first=1)
        out_stored = signal("out_stored", 1, 16, first=1)
        vec = signal("vector_step", PER["vec"])
        vec2 = signal("vector_step_rest", PER["vec2"])
        vec_k = signal("vector_step_keys", PER["vec_k"])
        act_s = signal("scalar_step", PER["act"])
        act_k = signal("scalar_step_keys", PER["act_k"])
        act2 = signal("scalar_step_rest", PER["act2"])
        xt_ps = signal("xt_in_psum", 1)
        xt_sb = signal("xt_in_sbuf", 1)
        proj_ps = signal("proj_in_psum", 4)
        proj_sb = signal("proj_in_sbuf", 4)
        kv_ps = signal("kv_in_psum", 1)
        kr_sp = signal("kr_logs_ready", 1)
        kv_in = signal("kv_dup_ready", 1)
        kt_ps = signal("kt_in_psum", 1)
        kt_sb = signal("kt_in_sbuf", 1)
        parts_ok = signal("table_parts_ready", 1)
        ix_ps = signal("index_scores_in_psum", 4 * NT)
        ix_relu = signal("index_relu_ready", 4 * NT)
        ix_used = signal("index_relu_used", 4 * NT)
        q_ps = signal("q_in_psum", NT)
        q_sp = signal("q_logs_ready", NT)
        q_rows = signal("q_rows_ready", NT)
        qT_ps = signal("qt_in_psum", NT + 1)
        qT_sb = signal("qt_in_sbuf", NT + 1)
        idx_ok = signal("idx_columns_ready", NT)
        ib_ps = signal("idx_spread_in_psum", 8 * NT)
        ib_sb = signal("idx_spread_in_sbuf", 8 * NT)
        oh_ok = signal("onehot_round_ready", 8 * NT)
        g_round = signal("rows_round_in_psum", 8 * NT)
        g_sb = signal("rows_in_sbuf", 4 * NT)
        g_sin = signal("rows_sin_ready", 4 * NT)
        g_rot = signal("rows_turned", 4 * NT)
        gt_ok = signal("picked_keys_ready", NT)
        sr_ps = signal("picked_scores_in_psum", NT)
        sr_d = signal("picked_scores_shifted", NT)
        pr_ok = signal("picked_probs_ready", NT)
        pbd_ok = signal("picked_probs_spread", NT)
        ro_ps = signal("picked_out_in_psum", NT)
        ro_sb = signal("picked_out_in_sbuf", NT)
        ro_st = signal("picked_out_stored", 16 * NT, 16)
        rb_in = signal("picked_out_back", NT, 16)
        sl_ps = signal("local_scores_in_psum", 2 * NT)
        ml_ok = signal("local_max_ready", 2 * NT)
        pl_ok = signal("local_probs_ready", 2 * NT)
        pt_ps = signal("local_probs_t_in_psum", 2 * NT)
        pt_sb = signal("local_probs_t_in_sbuf", 2 * NT)
        ol_ps = signal("local_out_in_psum", 2 * NT)
        dm_ok = signal("max_gaps_ready", NT)
        em_ok = signal("merge_weights_ready", NT)
        on_ok = signal("attn_rows_ready", NT)
        oT_ps = signal("attn_t_in_psum", NT)
        oT_sb = signal("attn_t_in_sbuf", NT)
        at_ps = signal("attn_out_in_psum", NT)
        at_used = signal("attn_out_added", NT)
        var_ok = signal("variances_ready", 4)
        rstd_ok = signal("rstd_ready", 4)
        ln_ok = signal("normed_rows_ready", 2)
        rT_ps = signal("rest_xt_in_psum", 3)
        rT_sb = signal("rest_xt_in_sbuf", 3)
        rl_ps = signal("router_logits_in_psum", 2)
        rl_e = signal("router_exp_ready", 1)
        comb_ok = signal("comb_ready", 1)
        ct_ps = signal("comb_t_in_psum", 1)
        ct_sb = signal("comb_t_in_sbuf", 1)
        ct_st = signal("comb_stored", 1, 16)
        cb_sb = signal("comb_spread", 2, 16)
        ga_ps = signal("gate_in_psum", 9)
        up_ps = signal("up_in_psum", 9)
        ga_used = signal("gate_used", 9)
        sl_ok = signal("gate_logs_ready", 9)
        sm_ok = signal("gate_log_sigmoid_ready", 9)
        sg_ok = signal("gate_sigmoid_ready", 9)
        hu_ok = signal("hidden_ready", 9)
        ht_ok = signal("hidden_scaled", 8)
        y_part = signal("expert_out_part", 9)
        xz_ps = signal("xz_in_psum", 4)
        xz_sb = signal("xz_in_sbuf", 2)
        zl_ok = signal("z_logs_ready", 2)
        zm_ok = signal("z_log_sigmoid_ready", 2)
        ze_ok = signal("z_sigmoid_ready", 2)
        sz_ok = signal("z_gate_ready", 2)
        cv_ok = signal("conv_ready", 2)
        ul_ok = signal("u_logs_ready", 2)
        um_ok = signal("u_log_sigmoid_ready", 2)
        ue_ok = signal("u_sigmoid_ready", 2)
        u_ok = signal("u_ready", 2)
        xd_ps = signal("xdbl_in_psum", 1)
        xd_sb = signal("xdbl_in_sbuf", 1)
        xd_st = signal("bc_rows_stored", 1, 16)
        dt_ps = signal("dt_in_psum", 2)
        dtx_ok = signal("dt_biased", 1)
        dt_sp = signal("dt_exp_ready", 1)
        del_ok = signal("delta_ready", 1)
        b_in = [signal(f"b_row_in_slot_{k}", DS // 2, 16) for k in range(2)]
        c_in = [signal(f"c_row_in_slot_{k}", DS // 2, 16) for k in range(2)]
        dA_ok = signal("decay_ready", 2 * DS)
        dBu_ok = signal("drive_ready", DS)
        scan_ok = signal("states_ready", DS)
        hC_ok = signal("readout_ready", DS)
        ysum = signal("readout_summed", 2 * DS)
        yg_ok = signal("gated_ready", 1)
        op_ps = signal("scan_out_in_psum", 1)
        pm_ok = signal("gate_shifted", 1)
        pe_ok = signal("gate_exp_ready", 1)
        mk_ok = signal("choice_ready", 1)
        loc_ps = signal("slots_in_psum", 1)
        gate_ok = signal("gates_ready", 1)
        gT_ps = signal("gates_t_in_psum", 1)
        gT_sb = signal("gates_t_in_sbuf", 1)
        bias_ps = signal("bias_in_psum", 1)
        e_ps = signal("top1_out_in_psum", 2 * NT)
        e_used = signal("top1_out_used", 2 * NT)

        def weave(first, second):
            live = [first, second]
            while live:
                for g in list(live):
                    if next(g, "end") == "end":
                        live.remove(g)

        def both(first, second):
            while True:
                ended = [next(g, "end") == "end" for g in (first, second)]
                if all(ended):
                    return
                yield

        def turn_of(alone, p):
            return p % 2 if alone else 0

        first_bank = (5, 0)

        def row_after(b):
            return (b, 1)

        def rows_loop(keys, tiles, merges, close, rest, fori):
            def attention(b, last=False):
                yield from tiles(b)
                yield from (merges(b) if last else both(merges(b), keys(row_after(b))))

            weave(keys(0), iter(()))
            weave(attention(0), iter(()))
            close(0)
            with fori(1, B - 1) as b:
                weave(attention(b), rest(b - 1))
                close(b)
            weave(attention(B - 1, last=True), rest(B - 2))
            close(B - 1)
            weave(rest(B - 1, alone=True), iter(()))

        block = ctx.enter_context(nc.Block())

        @block.sync
        def _(sp):
            def load(b):
                sp.dma_start(X[:, :, :], x[b].rearrange("(n p) d -> p n d", p=P)).then_inc(x_in.sem, x_in.up())

            def keys(b):
                for _ in range(KEY_PHASES):
                    yield

            def tiles(b, last=False):
                if not last:
                    sp.wait_ge(x_copied.sem, x_copied.at(b, 1))
                    sp.sem_inc(hold_sp, 1)
                    load(b + 1)
                for i in range(NT):
                    for _ in range(TILE_PHASES - 1):
                        yield
                    if i == 0:
                        sp.wait_ge(attn_done.sem, attn_done.at(b, 0))
                    sp.wait_ge(ro_sb.sem, ro_sb.at(b, i + 1))
                    to = scr[i % 2].rearrange("(b x a) (h e) -> a b h x e", b=4, a=4, h=NH)
                    for a in range(4):
                        for bb in range(4):
                            p0 = 32 * a + 8 * bb
                            sp.dma_start(to[a, bb], RO[p0:p0 + 8, :, :]).then_inc(ro_st.sem, ro_st.up())
                    sp.wait_ge(ro_st.sem, ro_st.at(b, 16 * (i + 1)))
                    if i >= 1:
                        sp.wait_ge(on_ok.sem, on_ok.at(b, i))
                    sp.dma_start(RB[:, :, :].rearrange("p h e -> p (h e)"), scr[i % 2]).then_inc(rb_in.sem, rb_in.up())
                    yield

            def merges(b):
                for _ in range(MERGE_PHASES):
                    yield

            def rest(b, alone=False):
                sp.wait_ge(rest_done.sem, rest_done.at(b, 0))
                for _ in range(ROUTE_PHASES - 1):
                    yield
                sp.wait_ge(ct_sb.sem, ct_sb.at(b, 1))
                sp.dma_start(comb_rows, CT[:, :]).then_inc(ct_st.sem, ct_st.up())
                sp.wait_ge(ct_st.sem, ct_st.at(b, 1))
                for e in range(2):
                    src = comb_rows.rearrange("(p e) t -> e p t", e=2)[e].unsqueeze(0).to_broadcast([64, NE // 2, L])
                    sp.dma_start(CB[64 * e:64 * e + 64, :, :], src).then_inc(cb_sb.sem, cb_sb.up())
                yield
                for _ in range(EXPERT_PHASES + NORM_PHASES + SCAN_IN_PHASES - 3):
                    yield
                sp.wait_ge(xd_sb.sem, xd_sb.at(b, 1))
                sp.dma_start(bc_rows, XD[DTR:DTR + 2 * DS, :]).then_inc(xd_st.sem, xd_st.up())
                sp.wait_ge(xd_st.sem, xd_st.at(b, 1))
                for n in range(DS):
                    if n == 2:
                        yield
                        yield
                        yield
                    if n >= 2:
                        sp.wait_ge(dBu_ok.sem, dBu_ok.at(b, n - 1))
                        sp.wait_ge(hC_ok.sem, hC_ok.at(b, n - 1))
                    for k in range(2):
                        src = bc_rows[k * DS + n:k * DS + n + 1, :].to_broadcast([P, L])
                        row_in = (b_in, c_in)[k][n % 2]
                        sp.dma_start(BC[:, n % 2, k, :], src).then_inc(row_in.sem, row_in.up())
                    if n >= 2:
                        yield
                for _ in range(2 + SCAN_OUT_PHASES + NORM_PHASES + TOP1_PHASES):
                    yield
                sp.wait_ge(rest_done.sem, rest_done.at(b, 1))
                sp.dma_start(out[b].rearrange("(n p) d -> p n d", p=P), OUT).then_inc(out_stored.sem, out_stored.up())

            load(0)
            sp.dma_start(CO[:, :], consts).then_inc(s_load, 16)
            sp.dma_start(CS, setup_c).then_inc(s_load, 16)
            later = at128["gate"][0]
            sp.dma_start(WH, w64).then_inc(s_load, 16)
            sp.dma_start(W[:, 0:later], w128[:, 0:later]).then_inc(s_load, 16)
            sp.sem_inc(out_stored.sem, 16)
            sp.dma_start(W[:, later:], w128[:, later:]).then_inc(s_later, 16)
            tiles_last = tiles(B - 1, last=True)
            rows_loop(keys, lambda b: tiles_last if isinstance(b, int) and b == B - 1 else tiles(b), merges,
                      lambda b: None, rest, sp.Fori)
            sp.wait_ge(out_stored.sem, 16 * (B + 1))

        @block.tensor
        def _(pe):
            mm = pe.matmul

            def turn(o, i_, k=P):
                return pe.transpose(o, i_, ident[0:k, 0:k])

            def merge_turn(b, i):
                pe.wait_ge(on_ok.sem, on_ok.at(b, i + 1))
                pe.sem_inc(hold_pe, 1)
                for k in range(2):
                    m = turn(bank[4][:, 256 + k * P:256 + (k + 1) * P],
                             On[:, 0, 4 * k:4 * k + 4, :].rearrange("p h c -> p (h c)"))
                m.then_inc(oT_ps.sem, oT_ps.up())

            def merge_out(b, i):
                pe.wait_ge(oT_sb.sem, oT_sb.at(b, i + 1))
                for k in range(2):
                    m = mm(bank[4][:, 0:P], OT[:, k, :], WVO[:, k, :], start=(k == 0), stop=(k == 1))
                m.then_inc(at_ps.sem, at_ps.up())

            def keys(b):

                pe.wait_ge(x_in.sem, x_in.at(b, 1))
                pe.sem_inc(hold_pe, 1)
                for i in range(NT):
                    m = turn(bank[0][:, i * P:(i + 1) * P], X[:, i, :])
                m.then_inc(xt_ps.sem, xt_ps.up())
                yield
                pe.wait_ge(xt_sb.sem, xt_sb.at(b, 1))
                if isinstance(b, tuple):
                    pe.wait_ge(ro_sb.sem, ro_sb.at(b[0], NT))
                    pe.wait_ge(g_sb.sem, g_sb.at(b[0], 4 * NT))
                mm(bank[1][:, :], w("wk2"), XT[:, :], start=True, stop=True).then_inc(proj_ps.sem, proj_ps.up())
                mm(bank[2][:, :], w("wq")[:, 0:P], XT[:, :], start=True, stop=True).then_inc(proj_ps.sem, proj_ps.up())
                mm(bank[3][:, :], w("wq")[:, P:2 * P], XT[:, :], start=True, stop=True).then_inc(proj_ps.sem, proj_ps.up())
                pe.wait_ge(proj_sb.sem, proj_sb.at(b, 1))
                mm(bank[1][0:64, :], w("dq"), XT[:, :], start=True, stop=True).then_inc(proj_ps.sem, proj_ps.up())
                for i in range(NT):
                    mm(bank[0][:, i * 64:(i + 1) * 64], XT[:, i * P:(i + 1) * P], w("kv"), start=True, stop=True)
                for i in range(1, NT):
                    m = mm(bank[0][0:64, 256 + 32 * i:288 + 32 * i], XT[:, i * P - 64:i * P], w("kv")[:, 0:DC],
                           start=True, stop=True)
                m.then_inc(kv_ps.sem, kv_ps.up())
                yield
                pe.wait_ge(kv_in.sem, kv_in.at(b, 1))
                pe.wait_ge(proj_sb.sem, proj_sb.at(b, 4))
                pe.sem_inc(hold_pe, 1)
                for i in range(NT):
                    m = turn(bank[1][:, i * P:(i + 1) * P], KD[:, i, :, :].rearrange("p a c -> p (a c)"))
                m.then_inc(kt_ps.sem, kt_ps.up())
                yield

            def tiles(b):

                for i in range(NT):
                    Wi, W0 = index_width(i), first_width(i)
                    c0 = 96 - W0
                    if i == 0:
                        pe.wait_ge(kt_sb.sem, kt_sb.at(b, 1))
                    else:
                        pe.wait_ge(ro_sb.sem, ro_sb.at(b, i))
                        pe.wait_ge(g_sb.sem, g_sb.at(b, 4 * i))
                    for h in range(NIH):
                        o = 64 * (h % 2)
                        mm(bank[h][:, 0:Wi], QI[o:o + 64, h // 2, i * P:(i + 1) * P], KI[o:o + 64, 0:Wi],
                                      start=True, stop=True).then_inc(ix_ps.sem, ix_ps.up())
                    pe.wait_ge(ix_relu.sem, ix_relu.at(b, 4 * i + 1))
                    mm(bank[0][:, :], CQ[:, i * P:(i + 1) * P], WQ[:, :, :].rearrange("p a c -> p (a c)"),
                                 start=True, stop=True).then_inc(q_ps.sem, q_ps.up())
                    yield
                    yield
                    pe.wait_ge(q_rows.sem, q_rows.at(b, i + 1))
                    pe.wait_ge(ix_relu.sem, ix_relu.at(b, 4 * i + 4))
                    pe.sem_inc(hold_pe, 1)
                    for p in range(4):
                        m = turn(bank[2][:, p * P:(p + 1) * P],
                                 QB[:, 2 * p:2 * p + 2, :, :].rearrange("p h k c -> p (h k c)"))
                    m.then_inc(qT_ps.sem, qT_ps.up())
                    if i == 0:
                        for p in range(4):
                            m = turn(bank[3][:, p * P:(p + 1) * P],
                                     QA[:, 2 * p:2 * p + 2, :, :].rearrange("p h k c -> p (h k c)"))
                        m.then_inc(qT_ps.sem, qT_ps.up())
                    yield

                    def local_scores(g):
                        for hh in range(4):
                            h = 4 * g + hh
                            o = 64 * (h % 2)
                            sc = bank[2 + hh % 2][:, 256 * (hh // 2):256 * (hh // 2) + 224]
                            mm(sc[:, c0:224], ident_bf[:, :], lmask_bf[:, min(i, 1), c0:224], start=True, stop=False)
                            if i == 0:
                                mm(sc[:, 0:96], QAT[o:o + 64, h // 2, :], KT[o:o + 64, 0:96], start=False, stop=True)
                                m = mm(sc[:, 96:224], QBT[o:o + 64, h // 2, :], KT[o:o + 64, 0:P],
                                       start=False, stop=True, skip_group_check=True)
                            else:
                                m = mm(sc[:, c0:224], QBT[o:o + 64, h // 2, :], KT[o:o + 64, i * P - 64:(i + 1) * P],
                                       start=False, stop=True)
                        m.then_inc(sl_ps.sem, sl_ps.up())

                    def local_turn(g):
                        pe.wait_ge(pl_ok.sem, pl_ok.at(b, 2 * i + g + 1))
                        if g == 1:
                            pe.wait_ge(pt_sb.sem, pt_sb.at(b, 2 * i + 1))
                        pe.sem_inc(hold_pe, 1)
                        for hh in range(4):
                            turn(bank[0][0:W0, hh * P:(hh + 1) * P], PL[:, hh, c0:96])
                        for hh in range(4):
                            m = turn(bank[1][:, hh * P:(hh + 1) * P], PL[:, hh, 96:224])
                        m.then_inc(pt_ps.sem, pt_ps.up())

                    def local_out(g):
                        pe.wait_ge(pt_sb.sem, pt_sb.at(b, 2 * i + g + 1))
                        if g == 0:
                            free = at_used if i >= 1 else attn_done
                            pe.wait_ge(free.sem, free.at(b, i))
                        pe.sem_inc(hold_pe, 1)
                        for hh in range(4):
                            h = 4 * g + hh
                            first = table[0:W0, 0, 0:DC] if i == 0 else prev_c[:, i - 1, :]
                            mm(bank[4][:, h * DC:(h + 1) * DC], PLT1[0:W0, hh, :], first, start=True, stop=False)
                            m = mm(bank[4][:, h * DC:(h + 1) * DC], PLT2[:, hh, :], table[:, i, 0:DC],
                                   start=False, stop=True)
                        m.then_inc(ol_ps.sem, ol_ps.up())

                    pe.wait_ge(qT_sb.sem, qT_sb.at(b, i + 2))
                    local_scores(0)
                    yield
                    if i >= 1:
                        merge_turn(b, i - 1)
                    local_turn(0)
                    local_scores(1)
                    if i >= 1:
                        merge_out(b, i - 1)
                    yield
                    local_out(0)
                    local_turn(1)
                    yield

                    def spread(r):
                        if r < 2:
                            pe.wait_ge(pt_sb.sem, pt_sb.at(b, 2 * i + 2))
                            pe.wait_ge(idx_ok.sem, idx_ok.at(b, i + 1))
                        else:
                            pe.wait_ge(ib_sb.sem, ib_sb.at(b, 8 * i + r - 1))
                        for q in range(4):
                            t = 4 * r + q
                            m = mm(bank[r % 2][:, q * P:(q + 1) * P], idxh[:, t:t + 1].to_broadcast([P, P]),
                                   ident_h[:, :], start=True, stop=True)
                        m.then_inc(ib_ps.sem, ib_ps.up())

                    def pick(r):
                        c = r // 2
                        pe.wait_ge(oh_ok.sem, oh_ok.at(b, 8 * i + r + 1))
                        if r % 2 == 0:
                            if c >= 2:
                                pe.wait_ge(g_sb.sem, g_sb.at(b, 4 * i + c - 1))
                            else:
                                pe.wait_ge(pl_ok.sem, pl_ok.at(b, 2 * i + 2))
                        for q in range(4):
                            for kt in range(i + 1):
                                kk = 64 if kt == i else P
                                for part in range(3):
                                    m = mm(bank[2 + c % 2][:, (4 * (r % 2) + q) * 64:(4 * (r % 2) + q + 1) * 64],
                                           onehot[0:kk, r % 2, kt, q * P:(q + 1) * P],
                                           tparts[0:kk, kt, part, :], start=(kt == 0 and part == 0),
                                           stop=(kt == i and part == 2))
                        m.then_inc(g_round.sem, g_round.up())

                    spread(0)
                    local_out(1)
                    spread(1)
                    yield
                    if i == 0:
                        pe.wait_ge(parts_ok.sem, parts_ok.at(b, 1))
                    for c in range(4):
                        pick(2 * c)
                        if c < 3:
                            spread(2 * c + 2)
                        pick(2 * c + 1)
                        if c < 3:
                            spread(2 * c + 3)
                        yield
                    pe.wait_ge(gt_ok.sem, gt_ok.at(b, i + 1))
                    pe.wait_ge(ib_sb.sem, ib_sb.at(b, 8 * i + 8))
                    pe.sem_inc(hold_pe, 1)
                    for t in range(NCOL):
                        xx, a = t // 4, t % 4
                        for kind in range(2):
                            m = mm(bank[0][32 * a:32 * a + 32, 32 * xx:32 * xx + 32],
                                   QBD[:, t, kind, :, :].rearrange("p b h -> p (b h)"), GT[:, kind, t, :],
                                   start=(kind == 0), stop=(kind == 1))
                    m.then_inc(sr_ps.sem, sr_ps.up())
                    yield
                    yield
                    pe.wait_ge(pbd_ok.sem, pbd_ok.at(b, i + 1))
                    pe.sem_inc(hold_pe, 1)
                    for t in range(NCOL):
                        xx, a = t // 4, t % 4
                        m = mm(bank[1][32 * a:32 * a + 32, 32 * xx:32 * xx + 32],
                               PBD[:, xx, a, :, :].rearrange("p b h -> p (b h)"), G[:, t, 0:DC], start=True, stop=True)
                    m.then_inc(ro_ps.sem, ro_ps.up())
                    yield

            def merges(b):
                yield
                merge_turn(b, NT - 1)
                merge_out(b, NT - 1)
                yield

            def close(b):
                pass

            def turn_rows(b, k):
                if k > 1:
                    pe.wait_ge(ln_ok.sem, ln_ok.at(b, k - 1))
                else:
                    pe.wait_ge(attn_done.sem, attn_done.at(b, 1))
                pe.sem_inc(hold_pe, 1)
                for i in range(NT):
                    m = turn(bank[5][:, i * P:(i + 1) * P], XR[:, i, :])
                m.then_inc(rT_ps.sem, rT_ps.up())

            def rest(b, alone=False):

                pe.wait_ge(s_later, 16)
                pe.wait_ge(rest_done.sem, rest_done.at(b, 0))
                turn_rows(b, 1)
                pe.wait_ge(rT_sb.sem, rT_sb.at(b, 1))
                for i in range(NT):
                    m = mm(bank[7][:, i * NE:(i + 1) * NE], XRT[:, i * P:(i + 1) * P], w("gate"), start=True, stop=True)
                m.then_inc(rl_ps.sem, rl_ps.up())
                yield
                pe.wait_ge(comb_ok.sem, comb_ok.at(b, 1))
                pe.sem_inc(hold_pe, 1)
                for i in range(NT):
                    m = turn(bank[7][0:NE, i * P:(i + 1) * P], rt[:, 5, i, :])
                m.then_inc(ct_ps.sem, ct_ps.up())
                yield

                def second(p):
                    free = ht_ok if p < 8 else hu_ok
                    pe.wait_ge(free.sem, free.at(b, p + 1))
                    kk = P if p < 8 else 64
                    wt = w("w2")[:, p, :] if p < 8 else w("w2s")[0:64, :]
                    pe.sem_inc(hold_pe, 1)
                    for i in range(NT):
                        m = mm(bank[7][:, i * P:(i + 1) * P], HT_turn[turn_of(alone, p)][0:kk, i * P:(i + 1) * P], wt,
                               start=(p == 0 and i == 0), stop=(p == 8), skip_group_check=True)
                    m.then_inc(y_part.sem, y_part.up())

                for p in range(9):
                    pe.wait_ge(ct_sb.sem, ct_sb.at(b, 1))
                    if p >= 1 + alone:
                        pe.wait_ge(ga_used.sem, ga_used.at(b, p - alone))
                    rows = P if p < 8 else 64
                    k0 = first_bank[turn_of(alone, p)]
                    wg = w("w1g")[:, p, :] if p < 8 else w("w1sg")
                    wu = w("w1u")[:, p, :] if p < 8 else w("w1su")
                    mm(bank[k0][0:rows, :], wg, XRT[:, :], start=True, stop=True).then_inc(ga_ps.sem, ga_ps.up())
                    if p >= 1 + alone:
                        pe.wait_ge(hu_ok.sem, hu_ok.at(b, p - alone))
                    mm(bank[k0 + 1][0:rows, :], wu, XRT[:, :], start=True, stop=True).then_inc(up_ps.sem, up_ps.up())
                    yield
                    if p >= 1:
                        second(p - 1)
                    yield
                second(8)
                yield
                yield

                turn_rows(b, 2)
                yield
                pe.wait_ge(rT_sb.sem, rT_sb.at(b, 2))
                for k in range(2):
                    mm(bank[5 + k][:, :], w("inp")[:, k * P:(k + 1) * P], XRT[:, :], start=True, stop=True).then_inc(xz_ps.sem, xz_ps.up())
                yield
                for k in range(2, 4):
                    pe.wait_ge(xz_sb.sem, xz_sb.at(b, k - 1))
                    mm(bank[3 + k][:, :], w("inp")[:, k * P:(k + 1) * P], XRT[:, :], start=True, stop=True).then_inc(xz_ps.sem, xz_ps.up())
                yield
                yield
                yield
                pe.wait_ge(u_ok.sem, u_ok.at(b, 2))
                pe.sem_inc(hold_pe, 1)
                for j in range(2):
                    m = mm(bank[7][0:40, :], w("xp")[:, j, :], U[:, j, :], start=(j == 0), stop=(j == 1))
                m.then_inc(xd_ps.sem, xd_ps.up())
                yield
                pe.wait_ge(xd_sb.sem, xd_sb.at(b, 1))
                pe.wait_ge(sz_ok.sem, sz_ok.at(b, 2))
                pe.sem_inc(hold_pe, 1)
                for j in range(2):
                    mm(bank[5 + j][:, :], w("dtw")[0:DTR, j * P:(j + 1) * P], XD[0:DTR, :], start=True, stop=True).then_inc(dt_ps.sem, dt_ps.up())
                yield
                yield
                yield
                for n in range(DS + 1):
                    if n == 1:
                        pe.wait_ge(dtx_ok.sem, dtx_ok.at(b, 1))
                    if n >= 1:
                        pe.wait_ge(hC_ok.sem, hC_ok.at(b, n))
                        for j in range(2):
                            mm(bank[5 + j][:, :], ident, hC[(n - 1) % 2][:, j, :], start=(n == 1), stop=(n == DS)).then_inc(ysum.sem, ysum.up())
                    if n < DS:
                        yield
                yield
                pe.wait_ge(yg_ok.sem, yg_ok.at(b, 1))
                for i in range(NT):
                    for j in range(2):
                        m = mm(bank[7][:, i * P:(i + 1) * P], YG[:, j, i * P:(i + 1) * P], w("op")[:, j, :],
                               start=(j == 0), stop=(j == 1))
                m.then_inc(op_ps.sem, op_ps.up())
                yield

                turn_rows(b, 3)
                pe.wait_ge(rT_sb.sem, rT_sb.at(b, 3))
                for i in range(NT):
                    m = mm(bank[7][:, i * NE2:(i + 1) * NE2], XRT[:, i * P:(i + 1) * P], w("wg"), start=True, stop=True)
                m.then_inc(rl_ps.sem, rl_ps.up())
                yield
                yield
                pe.wait_ge(mk_ok.sem, mk_ok.at(b, 1))
                for i in range(NT):
                    o = bank[7][:, 64 + i * NE2:64 + (i + 1) * NE2]
                    mm(o, tri_bf[:, :], mk_bf[:, i, :], start=True, stop=False)
                    for k in range(i):
                        mm(o, ones_bf[:, :], mk_bf[:, k, :], start=False, stop=False)
                    m = mm(o, ones_bf[:, :], cum_bf[:, :], start=False, stop=True)
                m.then_inc(loc_ps.sem, loc_ps.up())
                yield
                pe.wait_ge(gate_ok.sem, gate_ok.at(b, 1))
                pe.sem_inc(hold_pe, 1)
                for i in range(NT):
                    m = turn(bank[5][0:NE2, i * P:(i + 1) * P], gate[:, i, :])
                m.then_inc(gT_ps.sem, gT_ps.up())
                yield
                pe.wait_ge(gT_sb.sem, gT_sb.at(b, 1))
                pe.sem_inc(hold_pe, 1)
                for i in range(NT):
                    m = mm(bank[7][:, i * P:(i + 1) * P], GTs[:, i * P:(i + 1) * P], w("eb")[0:NE2, :], start=True, stop=True)
                m.then_inc(bias_ps.sem, bias_ps.up())
                for i in range(NT):
                    for k in range(2):
                        if i >= 1:
                            pe.wait_ge(e_used.sem, e_used.at(b, 2 * i + k - 1))
                        mm(bank[5 + k][:, :], XRT[:, i * P:(i + 1) * P], w("ew")[:, k * 512:(k + 1) * 512],
                                     start=True, stop=True).then_inc(e_ps.sem, e_ps.up())
                    yield
                yield
                yield

            pe.wait_ge(s_load, 64)
            for h in range(NH):
                m = mm(bank[0][0:64, h * DC:(h + 1) * DC], wh("uqT")[:, h, :], wh("ukT")[:, h, :],
                       start=True, stop=True)
            m.then_inc(s_setp, 1)
            for h in range(NH):
                m = mm(bank[1][32 * (h % 4):32 * (h % 4) + 32, (h // 4) * D:(h // 4 + 1) * D],
                       wh("uvT")[:, h, :], wh("out")[:, h, :], start=True, stop=True)
            m.then_inc(s_setp, 1)
            pe.wait_ge(set_v.sem, SET_VEC)
            pe.wait_ge(s_seta, 3)
            rows_loop(keys, tiles, merges, close, rest, pe.Fori)

        @block.scalar
        def _(act):
            A = act.activation

            def softplus_logs(b, step, src, steps, done):
                A(steps[0], src, ACT.Abs).then_inc(step.sem, step.up())
                act.wait_ge(step.sem, step.at(b, step.k))
                A(steps[1], steps[0], ACT.Exp, scale=-1.0).then_inc(step.sem, step.up())
                act.wait_ge(step.sem, step.at(b, step.k))
                A(steps[2], steps[1], ACT.Ln, bias=one[:, :]).then_inc(done.sem, done.up())

            def keys(b):

                act.wait_ge(xt_ps.sem, xt_ps.at(b, 1))
                A(XT[:, :], bank[0][:, :], ACT.Copy).then_inc(xt_sb.sem, xt_sb.up())
                yield
                for k, dst in enumerate((KI[:, :], QI[:, 0, :], QI[:, 1, :], CQ[:, :])):
                    act.wait_ge(proj_ps.sem, proj_ps.at(b, k + 1))
                    src = bank[1][0:64, :] if k == 3 else bank[1 + k][:, :]
                    A(dst, src, ACT.Copy).then_inc(proj_sb.sem, proj_sb.up())
                act.wait_ge(kv_ps.sem, kv_ps.at(b, 1))
                kr = bank[0][:, 0:256].rearrange("p (n c) -> p n c", n=NT)[:, :, 32:64]
                softplus_logs(b, act_k, kr, [kr_e[:, s, :, :] for s in range(3)], kr_sp)
                yield
                act.wait_ge(kt_ps.sem, kt_ps.at(b, 1))
                A(KT[:, :], bank[1][:, :], ACT.Copy).then_inc(kt_sb.sem, kt_sb.up())
                yield

            def tiles(b):

                for i in range(NT):
                    Wi, W0 = index_width(i), first_width(i)
                    c0 = 96 - W0
                    for h in range(NIH):
                        act.wait_ge(ix_ps.sem, ix_ps.at(b, 4 * i + h + 1))
                        if i >= 1:
                            act.wait_ge(ix_used.sem, ix_used.at(b, 4 * i + h - 3))
                        A(relu_s[:, h, 0:Wi], bank[h][:, 0:Wi], ACT.Relu).then_inc(ix_relu.sem, ix_relu.up())
                    act.wait_ge(q_ps.sem, q_ps.at(b, i + 1))
                    if i >= 1:
                        act.wait_ge(q_rows.sem, q_rows.at(b, i))
                    softplus_logs(b, act_s, bank[0][:, 0:256], [q_e[:, s, :] for s in range(3)], q_sp)
                    yield
                    yield
                    if i >= 1:
                        act.wait_ge(dm_ok.sem, dm_ok.at(b, i))
                        A(em[:, :, :], dm[:, :, :], ACT.Exp, scale=SCALE).then_inc(em_ok.sem, em_ok.up())
                    act.wait_ge(qT_ps.sem, qT_ps.at(b, 1 if i == 0 else i + 2))
                    A(QBT[:, :, :].rearrange("p a c -> p (a c)"), bank[2][:, :], ACT.Copy).then_inc(qT_sb.sem, qT_sb.up())
                    if i == 0:
                        act.wait_ge(qT_ps.sem, qT_ps.at(b, 2))
                        A(QAT[:, :, :].rearrange("p a c -> p (a c)"), bank[3][:, :], ACT.Copy).then_inc(qT_sb.sem, qT_sb.up())
                    yield

                    def local_probs(g):
                        act.wait_ge(ml_ok.sem, ml_ok.at(b, 2 * i + g + 1))
                        if g == 1:
                            act.wait_ge(pt_ps.sem, pt_ps.at(b, 2 * i + 1))
                        for hh in range(4):
                            h = 4 * g + hh
                            sc = bank[2 + hh % 2][:, 256 * (hh // 2) + c0:256 * (hh // 2) + 224]
                            m = A(PL[:, hh, c0:224], sc, ACT.Exp, scale=SCALE, bias=nml[:, h:h + 1],
                                  accum_out=ll[:, h:h + 1])
                        m.then_inc(pl_ok.sem, pl_ok.up())

                    def local_keys(g):
                        act.wait_ge(pt_ps.sem, pt_ps.at(b, 2 * i + g + 1))
                        if g == 0 and i >= 1:
                            act.wait_ge(ol_ps.sem, ol_ps.at(b, 2 * i))
                        if g == 1:
                            act.wait_ge(ol_ps.sem, ol_ps.at(b, 2 * i + 1))
                        A(PLT1[0:W0, :, :].rearrange("p a c -> p (a c)"), bank[0][0:W0, :], ACT.Copy)
                        A(PLT2[:, :, :].rearrange("p a c -> p (a c)"), bank[1][:, :], ACT.Copy).then_inc(pt_sb.sem, pt_sb.up())

                    local_probs(0)
                    yield
                    if i >= 1:
                        act.wait_ge(oT_ps.sem, oT_ps.at(b, i))
                        A(OT[:, :, :].rearrange("p a c -> p (a c)"), bank[4][:, 256:512], ACT.Copy).then_inc(oT_sb.sem, oT_sb.up())
                    local_keys(0)
                    local_probs(1)
                    yield
                    local_keys(1)
                    yield

                    def spread(r):
                        act.wait_ge(ib_ps.sem, ib_ps.at(b, 8 * i + r + 1))
                        if r >= 2:
                            act.wait_ge(oh_ok.sem, oh_ok.at(b, 8 * i + r - 1))
                        A(ib[:, r % 2, :], bank[r % 2][:, :], ACT.Copy).then_inc(ib_sb.sem, ib_sb.up())

                    spread(0)
                    spread(1)
                    yield
                    for c in range(4):
                        if c < 3:
                            spread(2 * c + 2)
                            spread(2 * c + 3)
                        act.wait_ge(g_round.sem, g_round.at(b, 8 * i + 2 * c + 2))
                        if i >= 1 and c == 0:
                            act.wait_ge(ro_ps.sem, ro_ps.at(b, i))
                        A(G[:, 8 * c:8 * c + 8, :].rearrange("p a c -> p (a c)"), bank[2 + c % 2][:, :], ACT.Copy).then_inc(g_sb.sem, g_sb.up())
                        yield
                    yield
                    act.wait_ge(sr_d.sem, sr_d.at(b, i + 1))
                    A(PR[:, :, :], SRd[:, :, :], ACT.Exp, scale=SCALE).then_inc(pr_ok.sem, pr_ok.up())
                    yield
                    act.wait_ge(ro_ps.sem, ro_ps.at(b, i + 1))
                    if i >= 1:
                        act.wait_ge(ro_st.sem, ro_st.at(b, 16 * i))
                    else:
                        act.wait_ge(attn_done.sem, attn_done.at(b, 0))
                    A(RO[:, :, 0:DC], bank[1][:, 0:256].rearrange("p (x c) -> p x c", x=8), ACT.Copy).then_inc(ro_sb.sem, ro_sb.up())
                    yield

            def merges(b):

                act.wait_ge(dm_ok.sem, dm_ok.at(b, NT))
                A(em[:, :, :], dm[:, :, :], ACT.Exp, scale=SCALE).then_inc(em_ok.sem, em_ok.up())
                yield
                act.wait_ge(oT_ps.sem, oT_ps.at(b, NT))
                A(OT[:, :, :].rearrange("p a c -> p (a c)"), bank[4][:, 256:512], ACT.Copy).then_inc(oT_sb.sem, oT_sb.up())
                yield

            def norm_scale(b, k):
                act.wait_ge(var_ok.sem, var_ok.at(b, k))
                A(lnv[:, :], mv[:, :, 1], ACT.Ln, bias=eps[:, :]).then_inc(act2.sem, act2.up())
                act.wait_ge(act2.sem, act2.at(b, act2.k))
                A(rstd[:, :], lnv[:, :], ACT.Exp, scale=-0.5).then_inc(rstd_ok.sem, rstd_ok.up())

            def close(b):
                norm_scale(b, 1)

            def rest(b, alone=False):

                def sigmoid_logs(src, dst, done):
                    A(dst, src, ACT.Abs).then_inc(act2.sem, act2.up())
                    act.wait_ge(act2.sem, act2.now(b))
                    A(dst, dst, ACT.Exp, scale=-1.0).then_inc(act2.sem, act2.up())
                    act.wait_ge(act2.sem, act2.now(b))
                    A(dst, dst, ACT.Ln, bias=one[:, :][0:dst.shape[0], :]).then_inc(done.sem, done.up())

                act.wait_ge(rest_done.sem, rest_done.at(b, 0))
                act.wait_ge(rT_ps.sem, rT_ps.at(b, 1))
                A(XRT[:, :], bank[5][:, :], ACT.Copy).then_inc(rT_sb.sem, rT_sb.up())
                act.wait_ge(rl_ps.sem, rl_ps.at(b, 1))
                A(rt[:, 0, :, :], bank[7][:, 0:NT * NE].rearrange("p (n e) -> p n e", n=NT), ACT.Exp, scale=-1.0).then_inc(rl_e.sem, rl_e.up())
                yield
                act.wait_ge(ct_ps.sem, ct_ps.at(b, 1))
                A(CT[:, :], bank[7][0:NE, :], ACT.Copy).then_inc(ct_sb.sem, ct_sb.up())
                yield
                for p in range(9):
                    rows = P if p < 8 else 64
                    SGp, k0 = SG_turn[turn_of(alone, p)], first_bank[turn_of(alone, p)]
                    act.wait_ge(ga_ps.sem, ga_ps.at(b, p + 1))
                    sigmoid_logs(bank[k0][0:rows, :], SGp[0:rows, 0, :], sl_ok)
                    yield
                    act.wait_ge(sm_ok.sem, sm_ok.at(b, p + 1))
                    if p >= 1 + alone:
                        act.wait_ge(ht_ok.sem, ht_ok.at(b, p - alone))
                    A(SGp[0:rows, 1, :], SGp[0:rows, 0, :], ACT.Exp).then_inc(sg_ok.sem, sg_ok.up())
                    yield
                yield
                norm_scale(b, 2)
                yield

                act.wait_ge(rT_ps.sem, rT_ps.at(b, 2))
                A(XRT[:, :], bank[5][:, :], ACT.Copy).then_inc(rT_sb.sem, rT_sb.up())
                yield
                for k in range(2):
                    act.wait_ge(xz_ps.sem, xz_ps.at(b, k + 1))
                    A(XP[:, k, DCONV - 1:], bank[5 + k][:, :], ACT.Copy).then_inc(xz_sb.sem, xz_sb.up())
                yield
                for k in range(2):
                    act.wait_ge(xz_ps.sem, xz_ps.at(b, k + 3))
                    sigmoid_logs(bank[5 + k][:, :], ez[:, k, :], zl_ok)
                yield
                for j in range(2):
                    act.wait_ge(cv_ok.sem, cv_ok.at(b, j + 1))
                    sigmoid_logs(CV[:, j, :], eu[:, j, :], ul_ok)
                yield
                for k in range(2):
                    act.wait_ge(zm_ok.sem, zm_ok.at(b, k + 1))
                    A(SZ[:, k, :], ez[:, k, :], ACT.Exp).then_inc(ze_ok.sem, ze_ok.up())
                yield
                for j in range(2):
                    act.wait_ge(um_ok.sem, um_ok.at(b, j + 1))
                    A(U[:, j, :], eu[:, j, :], ACT.Exp).then_inc(ue_ok.sem, ue_ok.up())
                yield
                act.wait_ge(xd_ps.sem, xd_ps.at(b, 1))
                A(XD[:, :], bank[7][0:40, :], ACT.Copy).then_inc(xd_sb.sem, xd_sb.up())
                yield
                act.wait_ge(dtx_ok.sem, dtx_ok.at(b, 1))
                A(dt_a, dt_x, ACT.Abs).then_inc(act2.sem, act2.up())
                act.wait_ge(act2.sem, act2.now(b))
                A(dt_b, dt_a, ACT.Exp, scale=-1.0).then_inc(act2.sem, act2.up())
                act.wait_ge(act2.sem, act2.now(b))
                A(dt_c, dt_b, ACT.Ln, bias=two[:, :]).then_inc(act2.sem, act2.up())
                act.wait_ge(act2.sem, act2.now(b))
                A(dt_c, dt_c, ACT.Exp, scale=-1.0).then_inc(dt_sp.sem, dt_sp.up())
                yield
                yield
                act.wait_ge(del_ok.sem, del_ok.at(b, 1))
                for n in range(DS):
                    for j in range(2):
                        if n >= 2:
                            act.wait_ge(scan_ok.sem, scan_ok.at(b, n - 1))
                        A(dA[:, n % 2, j, :], DEL[:, j, :], ACT.Exp, scale=Aneg[:, j, n:n + 1]).then_inc(dA_ok.sem, dA_ok.up())
                    if n >= 1:
                        yield
                yield
                yield
                norm_scale(b, 3)
                yield

                act.wait_ge(rT_ps.sem, rT_ps.at(b, 3))
                A(XRT[:, :], bank[5][:, :], ACT.Copy).then_inc(rT_sb.sem, rT_sb.up())
                yield
                act.wait_ge(pm_ok.sem, pm_ok.at(b, 1))
                A(pr[:, 1, :, :], pr[:, 0, :, :], ACT.Exp).then_inc(pe_ok.sem, pe_ok.up())
                yield
                yield
                act.wait_ge(gT_ps.sem, gT_ps.at(b, 1))
                A(GTs[:, :], bank[5][0:NE2, :], ACT.Copy).then_inc(gT_sb.sem, gT_sb.up())
                yield
                for i in range(NT):
                    yield
                norm_scale(b, 4)
                yield
                yield

            act.wait_ge(s_load, 64)
            A(dl[:, 0, :], w("rawd"), ACT.Exp, scale=-1.0).then_inc(s_seta, 1)
            A(Aneg[:, :, :].rearrange("p a c -> p (a c)"), w("alog").rearrange("p a c -> p (a c)"),
              ACT.Exp).then_inc(s_seta, 1)
            act.wait_ge(set_v.sem, SET_SIN)
            A(dl[:, 4, :], dl[:, 3, :], ACT.Sin)
            A(dl[:, 5, :], dl[:, 3, :], ACT.Sin, scale=0.5).then_inc(s_seta, 1)
            act.wait_ge(set_v.sem, SET_VEC)
            act.preload_act_table_set("natural_log_exp_and_others")

            @contextmanager
            def fori(first, end):
                with act.Fori(first, end) as b:
                    act.preload_act_table_set("natural_log_exp_and_others")
                    yield b
                act.preload_act_table_set("natural_log_exp_and_others")

            rows_loop(keys, tiles, merges, close, rest, fori)

        @block.gpsimd
        def _(pool):
            def keys(b):
                for _ in range(KEY_PHASES):
                    yield

            def tiles(b):

                pool.wait_ge(attn_done.sem, attn_done.at(b, 0))
                pool.wait_ge(x_in.sem, x_in.at(b, 1))
                pool.wait_ge(xt_ps.sem, xt_ps.at(b, 1))
                pool.sem_inc(hold_pool, 1)
                pool.tensor_copy(Y1[:, :, :], X[:, :, :]).then_inc(x_copied.sem, x_copied.up())
                for i in range(NT):
                    for _ in range(7):
                        yield
                    for c in range(4):
                        pool.wait_ge(g_sb.sem, g_sb.at(b, 4 * i + c + 1))
                        if 4 * i + c >= 2:
                            pool.wait_ge(g_rot.sem, g_rot.at(b, 4 * i + c - 1))
                        sn = trig[:, 1, 8, :].unsqueeze(1).to_broadcast([P, 8, HALF])
                        part = G[:, 8 * c:8 * c + 8, :]
                        pool.tensor_tensor(g_s[:, c % 2, :, 0:HALF], part[:, :, DC:DC + HALF], sn, ALU.mult)
                        pool.tensor_tensor(g_s[:, c % 2, :, HALF:DR], part[:, :, DC + HALF:64], sn, ALU.mult).then_inc(g_sin.sem, g_sin.up())
                        yield
                    for _ in range(TILE_PHASES - 11):
                        yield

            def merges(b):
                for _ in range(MERGE_PHASES):
                    yield

            def close(b):
                pass

            def rest(b, alone=False):

                pool.wait_ge(rest_done.sem, rest_done.at(b, 0))
                for _ in range(ROUTE_PHASES + 1):
                    yield
                for p in range(8):
                    pool.wait_ge(hu_ok.sem, hu_ok.at(b, p + 1))
                    if p >= 1 + alone:
                        pool.wait_ge(y_part.sem, y_part.at(b, p - alone))
                    pool.wait_ge(cb_sb.sem, cb_sb.at(b, 2))
                    pool.tensor_tensor(HT_turn[turn_of(alone, p)], SG_turn[turn_of(alone, p)][:, 1, :], CB[:, p, :], ALU.mult).then_inc(ht_ok.sem, ht_ok.up())
                    yield
                    yield
                for _ in range(EXPERT_PHASES - 17 + NORM_PHASES + SCAN_IN_PHASES):
                    yield
                for n in range(DS):
                    pool.wait_ge(del_ok.sem, del_ok.at(b, 1))
                    row_in = b_in[n % 2]
                    pool.wait_ge(row_in.sem, row_in.at(b, n // 2 + 1))
                    if n >= 2:
                        pool.wait_ge(scan_ok.sem, scan_ok.at(b, n - 1))
                    pool.tensor_tensor(dBu[:, n % 2, :, :], DU[:, :, :],
                                                   BC[:, n % 2, 0:1, :].to_broadcast([P, 2, L]), ALU.mult).then_inc(dBu_ok.sem, dBu_ok.up())
                    if n >= 1:
                        yield
                yield
                for _ in range(SCAN_OUT_PHASES + NORM_PHASES + TOP1_PHASES):
                    yield

            pool.wait_ge(set_v.sem, SET_VEC)
            pool.wait_ge(s_seta, 3)
            rows_loop(keys, tiles, merges, close, rest, pool.Fori)

        @block.vector
        def _(dve):
            TT, TS, STT, CP = dve.tensor_tensor, dve.tensor_scalar, dve.scalar_tensor_tensor, dve.tensor_copy

            def keys(b):

                yield
                yield
                if isinstance(b, tuple):
                    dve.wait_ge(ol_ps.sem, ol_ps.at(b[0], 2 * NT))
                dve.wait_ge(kv_ps.sem, kv_ps.at(b, 1))
                dve.wait_ge(proj_sb.sem, proj_sb.at(b, 4))
                dve.wait_ge(kr_sp.sem, kr_sp.at(b, 1))
                kv = bank[0][:, 0:256].rearrange("p (n c) -> p n c", n=NT)
                CP(table[:, :, 0:DC], kv[:, :, 0:DC])
                CP(prev_c[:, :, :], bank[0][0:64, 288:384].rearrange("p (n c) -> p n c", n=3))
                for k in range(2):
                    CP(KD[:, :, k, 0:DC], kv[:, :, 0:DC])
                STT(out=table[:, :, DC:64], in0=kv[:, :, DC:64], scalar=0.0, in1=kr_e[:, 2, :, :],
                         op0=ALU.max, op1=ALU.add).then_inc(vec_k.sem, vec_k.up())
                dve.wait_ge(vec_k.sem, vec_k.now(b))
                for s in range(2):
                    for hf in range(2):
                        m = TT(krot[:, s, :, HALF * hf:HALF * hf + HALF], table[:, :, DC + HALF * hf:DC + HALF * hf + HALF],
                               trig[:, s, 0:NT, :], ALU.mult)
                m.then_inc(vec_k.sem, vec_k.up())
                dve.wait_ge(vec_k.sem, vec_k.now(b))
                for k in range(2):
                    TT(KD[:, :, k, DC:DC + HALF], krot[:, 0, :, 0:HALF], krot[:, 1, :, HALF:DR], ALU.subtract)
                    m = TT(KD[:, :, k, DC + HALF:64], krot[:, 0, :, HALF:DR], krot[:, 1, :, 0:HALF], ALU.add)
                m.then_inc(kv_in.sem, kv_in.up())
                CP(tparts[:, :, 0, :], table[:, :, :]).then_inc(vec_k.sem, vec_k.up())
                dve.wait_ge(vec_k.sem, vec_k.now(b))
                TT(tres[:, 0, :, :], table[:, :, :], tparts[:, :, 0, :], ALU.subtract).then_inc(vec_k.sem, vec_k.up())
                dve.wait_ge(vec_k.sem, vec_k.now(b))
                CP(tparts[:, :, 1, :], tres[:, 0, :, :]).then_inc(vec_k.sem, vec_k.up())
                dve.wait_ge(vec_k.sem, vec_k.now(b))
                TT(tres[:, 1, :, :], tres[:, 0, :, :], tparts[:, :, 1, :], ALU.subtract).then_inc(vec_k.sem, vec_k.up())
                dve.wait_ge(vec_k.sem, vec_k.now(b))
                CP(tparts[:, :, 2, :], tres[:, 1, :, :]).then_inc(parts_ok.sem, parts_ok.up())
                dve.wait_ge(parts_ok.sem, parts_ok.now(b))
                yield

            def merge_a(b, i):

                dve.wait_ge(rb_in.sem, rb_in.at(b, i + 1))
                TT(mj[:, :], ml[:, :], RB[:, :, 32], ALU.max).then_inc(vec.sem, vec.up())
                dve.wait_ge(vec.sem, vec.now(b))
                TT(dm[:, 0, :], ml[:, :], mj[:, :], ALU.subtract)
                TT(dm[:, 1, :], RB[:, :, 32], mj[:, :], ALU.subtract).then_inc(dm_ok.sem, dm_ok.up())
                dve.wait_ge(dm_ok.sem, dm_ok.now(b))

            def merge_b(b, i):

                dve.wait_ge(em_ok.sem, em_ok.at(b, i + 1))
                dve.wait_ge(ol_ps.sem, ol_ps.at(b, 2 * i + 2))
                TT(den[:, 0, :], ll[:, :], em[:, 0, :], ALU.mult)
                TT(den[:, 1, :], RB[:, :, 33], em[:, 1, :], ALU.mult).then_inc(vec.sem, vec.up())
                dve.wait_ge(vec.sem, vec.now(b))
                TT(den[:, 2, :], den[:, 0, :], den[:, 1, :], ALU.add).then_inc(vec.sem, vec.up())
                dve.wait_ge(vec.sem, vec.now(b))
                dve.reciprocal(den[:, 3, :], den[:, 2, :]).then_inc(vec.sem, vec.up())
                dve.wait_ge(vec.sem, vec.now(b))
                TT(fac[:, :, :], em[:, :, :], den[:, 3, :].unsqueeze(1).to_broadcast([P, 2, NH]), ALU.mult).then_inc(vec.sem, vec.up())
                dve.wait_ge(vec.sem, vec.now(b))
                TT(On[:, 0, :, :], bank[4][:, 0:256].rearrange("p (h c) -> p h c", h=NH),
                   fac[:, 0, :].unsqueeze(2).to_broadcast([P, NH, DC]), ALU.mult)
                TT(On[:, 1, :, :], RB[:, :, 0:DC], fac[:, 1, :].unsqueeze(2).to_broadcast([P, NH, DC]), ALU.mult).then_inc(vec.sem, vec.up())
                dve.wait_ge(vec.sem, vec.now(b))
                TT(On[:, 0, :, :], On[:, 0, :, :], On[:, 1, :, :], ALU.add).then_inc(on_ok.sem, on_ok.up())
                dve.wait_ge(on_ok.sem, on_ok.now(b))

            def merge_c(b, i):
                dve.wait_ge(at_ps.sem, at_ps.at(b, i + 1))
                dve.wait_ge(x_copied.sem, x_copied.at(b, 1))
                TT(Y1[:, i, :], bank[4][:, 0:P], Y1[:, i, :], ALU.add).then_inc(at_used.sem, at_used.up())

            def tiles(b):

                def rotate(dst, src, n, cos, sin, tc, tsn, done):
                    for s, tmp in ((cos, tc), (sin, tsn)):
                        m = TT(tmp.rearrange("p n (k c) -> p n k c", k=2), src.rearrange("p n (k c) -> p n k c", k=2),
                               s.unsqueeze(1).unsqueeze(1).to_broadcast([P, n, 2, HALF]), ALU.mult)
                    m.then_inc(vec.sem, vec.up())
                    dve.wait_ge(vec.sem, vec.now(b))
                    TT(dst[:, :, 0:HALF], tc[:, :, 0:HALF], tsn[:, :, HALF:DR], ALU.subtract)
                    TT(dst[:, :, HALF:DR], tc[:, :, HALF:DR], tsn[:, :, 0:HALF], ALU.add).then_inc(done.sem, done.up())
                    dve.wait_ge(done.sem, done.now(b))

                for i in range(NT):
                    Wi, W0 = index_width(i), first_width(i)
                    c0 = 96 - W0
                    dve.wait_ge(ix_relu.sem, ix_relu.at(b, 4 * i + 1))
                    TS(score[:, 0, 0:Wi], relu_s[:, 0, 0:Wi], w("idxw")[:, 0:1], None, ALU.mult).then_inc(ix_used.sem, ix_used.up())
                    dve.wait_ge(ix_used.sem, ix_used.now(b))
                    for h in range(1, NIH):
                        dve.wait_ge(ix_relu.sem, ix_relu.at(b, 4 * i + h + 1))
                        STT(out=score[:, 0, 0:Wi], in0=relu_s[:, h, 0:Wi], scalar=w("idxw")[:, h:h + 1],
                                 in1=score[:, 0, 0:Wi], op0=ALU.mult, op1=ALU.add).then_inc(ix_used.sem, ix_used.up())
                        dve.wait_ge(ix_used.sem, ix_used.now(b))
                    lo = 0 if i == 0 else Wi - P
                    mask = co("top0") if i == 0 else co("top1")
                    TT(score[:, 0, lo:Wi], score[:, 0, lo:Wi], mask, ALU.add).then_inc(vec.sem, vec.up())
                    dve.wait_ge(vec.sem, vec.now(b))
                    yield
                    dve.wait_ge(q_sp.sem, q_sp.at(b, i + 1))
                    STT(out=muq[:, :, :].rearrange("p h c -> p (h c)"), in0=bank[0][:, 0:256], scalar=0.0,
                             in1=q_e[:, 2, :], op0=ALU.max, op1=ALU.add).then_inc(vec.sem, vec.up())
                    dve.wait_ge(vec.sem, vec.now(b))
                    CP(QA[:, :, 0, :], bank[0][:, 256:512].rearrange("p (h c) -> p h c", h=NH))
                    CP(QB[:, :, 0, :], bank[0][:, 256:512].rearrange("p (h c) -> p h c", h=NH))
                    rotate(QA[:, :, 1, :], muq[:, :, :], NH, trig[:, 0, i, :], trig[:, 1, i, :], qr_c[:, :, :], qr_s[:, :, :], vec)
                    rotate(QB[:, :, 1, :], muq[:, :, :], NH, trig[:, 0, 4 + i, :], trig[:, 1, 4 + i, :], qr_c[:, :, :], qr_s[:, :, :], q_rows)
                    yield

                    def top8(r):
                        cur, nxt = score[:, r % 2, 0:Wi], score[:, (r + 1) % 2, 0:Wi]
                        dve.sem_inc(hold_dve, 1)
                        dve.max(top[:, 8 * r:8 * r + 8], cur).then_inc(vec.sem, vec.up())
                        dve.wait_ge(vec.sem, vec.now(b))
                        dve.sem_inc(hold_dve, 1)
                        m = dve.max_index(idx[:, 8 * r:8 * r + 8], top[:, 8 * r:8 * r + 8], cur)
                        if r < 3:
                            m = dve.match_replace(nxt, top[:, 8 * r:8 * r + 8], cur, NEG_TOP)
                        m.then_inc(vec.sem, vec.up())
                        dve.wait_ge(vec.sem, vec.now(b))

                    def local_max(g):
                        dve.wait_ge(sl_ps.sem, sl_ps.at(b, 2 * i + g + 1))
                        for k in range(2):
                            m = dve.tensor_reduce(ml[:, 4 * g + k:4 * g + k + 3:2],
                                                  bank[2 + k][:, :].rearrange("p (h c) -> p h c", h=2)[:, :, c0:224],
                                                  AX.X, ALU.max)
                        m.then_inc(vec.sem, vec.up())
                        dve.wait_ge(vec.sem, vec.now(b))
                        TS(nml[:, 4 * g:4 * g + 4], ml[:, 4 * g:4 * g + 4], -SCALE, None, ALU.mult).then_inc(ml_ok.sem, ml_ok.up())

                    if i >= 1:
                        merge_a(b, i - 1)
                    top8(0)
                    if i >= 1:
                        merge_b(b, i - 1)
                    yield
                    local_max(0)
                    top8(1)
                    top8(2)
                    yield
                    top8(3)
                    dve.transpose(idxT[:, :], idx[:, :]).then_inc(vec.sem, vec.up())
                    dve.wait_ge(vec.sem, vec.now(b))
                    CP(idxh[:, :], idxT[:, :]).then_inc(idx_ok.sem, idx_ok.up())
                    dve.wait_ge(idx_ok.sem, idx_ok.now(b))
                    local_max(1)
                    if i >= 1:
                        merge_c(b, i - 1)
                    yield
                    yield
                    dve.transpose(QT[:, :, :, :], QA[:, :, :, :]).then_inc(vec.sem, vec.up())
                    dve.wait_ge(vec.sem, vec.now(b))
                    for bb in range(4):
                        m = CP(QBD[32 * bb:32 * bb + 32, :, :, bb, :].rearrange("p t k h -> p k h t"),
                               QT[32 * bb:32 * bb + 32, :, :, :].rearrange("p h k t -> p k h t"))
                    yield

                    def onehots(r):
                        dve.wait_ge(ib_sb.sem, ib_sb.at(b, 8 * i + r + 1))
                        if 8 * i + r >= 2:
                            dve.wait_ge(g_round.sem, g_round.at(b, 8 * i + r - 1))
                        for kt in range(i + 1):
                            kk = 64 if kt == i else P
                            m = TS(onehot[0:kk, r % 2, kt, :], ib[0:kk, r % 2, :], co("pos")[0:kk, kt:kt + 1], None,
                                   ALU.is_equal)
                        m.then_inc(oh_ok.sem, oh_ok.up())

                    def turned(c):
                        dve.wait_ge(g_sb.sem, g_sb.at(b, 4 * i + c + 1))
                        part = G[:, 8 * c:8 * c + 8, :]
                        TT(g_c[:, :, :].rearrange("p x (k c) -> p x k c", k=2),
                                part[:, :, DC:64].rearrange("p x (k c) -> p x k c", k=2),
                                trig[:, 0, 8, :].unsqueeze(1).unsqueeze(1).to_broadcast([P, 8, 2, HALF]), ALU.mult).then_inc(vec.sem, vec.up())
                        dve.wait_ge(vec.sem, vec.now(b))
                        dve.wait_ge(g_sin.sem, g_sin.at(b, 4 * i + c + 1))
                        TT(GR[:, :, 0:HALF], g_c[:, :, 0:HALF], g_s[:, c % 2, :, HALF:DR], ALU.subtract)
                        TT(GR[:, :, HALF:DR], g_c[:, :, HALF:DR], g_s[:, c % 2, :, 0:HALF], ALU.add).then_inc(g_rot.sem, g_rot.up())
                        dve.wait_ge(g_rot.sem, g_rot.now(b))
                        dve.transpose(GT[:, 0, 8 * c:8 * c + 8, :], part[:, :, 0:DC])
                        done = gt_ok if c == 3 else vec
                        dve.transpose(GT[:, 1, 8 * c:8 * c + 8, :], GR[:, :, :]).then_inc(done.sem, done.up())
                        dve.wait_ge(done.sem, done.now(b))

                    for c in range(4):
                        onehots(2 * c)
                        onehots(2 * c + 1)
                        if c >= 1:
                            turned(c - 1)
                        yield
                    turned(3)
                    yield
                    dve.wait_ge(sr_ps.sem, sr_ps.at(b, i + 1))
                    sp_ = bank[0][:, 0:256].rearrange("p (x j) -> p x j", x=8)
                    if i == 0:
                        TT(SR[:, :, :], sp_, co("rmask"), ALU.add).then_inc(vec.sem, vec.up())
                        dve.wait_ge(vec.sem, vec.now(b))
                        sp_ = SR[:, :, :]
                    else:
                        dve.wait_ge(ro_st.sem, ro_st.at(b, 16 * i))
                    dve.tensor_reduce(RO[:, :, 32], sp_, AX.X, ALU.max).then_inc(vec.sem, vec.up())
                    dve.wait_ge(vec.sem, vec.now(b))
                    TT(SRd[:, :, :], sp_, RO[:, :, 32:33].to_broadcast([P, 8, 32]), ALU.subtract).then_inc(sr_d.sem, sr_d.up())
                    dve.wait_ge(sr_d.sem, sr_d.now(b))
                    yield
                    dve.wait_ge(pr_ok.sem, pr_ok.at(b, i + 1))
                    dve.tensor_reduce(RO[:, :, 33], PR[:, :, :], AX.X, ALU.add)
                    dve.transpose(PT[:, :, :], PR[:, :, :]).then_inc(vec.sem, vec.up())
                    dve.wait_ge(vec.sem, vec.now(b))
                    for a in range(4):
                        for bb in range(4):
                            m = CP(PBD[32 * bb:32 * bb + 32, :, a, bb, :], PT[32 * a:32 * a + 32, :, 8 * bb:8 * bb + 8])
                    m.then_inc(pbd_ok.sem, pbd_ok.up())
                    yield

            def merges(b):

                merge_a(b, NT - 1)
                yield
                merge_b(b, NT - 1)
                yield

            def norm_sums(b, Y):
                dve.sem_inc(hold_dve, 1)
                for i in range(NT):
                    m = dve.bn_stats(stats[:, i, :], Y[:, i, :])
                m.then_inc(vec2.sem, vec2.up())
                dve.wait_ge(vec2.sem, vec2.at(b, vec2.k))
                dve.sem_inc(hold_dve, 1)
                for i in range(NT):
                    m = dve.bn_aggr(mv[:, i, :], stats[:, i, :])
                m.then_inc(var_ok.sem, var_ok.up())
                dve.wait_ge(var_ok.sem, var_ok.at(b, var_ok.k))

            def norm_rows(b, Y, k, dst, done):
                dve.wait_ge(rstd_ok.sem, rstd_ok.at(b, k))
                for i in range(NT):
                    m = TS(dst[:, i, :], Y[:, i, :], mv[:, i, 0:1], rstd[:, i:i + 1], ALU.subtract, ALU.mult)
                m.then_inc(done.sem, done.up())
                dve.wait_ge(done.sem, done.at(b, done.k))

            def close(b):
                dve.wait_ge(at_ps.sem, at_ps.at(b, NT))
                dve.wait_ge(x_copied.sem, x_copied.at(b, 1))
                TT(Y1[:, NT - 1, :], bank[4][:, 0:P], Y1[:, NT - 1, :], ALU.add).then_inc(at_used.sem, at_used.up())
                dve.wait_ge(at_used.sem, at_used.at(b, NT))
                norm_sums(b, Y1)
                dve.wait_ge(rest_done.sem, rest_done.at(b, 0))
                norm_rows(b, Y1, 1, XR, attn_done)

            def rest(b, alone=False):

                dve.wait_ge(s_later, 16)
                dve.wait_ge(rest_done.sem, rest_done.at(b, 0))
                dve.wait_ge(rl_e.sem, rl_e.at(b, 1))
                TS(rt[:, 1, :, :], rt[:, 0, :, :], 1.0, None, ALU.add).then_inc(vec2.sem, vec2.up())
                dve.wait_ge(vec2.sem, vec2.now(b))
                dve.reciprocal(rt[:, 2, :, :], rt[:, 1, :, :]).then_inc(vec2.sem, vec2.up())
                dve.wait_ge(vec2.sem, vec2.now(b))
                TT(rt[:, 3, :, :], rt[:, 2, :, :], w("gb").unsqueeze(1).to_broadcast([P, NT, NE]), ALU.add).then_inc(vec2.sem, vec2.up())
                dve.wait_ge(vec2.sem, vec2.now(b))
                yield
                dve.sem_inc(hold_dve, 1)
                for i in range(NT):
                    m = dve.max(r8[:, i, :], rt[:, 3, i, :])
                m.then_inc(vec2.sem, vec2.up())
                dve.wait_ge(vec2.sem, vec2.now(b))
                dve.sem_inc(hold_dve, 1)
                for i in range(NT):
                    m = dve.max_index(ri[:, i, :], r8[:, i, :], rt[:, 3, i, :])
                m.then_inc(vec2.sem, vec2.up())
                dve.wait_ge(vec2.sem, vec2.now(b))
                CP(rif[:, :, :], ri[:, :, :]).then_inc(vec2.sem, vec2.up())
                dve.wait_ge(vec2.sem, vec2.now(b))
                for i in range(NT):
                    m = TT(req[:, i, :, :], co("iota")[:, 0:NE].unsqueeze(2).to_broadcast([P, NE, TOP_E]),
                           rif[:, i, 0:TOP_E].unsqueeze(1).to_broadcast([P, NE, TOP_E]), ALU.is_equal)
                m.then_inc(vec2.sem, vec2.up())
                dve.wait_ge(vec2.sem, vec2.now(b))
                dve.tensor_reduce(rt[:, 4, :, :], req[:, :, :, :], AX.X, ALU.add).then_inc(vec2.sem, vec2.up())
                dve.wait_ge(vec2.sem, vec2.now(b))
                TT(rt[:, 4, :, :], rt[:, 4, :, :], rt[:, 2, :, :], ALU.mult).then_inc(vec2.sem, vec2.up())
                dve.wait_ge(vec2.sem, vec2.now(b))
                dve.tensor_reduce(rs[:, 0, :], rt[:, 4, :, :], AX.X, ALU.add).then_inc(vec2.sem, vec2.up())
                dve.wait_ge(vec2.sem, vec2.now(b))
                dve.reciprocal(rs[:, 1, :], rs[:, 0, :]).then_inc(vec2.sem, vec2.up())
                dve.wait_ge(vec2.sem, vec2.now(b))
                STT(out=rt[:, 5, :, :], in0=rt[:, 4, :, :], scalar=ROUTE,
                         in1=rs[:, 1, :].unsqueeze(2).to_broadcast([P, NT, NE]), op0=ALU.mult, op1=ALU.mult).then_inc(comb_ok.sem, comb_ok.up())
                dve.wait_ge(comb_ok.sem, comb_ok.now(b))
                yield
                yield

                for p in range(9):
                    rows = P if p < 8 else 64
                    SGp, k0 = SG_turn[turn_of(alone, p)], first_bank[turn_of(alone, p)]
                    dve.wait_ge(sl_ok.sem, sl_ok.at(b, p + 1))
                    STT(out=SGp[0:rows, 0, :], in0=bank[k0][0:rows, :], scalar=0.0, in1=SGp[0:rows, 0, :],
                             op0=ALU.min, op1=ALU.subtract).then_inc(sm_ok.sem, sm_ok.up())
                    dve.wait_ge(sm_ok.sem, sm_ok.now(b))
                    yield
                    dve.wait_ge(sg_ok.sem, sg_ok.at(b, p + 1))
                    TT(SGp[0:rows, 1, :], SGp[0:rows, 1, :], bank[k0][0:rows, :], ALU.mult).then_inc(ga_used.sem, ga_used.up())
                    dve.wait_ge(ga_used.sem, ga_used.now(b))
                    dve.wait_ge(up_ps.sem, up_ps.at(b, p + 1))
                    if p == 8:
                        dve.wait_ge(y_part.sem, y_part.at(b, 8))
                    dst = SGp[:, 1, :] if p < 8 else HT[0:rows, :]
                    TT(dst, SGp[0:rows, 1, :], bank[k0 + 1][0:rows, :], ALU.mult).then_inc(hu_ok.sem, hu_ok.up())
                    dve.wait_ge(hu_ok.sem, hu_ok.now(b))
                    yield
                dve.wait_ge(y_part.sem, y_part.at(b, 9))
                TT(Y2[:, :, :], bank[7][:, :].rearrange("p (n d) -> p n d", n=NT), XR[:, :, :], ALU.add).then_inc(vec2.sem, vec2.up())
                dve.wait_ge(vec2.sem, vec2.now(b))
                norm_sums(b, Y2)
                yield
                norm_rows(b, Y2, 2, XR, ln_ok)
                yield

                yield
                dve.wait_ge(out_stored.sem, out_stored.at(b, 0))
                for j in range(2):
                    dve.wait_ge(xz_sb.sem, xz_sb.at(b, j + 1))
                    cw = w("cw")[:, j, :]
                    TS(CV[:, j, :], XP[:, j, 0:L], cw[:, 0:1], w("cb")[:, j:j + 1], ALU.mult, ALU.add).then_inc(vec2.sem, vec2.up())
                    dve.wait_ge(vec2.sem, vec2.now(b))
                    for k in range(1, DCONV):
                        done = cv_ok if k == DCONV - 1 else vec2
                        STT(out=CV[:, j, :], in0=XP[:, j, k:k + L], scalar=cw[:, k:k + 1], in1=CV[:, j, :],
                                 op0=ALU.mult, op1=ALU.add).then_inc(done.sem, done.up())
                        dve.wait_ge(done.sem, done.now(b))
                yield
                for j in range(2):
                    dve.wait_ge(zl_ok.sem, zl_ok.at(b, j + 1))
                    STT(out=ez[:, j, :], in0=bank[5 + j][:, :], scalar=0.0, in1=ez[:, j, :],
                                   op0=ALU.min, op1=ALU.subtract).then_inc(zm_ok.sem, zm_ok.up())
                yield
                for j in range(2):
                    dve.wait_ge(ul_ok.sem, ul_ok.at(b, j + 1))
                    STT(out=eu[:, j, :], in0=CV[:, j, :], scalar=0.0, in1=eu[:, j, :],
                                   op0=ALU.min, op1=ALU.subtract).then_inc(um_ok.sem, um_ok.up())
                for j in range(2):
                    dve.wait_ge(ze_ok.sem, ze_ok.at(b, j + 1))
                    TT(SZ[:, j, :], SZ[:, j, :], bank[5 + j][:, :], ALU.mult).then_inc(sz_ok.sem, sz_ok.up())
                yield
                for j in range(2):
                    dve.wait_ge(ue_ok.sem, ue_ok.at(b, j + 1))
                    TT(U[:, j, :], U[:, j, :], CV[:, j, :], ALU.mult).then_inc(u_ok.sem, u_ok.up())
                    dve.wait_ge(u_ok.sem, u_ok.now(b))
                yield
                for j in range(2):
                    dve.wait_ge(dt_ps.sem, dt_ps.at(b, j + 1))
                    m = TS(dt_x[:, j, :], bank[5 + j][:, :], dtb2[:, j:j + 1], None, ALU.add)
                m.then_inc(dtx_ok.sem, dtx_ok.up())
                dve.wait_ge(dtx_ok.sem, dtx_ok.now(b))
                yield
                dve.wait_ge(dt_sp.sem, dt_sp.at(b, 1))
                TT(dt_a, dt_b, dt_c, ALU.mult).then_inc(vec2.sem, vec2.up())
                dve.wait_ge(vec2.sem, vec2.now(b))
                TT(dt_c, dt_a, dt_a, ALU.mult).then_inc(vec2.sem, vec2.up())
                dve.wait_ge(vec2.sem, vec2.now(b))
                TS(dt_b, dt_c, LOG1P[4], None, ALU.mult).then_inc(vec2.sem, vec2.up())
                dve.wait_ge(vec2.sem, vec2.now(b))
                yield
                for c in LOG1P[3:0:-1]:
                    STT(out=dt_b, in0=dt_b, scalar=c, in1=dt_c, op0=ALU.add, op1=ALU.mult).then_inc(vec2.sem, vec2.up())
                    dve.wait_ge(vec2.sem, vec2.now(b))
                STT(out=dt_b, in0=dt_b, scalar=LOG1P[0], in1=dt_a, op0=ALU.add, op1=ALU.mult).then_inc(vec2.sem, vec2.up())
                dve.wait_ge(vec2.sem, vec2.now(b))
                STT(out=DEL[:, :, :], in0=dt_x, scalar=0.0, in1=dt_b, op0=ALU.max, op1=ALU.add).then_inc(vec2.sem, vec2.up())
                dve.wait_ge(vec2.sem, vec2.now(b))
                TT(DU[:, :, :], DEL[:, :, :], U[:, :, :], ALU.mult).then_inc(del_ok.sem, del_ok.up())
                dve.wait_ge(del_ok.sem, del_ok.now(b))
                yield
                for n in range(DS):
                    dve.wait_ge(dA_ok.sem, dA_ok.at(b, 2 * n + 2))
                    dve.wait_ge(dBu_ok.sem, dBu_ok.at(b, n + 1))
                    for j in range(2):
                        m = dve.tensor_tensor_scan(hs[:, j, :], dA[:, n % 2, j, :], dBu[:, n % 2, j, :], 0.0,
                                                   ALU.mult, ALU.add)
                    m.then_inc(scan_ok.sem, scan_ok.up())
                    dve.wait_ge(scan_ok.sem, scan_ok.now(b))
                    row_in = c_in[n % 2]
                    dve.wait_ge(row_in.sem, row_in.at(b, n // 2 + 1))
                    if n >= 2:
                        dve.wait_ge(ysum.sem, ysum.at(b, 2 * (n - 1)))
                    TT(hC[n % 2][:, :, :], hs[:, :, :], BC[:, n % 2, 1:2, :].to_broadcast([P, 2, L]), ALU.mult).then_inc(hC_ok.sem, hC_ok.up())
                    dve.wait_ge(hC_ok.sem, hC_ok.now(b))
                    yield
                dve.wait_ge(ysum.sem, ysum.at(b, 2 * DS))
                for j in range(2):
                    m = STT(out=CV[:, j, :], in0=U[:, j, :], scalar=w("Dp")[:, j:j + 1], in1=bank[5 + j][:, :],
                            op0=ALU.mult, op1=ALU.add)
                m.then_inc(vec2.sem, vec2.up())
                dve.wait_ge(vec2.sem, vec2.now(b))
                TT(YG[:, :, :], CV[:, :, :], SZ[:, :, :], ALU.mult).then_inc(yg_ok.sem, yg_ok.up())
                dve.wait_ge(yg_ok.sem, yg_ok.now(b))
                yield
                dve.wait_ge(op_ps.sem, op_ps.at(b, 1))
                TT(Y2[:, :, :], bank[7][:, :].rearrange("p (n d) -> p n d", n=NT), XR[:, :, :], ALU.add).then_inc(vec2.sem, vec2.up())
                dve.wait_ge(vec2.sem, vec2.now(b))
                norm_sums(b, Y2)
                yield
                norm_rows(b, Y2, 3, XR, ln_ok)
                yield

                dve.wait_ge(rl_ps.sem, rl_ps.at(b, 2))
                lg = bank[7][:, 0:NT * NE2].rearrange("p (n e) -> p n e", n=NT)
                dve.tensor_reduce(ps1[:, 0, :], lg, AX.X, ALU.max).then_inc(vec2.sem, vec2.up())
                dve.wait_ge(vec2.sem, vec2.now(b))
                TT(pr[:, 0, :, :], lg, ps1[:, 0, :].unsqueeze(2).to_broadcast([P, NT, NE2]), ALU.subtract).then_inc(pm_ok.sem, pm_ok.up())
                dve.wait_ge(pm_ok.sem, pm_ok.now(b))
                yield
                dve.wait_ge(pe_ok.sem, pe_ok.at(b, 1))
                dve.tensor_reduce(ps1[:, 1, :], pr[:, 1, :, :], AX.X, ALU.add).then_inc(vec2.sem, vec2.up())
                dve.wait_ge(vec2.sem, vec2.now(b))
                dve.reciprocal(ps1[:, 2, :], ps1[:, 1, :]).then_inc(vec2.sem, vec2.up())
                dve.wait_ge(vec2.sem, vec2.now(b))
                TT(pr[:, 2, :, :], pr[:, 1, :, :], ps1[:, 2, :].unsqueeze(2).to_broadcast([P, NT, NE2]), ALU.mult).then_inc(vec2.sem, vec2.up())
                dve.wait_ge(vec2.sem, vec2.now(b))
                dve.sem_inc(hold_dve, 1)
                for i in range(NT):
                    m = dve.max(r8[:, i, :], pr[:, 2, i, :])
                m.then_inc(vec2.sem, vec2.up())
                dve.wait_ge(vec2.sem, vec2.now(b))
                dve.sem_inc(hold_dve, 1)
                for i in range(NT):
                    m = dve.max_index(ri[:, i, :], r8[:, i, :], pr[:, 2, i, :])
                m.then_inc(vec2.sem, vec2.up())
                dve.wait_ge(vec2.sem, vec2.now(b))
                CP(rif[:, :, :], ri[:, :, :]).then_inc(vec2.sem, vec2.up())
                dve.wait_ge(vec2.sem, vec2.now(b))
                TT(mk[:, :, :], co("iota")[:, 0:NE2].unsqueeze(1).to_broadcast([P, NT, NE2]),
                        rif[:, :, 0:1].to_broadcast([P, NT, NE2]), ALU.is_equal).then_inc(vec2.sem, vec2.up())
                dve.wait_ge(vec2.sem, vec2.now(b))
                CP(mk_bf[:, :, :], mk[:, :, :]).then_inc(mk_ok.sem, mk_ok.up())
                dve.wait_ge(mk_ok.sem, mk_ok.now(b))
                yield
                TT(pr[:, 3, :, :], pr[:, 2, :, :], mk[:, :, :], ALU.mult).then_inc(vec2.sem, vec2.up())
                dve.wait_ge(vec2.sem, vec2.now(b))
                dve.wait_ge(loc_ps.sem, loc_ps.at(b, 1))
                TS(keep[:, :, :], bank[7][:, 64:64 + NT * NE2].rearrange("p (n e) -> p n e", n=NT), float(CAP), None,
                        ALU.is_lt).then_inc(vec2.sem, vec2.up())
                dve.wait_ge(vec2.sem, vec2.now(b))
                TT(gate[:, :, :], pr[:, 3, :, :], keep[:, :, :], ALU.mult).then_inc(gate_ok.sem, gate_ok.up())
                dve.wait_ge(gate_ok.sem, gate_ok.now(b))
                dve.tensor_reduce(csum[:, :], mk[:, :, :].rearrange("p n e -> p e n"), AX.X, ALU.add).then_inc(vec2.sem, vec2.up())
                dve.wait_ge(vec2.sem, vec2.now(b))
                TT(cum[:, :], cum[:, :], csum[:, :], ALU.add).then_inc(vec2.sem, vec2.up())
                dve.wait_ge(vec2.sem, vec2.now(b))
                CP(cum_bf[:, :], cum[:, :]).then_inc(vec2.sem, vec2.up())
                dve.wait_ge(vec2.sem, vec2.now(b))
                yield
                dve.wait_ge(bias_ps.sem, bias_ps.at(b, 1))
                TT(Y2[:, :, :], bank[7][:, :].rearrange("p (n d) -> p n d", n=NT), XR[:, :, :], ALU.add).then_inc(vec2.sem, vec2.up())
                dve.wait_ge(vec2.sem, vec2.now(b))
                for i in range(NT):
                    for k in range(2):
                        dve.wait_ge(e_ps.sem, e_ps.at(b, 2 * i + k + 1))
                        m = TT(gated[:, 4 * k:4 * k + 4, :], bank[5 + k][:, :].rearrange("p (e d) -> p e d", e=4),
                               gate[:, i, 4 * k:4 * k + 4].unsqueeze(2).to_broadcast([P, 4, P]), ALU.mult)
                        m.then_inc(e_used.sem, e_used.up())
                    dve.wait_ge(e_used.sem, e_used.at(b, 2 * i + 2))
                    dve.tensor_reduce(gsum[:, :], gated[:, :, :].rearrange("p e d -> p d e"), AX.X, ALU.add).then_inc(vec2.sem, vec2.up())
                    dve.wait_ge(vec2.sem, vec2.now(b))
                    TT(Y2[:, i, :], Y2[:, i, :], gsum[:, :], ALU.add).then_inc(vec2.sem, vec2.up())
                    dve.wait_ge(vec2.sem, vec2.now(b))
                    yield
                norm_sums(b, Y2)
                yield
                norm_rows(b, Y2, 4, OUT, rest_done)
                yield

            for t in (QBD[:, :, :, :, :], PBD[:, :, :, :, :], XP[:, :, :]):
                dve.memset(t, 0.0)
            dve.memset(cum[:, :], 0.0)
            dve.memset(one[:, :], 1.0)
            dve.memset(two[:, :], 2.0)
            dve.memset(eps[:, :], EPS)
            dve.memset(ones_bf[:, :], 1.0)
            dve.memset(cum_bf[:, :], 0.0)
            dve.wait_ge(s_load, 64)
            CP(ident_bf[:, :], ident)
            CP(ident_h[:, :], ident)
            CP(tri_bf[:, :], once("tri"))
            CP(lmask_bf[:, :, :], once("lmask"))
            TS(dtb2[:, :], w("dtb"), 2.0, None, ALU.mult)
            CP(WQ[:, 0, :], wh("qr"))
            dve.wait_ge(s_seta, 2)
            TS(Aneg[:, :, :], Aneg[:, :, :], -1.0, None, ALU.mult).then_inc(set_v.sem, set_v.up())
            dve.wait_ge(set_v.sem, set_v.k)
            TS(dl[:, 1, :], dl[:, 0, :], 1.0, None, ALU.add).then_inc(set_v.sem, set_v.up())
            dve.wait_ge(set_v.sem, set_v.k)
            dve.reciprocal(dl[:, 2, :], dl[:, 1, :]).then_inc(set_v.sem, set_v.up())
            dve.wait_ge(set_v.sem, set_v.k)
            TS(dl[:, 3, :], dl[:, 2, :], -2.0 * np.pi, np.pi, ALU.mult, ALU.add).then_inc(set_v.sem, set_v.up())
            dve.wait_ge(set_v.sem, set_v.k)
            TS(dl[:, 3, :], dl[:, 3, :], 3.1415925, -3.1415925, ALU.min, ALU.max).then_inc(set_v.sem, set_v.up())
            dve.wait_ge(set_v.sem, set_v.k)
            assert set_v.k == SET_SIN
            dve.wait_ge(s_setp, 2)
            CP(WQ[:, 1, :], bank[0][0:64, 0:256])
            CP(WVO[:, :, :].rearrange("p a c -> p (a c)"), bank[1][:, 0:256])
            dve.wait_ge(s_seta, 3)
            TT(dl[:, 6, :], dl[:, 5, :], dl[:, 5, :], ALU.mult).then_inc(set_v.sem, set_v.up())
            dve.wait_ge(set_v.sem, set_v.k)
            TS(dl[:, 6, :], dl[:, 6, :], 2.0, -1.0, ALU.mult, ALU.add)
            TS(dl[:, 7, :], dl[:, 4, :], -1.0, None, ALU.mult).then_inc(set_v.sem, set_v.up())
            dve.wait_ge(set_v.sem, set_v.k)
            cd = dl[:, 6, :].unsqueeze(1).to_broadcast([P, 9, HALF])
            sd = dl[:, 7, :].unsqueeze(1).to_broadcast([P, 9, HALF])
            trig_t = Y1[:, :, :].rearrange("p n d -> p (n d)")[:, 0:18 * HALF].rearrange("p (s a c) -> p s a c", s=2, a=9)
            TT(trig[:, 0, :, :], once("cosb"), cd, ALU.mult)
            TT(trig_t[:, 0, :, :], once("sinb"), sd, ALU.mult)
            TT(trig[:, 1, :, :], once("sinb"), cd, ALU.mult)
            TT(trig_t[:, 1, :, :], once("cosb"), sd, ALU.mult).then_inc(set_v.sem, set_v.up())
            dve.wait_ge(set_v.sem, set_v.k)
            TT(trig[:, 0, :, :], trig[:, 0, :, :], trig_t[:, 0, :, :], ALU.subtract)
            TT(trig[:, 1, :, :], trig[:, 1, :, :], trig_t[:, 1, :, :], ALU.add).then_inc(set_v.sem, set_v.up())
            dve.wait_ge(set_v.sem, set_v.k)
            assert set_v.k == SET_VEC
            dve.sem_inc(attn_done.sem, 1)
            dve.sem_inc(rest_done.sem, 1)
            rows_loop(keys, tiles, merges, close, rest, dve.Fori)

        for name, s in signals.items():
            assert s.k == s.per, f"{name} rises {s.k} times in a batch row, not {s.per}"


PER = {"vec": 129, "vec2": 54, "vec_k": 6, "act": 8, "act2": 33, "act_k": 2}
SET_SIN = 5
SET_VEC = 9
KEY_PHASES, TILE_PHASES, MERGE_PHASES = 3, 14, 2
ROUTE_PHASES, EXPERT_PHASES, NORM_PHASES, SCAN_IN_PHASES, SCAN_OUT_PHASES, TOP1_PHASES = 2, 19, 1, 9, 1, 10


def pack(pieces, rows):
    where, cols, off = {}, [], 0
    for name, a in pieces.items():
        a = np.asarray(a)
        where[name] = (off, a.shape[0], a.shape[1:])
        flat = a.reshape(a.shape[0], -1)
        if a.shape[0] < rows:
            flat = np.concatenate([flat, np.zeros((rows - a.shape[0], flat.shape[1]), flat.dtype)], 0)
        cols.append(flat)
        off += flat.shape[1]
    return np.ascontiguousarray(np.concatenate(cols, 1)), where


def constants():
    p = np.arange(P)[:, None]
    c = np.arange(P)[None, :]
    theta = (1.0 / np.float32(10000.0) ** (2.0 * np.arange(HALF, dtype=np.float32) / DR)).astype(np.float32)
    pos = np.zeros((P, 9), np.float32)
    for i in range(NT):
        pos[:, i] = P * i + np.arange(P)
        pos[:, 4 + i] = 2 * (P * i + np.arange(P)) - (LW - 1)
    pos[:, 8] = LW + np.arange(P) % 32
    ang = (pos[:, :, None] * theta[None, None, :]).astype(np.float32).astype(np.float64)
    lm = np.full((P, 2, 224), NEG, np.float32)
    a96, s128 = np.arange(96)[None, :], np.arange(P)[None, :]
    lm[:, 0, 0:96][(p < 64) | ((p <= TOPK - 2) & (a96 > p))] = 0
    lm[:, 0, 96:224][(p >= 64) & (s128 <= p) & (s128 >= p - (LW - 1))] = 0
    w192 = np.arange(192)[None, :] - 64
    lm[:, 1, 32:224][(w192 <= p) & (w192 >= p - (LW - 1))] = 0
    a, bb, xx, j = (np.arange(P) // 32)[:, None, None], (np.arange(P) // 8 % 4)[:, None, None], \
        np.arange(8)[None, :, None], np.arange(32)[None, None, :]
    t = 32 * bb + 4 * xx + a
    f = np.float32
    return {
        "ident": np.eye(P, dtype=f), "tri": (p < c).astype(f), "lmask": lm,
        "top0": np.where(c[:, 0:64] <= p - 64, 0, NEG_TOP).astype(f), "top1": np.where(c <= p, 0, NEG_TOP).astype(f),
        "rmask": np.where(j <= t - LW, 0, NEG).astype(f),
        "cosb": np.cos(ang).astype(f), "sinb": np.sin(ang).astype(f),
        "pos": (p + P * np.arange(NT)[None, :]).astype(f), "iota": np.broadcast_to(np.arange(NE), (P, NE)).astype(f),
    }


def kernel(**inputs):
    import concourse.bacc as _bacc
    from concourse.bass_utils import run_bass_kernel_spmd as _run

    a = {k: np.asarray(v) for k, v in inputs.items()}
    g = lambda n: a["L0_attn_" + n]
    f = lambda n: a["L0_ffn_" + n]
    m = lambda n: a["L1_attn_" + n]
    rows = lambda v: np.broadcast_to(v[None, :], (P, v.shape[0]))
    w13 = f("w13").transpose(2, 0, 1)
    w128, at128 = pack({
        "wk2": np.concatenate([g("idx_wk"), g("idx_wk")], 1), "wq": g("idx_wq"), "dq": g("W_dq"),
        "kv": np.concatenate([g("W_dkv"), g("W_kr")], 1), "idxw": rows(g("idx_w")), "rawd": rows(g("raw_delta")),
        "alog": m("A_log").reshape(2, P, DS).transpose(1, 0, 2), "dtb": m("dt_proj_b").reshape(2, P).T,
        "gate": f("gate_w").T, "gb": rows(f("gate_b")),
        "w1g": w13[:, :, 0:64].reshape(D, NE // 2, P), "w1u": w13[:, :, 64:].reshape(D, NE // 2, P),
        "w1sg": f("w13_s").T[:, 0:64], "w1su": f("w13_s").T[:, 64:],
        "w2": f("w2").transpose(0, 2, 1).reshape(NE // 2, P, D).transpose(1, 0, 2), "w2s": f("w2_s").T,
        "inp": m("in_proj_w").T, "cw": m("conv_w")[:, 0, :].reshape(2, P, DCONV).transpose(1, 0, 2),
        "cb": m("conv_b").reshape(2, P).T, "xp": m("x_proj_w").T.reshape(2, P, 40).transpose(1, 0, 2),
        "dtw": m("dt_proj_w").T, "Dp": m("D").reshape(2, P).T,
        "op": m("out_proj_w").T.reshape(2, P, D).transpose(1, 0, 2),
        "wg": a["L1_ffn_wg"], "ew": a["L1_ffn_W"].transpose(2, 0, 1).reshape(D, NE2 * D), "eb": a["L1_ffn_b"],
    }, P)
    w64, at64 = pack({
        "qr": g("W_qr"), "uqT": g("W_uq").reshape(DQ, NH, DH).transpose(2, 1, 0),
        "ukT": g("W_uk").reshape(DC, NH, DH).transpose(2, 1, 0), "uvT": g("W_uv").reshape(DC, NH, DH).transpose(2, 1, 0),
        "out": g("W_out").reshape(NH, DH, D).transpose(1, 0, 2),
    }, 64)
    every = constants()
    first = ("tri", "lmask", "cosb", "sinb")
    consts, atc = pack({k: v for k, v in every.items() if k not in first}, P)
    setup_c, ats = pack({k: every[k] for k in first}, P)
    arrays = {"x": np.ascontiguousarray(g("x")), "w128": w128, "w64": w64, "consts": consts, "setup_c": setup_c}
    nc = _bacc.Bacc("TRN2", target_bir_lowering=False, num_devices=1)
    aps = [nc.dram_tensor(k, v.shape, mybir.dt.from_np(v.dtype), kind="ExternalInput").ap() for k, v in arrays.items()]
    o = nc.dram_tensor("out", (B, L, D), F32, kind="ExternalOutput").ap()
    nc.disable_value_cache = True
    build(nc, *aps, o, at128, at64, atc, ats)
    r = _run(nc, [arrays], core_ids=[0])
    return r.results[0]["out"]
```
